# Optimizing a Trainium2 kernel written in Bass

```python
import numpy as np
import jax
import jax.numpy as jnp

def _softmax(x, axis=-1):
    return jax.nn.softmax(x, axis=axis)

def _gelu(x):
    return jax.nn.gelu(x, approximate=True)

def _silu(x):
    return jax.nn.silu(x)

def _sigmoid(x):
    return jax.nn.sigmoid(x)

def _layernorm(x, axis=-1, eps=1e-05):
    m = jnp.mean(x, axis=axis, keepdims=True)
    v = jnp.var(x, axis=axis, keepdims=True)
    return (x - m) / jnp.sqrt(v + eps)

def _scatter_add(tgt, idx, src, axis=0):
    return tgt.at[idx].add(src)

def _segment_sum(src, seg, n):
    return jax.ops.segment_sum(src, seg, n)
kernel_name = 'mk_gnn_resnorm_d2_gnn_r32_ddeaed'

def setup_inputs(seed: int=0):
    np.random.seed(seed)
    _w = jnp.asarray

    def _rec_inputs():
        import jax
        import jax.numpy as jnp
        _gk = jax.random.key(seed)
        x = -0.000202 + 1 * jax.random.normal(jax.random.fold_in(_gk, 1), (50000, 128), jnp.float32)
        src = jax.random.randint(jax.random.fold_in(_gk, 2), (25000,), 0, 50000, jnp.int32)
        dst = jnp.minimum((50000 * jax.random.uniform(jax.random.fold_in(_gk, 3), (25000,)) ** 2.0).astype(jnp.int32), 49999)
        _o = jnp.argsort(dst, stable=True)
        src = src[_o]
        dst = dst[_o]
        edge_type_32 = jax.random.randint(jax.random.fold_in(_gk, 13), (25000,), 0, 32, jnp.int32)
        edge_weight = 0.00107675 + 0.999702 * jax.random.normal(jax.random.fold_in(_gk, 14), (25000,), jnp.float32)
        return (x, src, dst, edge_type_32, edge_weight)
    x, src, dst, edge_type_32, edge_weight = _rec_inputs()

    def _L0_gnn_setup():
        import jax, jax.numpy as jnp
        import numpy as np
        import math
        N_NODES, N_EDGES, DIM, N_HEADS = (50000, 25000, 128, 8)
        D_K = DIM // N_HEADS
        key = jax.random.key(seed)
        ks = jax.random.split(key, 12)
        f32 = jnp.float32
        s = 1.0 / math.sqrt(DIM)
        return {'x': jax.random.normal(ks[0], (N_NODES, DIM), f32), 'src': jax.random.randint(ks[1], (N_EDGES,), 0, N_NODES), 'dst': jax.random.randint(ks[2], (N_EDGES,), 0, N_NODES), 'edge_weight': jax.random.normal(ks[3], (N_EDGES,), f32), 'Wk': jax.random.normal(ks[4], (DIM, DIM), f32) * s, 'bk': jax.random.normal(ks[5], (DIM,), f32) * 0.01, 'Wq': jax.random.normal(ks[6], (DIM, DIM), f32) * s, 'bq': jax.random.normal(ks[7], (DIM,), f32) * 0.01, 'Wv': jax.random.normal(ks[8], (DIM, DIM), f32) * s, 'bv': jax.random.normal(ks[9], (DIM,), f32) * 0.01, 'rel_att': jax.random.normal(ks[10], (N_HEADS, D_K), f32) * 0.1, 'rel_msg': jax.random.normal(ks[11], (N_HEADS, D_K, D_K), f32) / math.sqrt(D_K)}
    _L0_gnn_all = _L0_gnn_setup()
    _L0_gnn_in = {k: v for k, v in _L0_gnn_all.items() if k in ('Wk', 'bk', 'Wq', 'bq', 'Wv', 'bv', 'rel_att', 'rel_msg')}
    del _L0_gnn_all

    def _L1_gnn_setup():
        import jax, jax.numpy as jnp
        import numpy as np
        N, E = (1250, 20000)
        D_IN, D_OUT, R, B = (128, 128, 32, 8)
        EPS = 1e-05
        SLOPE = 0.01
        key = jax.random.key(seed)
        ks = jax.random.split(key, 12)
        x = jax.random.normal(ks[0], (N, D_IN), jnp.float32)
        norm = jax.random.uniform(ks[1], (N, 1), jnp.float32)
        edge_src = jax.random.randint(ks[2], (E,), 0, N)
        edge_dst = jax.random.randint(ks[3], (E,), 0, N)
        edge_rel = jax.random.randint(ks[4], (E,), 0, R)
        s_loop = (6.0 / (D_IN + D_OUT)) ** 0.5 * 2.0 ** 0.5
        w_loop = jax.random.uniform(ks[5], (D_IN, D_OUT), jnp.float32, -s_loop, s_loop)
        w_bases = jax.random.uniform(ks[6], (B, D_IN, D_OUT), jnp.float32, -s_loop, s_loop)
        s_rel = (6.0 / (R + B)) ** 0.5 * 2.0 ** 0.5
        w_rel_coef = jax.random.uniform(ks[7], (R, B), jnp.float32, -s_rel, s_rel)
        s_att = (6.0 / (D_OUT + 1)) ** 0.5 * 2.0 ** 0.5
        att_l_w = jax.random.uniform(ks[8], (1, D_OUT), jnp.float32, -s_att, s_att)
        w_bias = jnp.zeros((D_OUT,), jnp.float32)
        bn_gamma = jnp.ones((D_OUT,), jnp.float32)
        bn_beta = jnp.zeros((D_OUT,), jnp.float32)
        return {'x': x, 'norm': norm, 'edge_src': edge_src, 'edge_dst': edge_dst, 'edge_rel': edge_rel, 'w_loop': w_loop, 'w_bases': w_bases, 'w_rel_coef': w_rel_coef, 'att_l_w': att_l_w, 'w_bias': w_bias, 'bn_gamma': bn_gamma, 'bn_beta': bn_beta}
    _L1_gnn_all = _L1_gnn_setup()
    _L1_gnn_in = {k: v for k, v in _L1_gnn_all.items() if k in ('w_loop', 'w_bases', 'w_rel_coef', 'att_l_w', 'w_bias', 'bn_gamma', 'bn_beta')}
    del _L1_gnn_all
    return {'x': x, 'src': src, 'dst': dst, 'edge_type_32': edge_type_32, 'edge_weight': edge_weight, 'L0_gnn_Wk': _L0_gnn_in['Wk'], 'L0_gnn_bk': _L0_gnn_in['bk'], 'L0_gnn_Wq': _L0_gnn_in['Wq'], 'L0_gnn_bq': _L0_gnn_in['bq'], 'L0_gnn_Wv': _L0_gnn_in['Wv'], 'L0_gnn_bv': _L0_gnn_in['bv'], 'L0_gnn_rel_att': _L0_gnn_in['rel_att'], 'L0_gnn_rel_msg': _L0_gnn_in['rel_msg'], 'L1_gnn_w_loop': _L1_gnn_in['w_loop'], 'L1_gnn_w_bases': _L1_gnn_in['w_bases'], 'L1_gnn_w_rel_coef': _L1_gnn_in['w_rel_coef'], 'L1_gnn_att_l_w': _L1_gnn_in['att_l_w'], 'L1_gnn_w_bias': _L1_gnn_in['w_bias'], 'L1_gnn_bn_gamma': _L1_gnn_in['bn_gamma'], 'L1_gnn_bn_beta': _L1_gnn_in['bn_beta']}

def reference(x, src, dst, edge_type_32, edge_weight, L0_gnn_Wk, L0_gnn_bk, L0_gnn_Wq, L0_gnn_bq, L0_gnn_Wv, L0_gnn_bv, L0_gnn_rel_att, L0_gnn_rel_msg, L1_gnn_w_loop, L1_gnn_w_bases, L1_gnn_w_rel_coef, L1_gnn_att_l_w, L1_gnn_w_bias, L1_gnn_bn_gamma, L1_gnn_bn_beta):
    import jax
    import jax.numpy as jnp

    def _L0_gnn_ref(x, src, dst, edge_weight, Wk, bk, Wq, bq, Wv, bv, rel_att, rel_msg):
        import jax, jax.numpy as jnp
        import numpy as np
        import math
        N_NODES, N_EDGES, DIM, N_HEADS = (50000, 25000, 128, 8)
        D_K = DIM // N_HEADS
        N, D = x.shape
        H, dk = rel_att.shape
        inv_sqrt_dk = jnp.asarray(1.0 / math.sqrt(dk), x.dtype)
        k = (x @ Wk.T + bk).reshape(N, H, dk)
        q = (x @ Wq.T + bq).reshape(N, H, dk)
        v = (x @ Wv.T + bv).reshape(N, H, dk)
        qp = edge_weight[:, None, None] * rel_att[None]
        att = ((q[dst] + qp) * k[src]).sum(-1) * inv_sqrt_dk
        val = jnp.einsum('ehd,hdk->ehk', v[src], rel_msg)
        m = jax.ops.segment_max(att, dst, num_segments=N)
        e = jnp.exp(att - m[dst])
        s = jax.ops.segment_sum(e, dst, num_segments=N)
        w = e / s[dst]
        h = jax.ops.segment_sum(w[..., None] * val, dst, num_segments=N)
        return jax.nn.relu(h.reshape(N, D))

    def _L1_gnn_ref(x, norm, edge_src, edge_dst, edge_rel, w_loop, w_bases, w_rel_coef, att_l_w, w_bias, bn_gamma, bn_beta):
        import jax, jax.numpy as jnp
        import numpy as np
        N, E = (1250, 20000)
        D_IN, D_OUT, R, B = (128, 128, 32, 8)
        EPS = 1e-05
        SLOPE = 0.01
        n = x.shape[0]
        W = jnp.einsum('rb,bio->rio', w_rel_coef, w_bases)
        xr = jnp.einsum('ni,rio->nro', x, W)
        src_r = xr[edge_src, edge_rel]
        dst_r = xr[edge_dst, edge_rel]
        score = (src_r + dst_r) @ att_l_w[0]
        score = jnp.where(score >= 0, score, SLOPE * score)
        m = jax.ops.segment_max(score, edge_dst, num_segments=n)
        m = jnp.where(jnp.isfinite(m), m, 0.0)
        ex = jnp.exp(score - m[edge_dst])
        denom = jax.ops.segment_sum(ex, edge_dst, num_segments=n)
        denom = jnp.where(denom > 0, denom, 1.0)
        e = ex / denom[edge_dst]
        accum = jax.ops.segment_sum(e[:, None] * src_r, edge_dst, num_segments=n)
        ft = accum * norm
        ft = ft + w_bias + x @ w_loop
        mu = jnp.mean(ft, axis=0)
        var = jnp.mean((ft - mu) ** 2, axis=0)
        ft = bn_gamma * (ft - mu) / jnp.sqrt(var + EPS) + bn_beta
        return jax.nn.relu(ft)
    deg = jnp.maximum(jax.ops.segment_sum(jnp.ones(dst.shape, jnp.float32), dst, num_segments=50000), 1.0)
    deg_isqrt = deg ** (-0.5)
    x = _layernorm(x + _L0_gnn_ref(x, src, dst, edge_weight, L0_gnn_Wk, L0_gnn_bk, L0_gnn_Wq, L0_gnn_bq, L0_gnn_Wv, L0_gnn_bv, L0_gnn_rel_att, L0_gnn_rel_msg), axis=-1)
    x = _layernorm(x + _L1_gnn_ref(x, deg_isqrt[:, None], src, dst, edge_type_32, L1_gnn_w_loop, L1_gnn_w_bases, L1_gnn_w_rel_coef, L1_gnn_att_l_w, L1_gnn_w_bias, L1_gnn_bn_gamma, L1_gnn_bn_beta), axis=-1)
    return x

_drawn_inputs = setup_inputs


def setup_inputs(seed=0):
    import zlib

    import numpy as np

    out = dict(_drawn_inputs(seed))
    spreads = {'L1_gnn_w_bias': (0.0, 2.0), 'L1_gnn_bn_gamma': (1.0, 0.2), 'L1_gnn_bn_beta': (0.0, 0.1)}
    factors = {'edge_weight': 6.837,
     'L0_gnn_bk': 33.251,
     'L0_gnn_bq': 64.0,
     'L0_gnn_bv': 8.0,
     'L0_gnn_rel_att': 6.675}
    for name, (base, spread) in spreads.items():
        noise = np.random.default_rng([zlib.crc32(name.encode()), seed]).standard_normal(out[name].shape)
        drawn = base * np.exp(spread * noise) if base else spread * noise
        out[name] = jnp.asarray(drawn.astype(out[name].dtype))
    for name, factor in factors.items():
        out[name] = (out[name] * factor).astype(out[name].dtype)
    return out
```

```python
from contextlib import ExitStack, contextmanager

import concourse.bass as bass
from concourse import mybir

ALU = mybir.AluOpType
ACT = mybir.ActivationFunctionType
AX = mybir.AxisListType
F32 = mybir.dt.float32
I32 = mybir.dt.int32

NODES = 50000
EDGES = 25000
D = 128
HEADS = 8
DK = D // HEADS
RELS = 32
BASES = 8
P = 128
T = -(-EDGES // P)
G = 4
NG = T // G
PAIRS = NG // 2
CH = 8
CHUNK = P * CH
NCH = -(-NODES // CHUNK)
LASTP = (NODES - (NCH - 1) * CHUNK) // CH
FIX = T + 1
FAR = 3.0e38
EPS = 1e-5
SLOPE = 0.01
assert NG * G == T and NG == 2 * PAIRS + 1 and NCH == NG and (NCH - 1) * CHUNK + LASTP * CH == NODES
ds = bass.ds


def in_pairs(eng, body):
    body(0, 0)
    body(0, 1)
    with eng.Fori(1, PAIRS) as i:
        body(i, 0)
        body(i, 1)
    body(PAIRS, 0)


def in_pairs_ahead(eng, first, body):
    first(0, 0)
    body(0, 0, (0, 1))
    body(0, 1, (1, 0))
    with eng.Fori(1, PAIRS) as i:
        body(i, 0, (i, 1))
        body(i, 1, (i + 1, 0))
    body(PAIRS, 0, None)


class Chain:

    def __init__(self, eng, sem):
        self.eng, self.sem, self.n = eng, sem, 0

    def __call__(self, ins):
        self.n += 1
        ins.then_inc(self.sem, 1)
        self.eng.wait_ge(self.sem, self.n)


class LoopChain:

    def __init__(self, eng, sem, per, turn):
        self.eng, self.sem, self.per, self.turn, self.n = eng, sem, per, turn, 0

    def __call__(self, ins, wait=True):
        self.n += 1
        ins.then_inc(self.sem, 1)
        if wait:
            self.wait(self.n)

    def wait(self, n):
        self.eng.wait_ge(self.sem, self.turn * self.per + n)

    def end(self):
        assert self.n == self.per, (self.n, self.per)


def program(nc, x, src, dst, near, rel, ew, wk, wk_t, bk, wq_t, bq, wv, bv, rel_att, rel_msg, w_loop, w_bases,
            w_coef, w_coef_t, att_l, w_bias, gamma, beta, out):
    x1_table = nc.dram_tensor("x1_table", [NODES, D], F32).ap()
    xd_kept = [nc.dram_tensor(f"xd_kept{n}", [P, T, D], F32).ap() for n in range(2)]
    ctx = ExitStack()

    def sb(name, shape, dt=F32, c=ctx):
        return c.enter_context(nc.sbuf_tensor(name, shape, dt))

    with ctx:
        rows = sb("rows", [P, T + 2, D])
        ident = sb("ident", [P, P])
        ones_row = sb("ones_row", [1, P])
        ones_col = sb("ones_col", [P, 1])
        carried_by = sb("carried_by", [P, P])
        dst_x = sb("dst_x", [P, T + 2])
        cont = sb("cont", [P, T])
        more = sb("more", [P, T])
        pen_cont = sb("pen_cont", [P, T])
        pen_more = sb("pen_more", [P, T])
        stops = sb("stops", [P, T])
        in_first = sb("in_first", [P, T])
        in_last = sb("in_last", [P, T])
        inside = sb("inside", [P, T])
        pen_first = sb("pen_first", [P, T])
        pen_last = sb("pen_last", [P, T])
        head_end = sb("head_end", [P, T])
        valid = sb("valid", [P, T + 1])
        apart = sb("apart", [P, 1])
        same = [sb(f"same{q}", [P, 2 * P]) for q in range(2)]
        pen_same = [sb(f"pen_same{q}", [P, 2 * P]) for q in range(2)]
        gather_idx = sb("gather_idx", [P, NG, 2 * G], I32)
        scatter_idx = sb("scatter_idx", [P, T + G], I32)
        ew_sb = sb("ew_sb", [P, T])
        rel_f = sb("rel_f", [P, T])
        iota_rel = sb("iota_rel", [P, RELS])
        coef = sb("coef", [P, T, BASES])
        att = sb("att", [P, HEADS, T])
        weight = sb("weight", [P, HEADS + 1, T])
        norm = sb("norm", [P, T])
        head_sum = sb("head_sum", [P, D])
        eps_col = sb("eps_col", [P, 1])
        scrap = sb("scrap", [P, 2])
        wq_sb = sb("wq_sb", [D, D])
        wkv_sb = sb("wkv_sb", [D, 2 * D + HEADS])
        bq_row = sb("bq_row", [1, D])
        bkv_row = sb("bkv_row", [1, 2 * D + HEADS])
        wloop_sb = sb("wloop_sb", [D, D])
        bases_sb = sb("bases_sb", [D, BASES * D])
        a_sb = sb("a_sb", [D, RELS])
        coef_blocks = sb("coef_blocks", [P, G * BASES])
        vec_rows = sb("vec_rows", [1, 3, D])
        centre_row = sb("centre_row", [1, D])
        var_row = sb("var_row", [1, D])
        gram_sb = sb("gram_sb", [P, D + 1])
        sums_row = sb("sums_row", [1, 2 * D])

        setup(nc, locals())
        m = locals()
        project(nc, m)
        segment_softmax(nc, m, 0)
        sum_layer0(nc, m)
        messages(nc, m)
        segment_softmax(nc, m, 1)
        centre(nc, m)
        sum_layer1(nc, m)
        output(nc, m)


@contextmanager
def phase_sems(nc):
    made = []

    def sem(name):
        made.append(nc.alloc_semaphore(name))
        return made[-1]
    yield sem
    nc.clear_and_free_semaphores(made)
    nc.all_engine_barrier()


def carry_wait(nc, m, n=0):
    nc.gpsimd.tensor_tensor(m["scrap"][:, n:n + 1], m["eps_col"][:, :], m["eps_col"][:, :], ALU.add)


def row_stats(nc, link, st, part, np, x, n):
    for j in range(n):
        last = nc.vector.bn_stats(st[0:np, j, :], x[0:np, j, :])
    link(last)
    s, p = st[0:np, 0:n, :], part[0:np]
    tt = nc.vector.tensor_tensor
    tt(p[:, 2, 0:n], s[:, :, 1], s[:, :, 4], ALU.add)
    tt(p[:, 1, 0:n], s[:, :, 2], s[:, :, 5], ALU.add)
    link(tt(p[:, 0, 0:n], s[:, :, 1], s[:, :, 4], ALU.subtract))
    link(tt(p[:, 0, 0:n], p[:, 0, 0:n], p[:, 0, 0:n], ALU.mult))
    return nc.vector.scalar_tensor_tensor(p[:, 1, 0:n], p[:, 0, 0:n], D / 4.0, p[:, 1, 0:n], ALU.mult, ALU.add)


def setup(nc, m):
    (dst_x, cont, more, pen_cont, pen_more, stops, in_first, in_last, inside, pen_first, pen_last, head_end, valid,
     apart, same, pen_same, ident) = (m[n] for n in (
        "dst_x", "cont", "more", "pen_cont", "pen_more", "stops", "in_first", "in_last", "inside", "pen_first",
        "pen_last", "head_end", "valid", "apart", "same", "pen_same", "ident"))
    gather_idx, scatter_idx, carried_by, rows = m["gather_idx"], m["scatter_idx"], m["carried_by"], m["rows"]
    ends_dram = nc.dram_tensor("ends_dram", [P, 2], F32).ap()
    with ExitStack() as c:
        new_sem = c.enter_context(phase_sems(nc))

        def sb(name, shape, dt=F32):
            return c.enter_context(nc.sbuf_tensor(name, shape, dt))

        def sem(name):
            return new_sem(name)

        edge_i = sb("edge_i", [P, 3, T], I32)
        near_i = sb("near_i", [P, 2], I32)
        iota_i = sb("iota_i", [P, RELS], I32)
        equal = sb("equal", [P, T + 1])
        t0 = sb("t0", [P, T + 1])
        t1 = sb("t1", [P, T + 1])
        ends = sb("ends", [P, 2])
        ends_all = sb("ends_all", [P, P, 2])
        wk_nat = sb("wk_nat", [D, D])
        wv_nat = sb("wv_nat", [D, D])
        msg_blocks = sb("msg_blocks", [D, D])
        att_blocks = sb("att_blocks", [D, HEADS])
        bk_col = sb("bk_col", [D, 1])
        bv_col = sb("bv_col", [D, 1])
        att_row = sb("att_row", [1, D])
        coef_t = sb("coef_t", [BASES, RELS])
        base_att = sb("base_att", [D, BASES])
        base_tmp = sb("base_tmp", [D, BASES * D])
        base_att_t = sb("base_att_t", [BASES, D])
        ps = c.enter_context(nc.psum_tensor("ps_setup", [P, 4, 512], F32))
        s_zero, s_blocks, s_edges, s_weights = sem("s_zero"), sem("s_blocks"), sem("s_edges"), sem("s_weights")
        s_pool, s_pool_done, s_dve, s_mm, s_base, s_bt = (sem(n) for n in (
            "s_pool", "s_pool_done", "s_dve", "s_mm", "s_base", "s_bt"))
        s_ends, s_ends_out, s_ends_in, s_fold, s_base_t = (sem(n) for n in (
            "s_ends", "s_ends_out", "s_ends_in", "s_fold", "s_base_t"))
        block = c.enter_context(nc.Block())
        N_BLOCKS = 2 * HEADS + G

        @block.sync
        def _(sp):
            n_edges = 0
            for a, b in ((m["src"].rearrange("(p t) -> p t", t=T), edge_i[:, 0, :]),
                         (m["dst"].rearrange("(p t) -> p t", t=T), edge_i[:, 1, :]),
                         (m["rel"].rearrange("(p t) -> p t", t=T), edge_i[:, 2, :]),
                         (m["near"], near_i[:, :]),
                         (m["ew"].rearrange("(p t) -> p t", t=T), m["ew_sb"][:, :])):
                sp.dma_start(b, a).then_inc(s_edges, 16)
                n_edges += 1
            assert n_edges == 5
            row = lambda v: v.rearrange("(a n) -> a n", a=1)
            col = lambda v: v.rearrange("(n a) -> n a", a=1)
            for a, b in ((m["wk"], wk_nat[:, :]), (m["wv"], wv_nat[:, :]), (m["wk_t"], m["wkv_sb"][:, 0:D]),
                         (m["wq_t"], m["wq_sb"][:, :]), (row(m["bq"]), m["bq_row"][:, :]),
                         (row(m["bk"]), m["bkv_row"][:, 0:D]), (col(m["bk"]), bk_col[:, :]),
                         (col(m["bv"]), bv_col[:, :]), (m["w_loop"], m["wloop_sb"][:, :]),
                         (m["w_bases"].rearrange("b i o -> i b o"),
                          m["bases_sb"][:, :].rearrange("i (b o) -> i b o", b=BASES)),
                         (m["w_coef_t"], coef_t[:, :]), (m["att_l"], att_row[:, :]),
                         (row(m["w_bias"]), m["vec_rows"][:, 0, :]), (row(m["gamma"]), m["vec_rows"][:, 1, :]),
                         (row(m["beta"]), m["vec_rows"][:, 2, :])):
                sp.dma_start(b, a).then_inc(s_weights, 16)
            sp.wait_ge(s_ends, 1)
            sp.dma_start(ends_dram, ends[:, :]).then_inc(s_ends_out, 16)
            sp.wait_ge(s_ends_out, 16)
            sp.dma_start(ends_all[:, :, :], ends_dram.partition_broadcast(P)).then_inc(s_ends_in, 16)

        @block.scalar
        def _(act):
            act.wait_ge(s_zero, 1)
            for h in range(HEADS):
                a, b = h * DK, (h + 1) * DK
                act.dma_start(msg_blocks[a:b, a:b], m["rel_msg"][h]).then_inc(s_blocks, 16)
                act.dma_start(att_blocks[a:b, h:h + 1],
                              m["rel_att"][h].rearrange("(d a) -> d a", a=1), allow_slow_non_contiguous=True).then_inc(s_blocks, 16)
            for j in range(G):
                act.dma_start(m["coef_blocks"][j * RELS:(j + 1) * RELS, j * BASES:(j + 1) * BASES],
                              m["w_coef"]).then_inc(s_blocks, 16)

        @block.gpsimd
        def _(pool):
            nc.gpsimd.memset(msg_blocks[:, :], 0.0)
            nc.gpsimd.memset(att_blocks[:, :], 0.0)
            nc.gpsimd.memset(m["coef_blocks"][:, :], 0.0).then_inc(s_zero, 1)
            nc.gpsimd.memset(m["ones_row"][:, :], 1.0)
            nc.gpsimd.memset(m["ones_col"][:, :], 1.0)
            nc.gpsimd.memset(m["eps_col"][:, :], EPS)
            nc.gpsimd.memset(m["head_sum"][:, :], 0.0)
            nc.gpsimd.memset(rows[:, 0, :], 0.0)
            nc.gpsimd.iota(iota_i[:, :], pattern=[[1, RELS]], base=0, channel_multiplier=0)
            nc.gpsimd.memset(carried_by[:, :], 1.0)
            nc.gpsimd.memset(ident[:, :], 0.0).then_inc(s_pool, 1)
            pool.wait_ge(s_pool, 1)
            nc.gpsimd.affine_select(out=ident[:, :], in_=ident[:, :], compare_op=ALU.not_equal, fill=1.0, base=0,
                                    pattern=[[-1, P]], channel_multiplier=1)
            nc.gpsimd.affine_select(out=carried_by[:, :], in_=carried_by[:, :], compare_op=ALU.is_gt, fill=0.0,
                                    base=0, pattern=[[1, P]], channel_multiplier=-1).then_inc(s_pool_done, 1)

        @block.vector
        def _(dve):
            link = Chain(dve, s_dve)
            ts, tt, cp = nc.vector.tensor_scalar, nc.vector.tensor_tensor, nc.vector.tensor_copy
            dve.wait_ge(s_edges, 16 * 5)
            cp(dst_x[:, 1:T + 1], edge_i[:, 1, :])
            cp(dst_x[:, 0:1], near_i[:, 0:1])
            cp(dst_x[:, T + 1:T + 2], near_i[:, 1:2])
            cp(m["rel_f"][:, :], edge_i[:, 2, :])
            cp(gather_idx[:, :, 0:G], edge_i[:, 0, :].rearrange("p (g j) -> p g j", j=G))
            link(cp(ends[:, 0:1], edge_i[:, 1, 0:1]))
            cp(ends[:, 1:2], edge_i[:, 1, T - 1:T]).then_inc(s_ends, 1)
            link(ts(t0[:, 0:T], dst_x[:, 1:T + 1], float(NODES - 1), None, ALU.min))
            link(cp(gather_idx[:, :, G:2 * G], t0[:, 0:T].rearrange("p (g j) -> p g j", j=G)))
            link(tt(equal[:, :], dst_x[:, 0:T + 1], dst_x[:, 1:T + 2], ALU.is_equal))
            nc.vector.memset(cont[:, 0:1], 0.0)
            cp(cont[:, 1:T], equal[:, 1:T])
            cp(more[:, 0:T - 1], equal[:, 1:T])
            link(nc.vector.memset(more[:, T - 1:T], 0.0))
            ts(pen_cont[:, :], cont[:, :], -1.0, FAR, ALU.add, ALU.mult)
            ts(pen_more[:, :], more[:, :], -1.0, FAR, ALU.add, ALU.mult)
            ts(stops[:, :], more[:, :], -1.0, 1.0, ALU.mult, ALU.add)
            ts(in_first[:, :], dst_x[:, 1:T + 1], dst_x[:, 1:2], None, ALU.is_equal)
            ts(in_last[:, :], dst_x[:, 1:T + 1], dst_x[:, T:T + 1], None, ALU.is_equal)
            link(tt(apart[:, :], dst_x[:, 1:2], dst_x[:, T:T + 1], ALU.not_equal))
            ts(pen_first[:, :], in_first[:, :], -1.0, FAR, ALU.add, ALU.mult)
            link(ts(pen_last[:, :], in_last[:, :], -1.0, FAR, ALU.add, ALU.mult))
            link(ts(in_last[:, :], in_last[:, :], apart[:, 0:1], None, ALU.mult))
            link(tt(t1[:, 0:T], in_first[:, :], in_last[:, :], ALU.add))
            link(ts(inside[:, :], t1[:, 0:T], -1.0, 1.0, ALU.mult, ALU.add))
            link(ts(t1[:, 0:T], in_first[:, :], equal[:, 0:1], None, ALU.mult))
            link(tt(head_end[:, :], t1[:, 0:T], stops[:, :], ALU.mult))
            link(ts(t0[:, 0:T], equal[:, 1:T + 1], -1.0, 1.0, ALU.mult, ALU.add))
            link(tt(pen_same[0][:, 0:T], t0[:, 0:T], head_end[:, :], ALU.mult))
            link(nc.vector.reduce_sum(valid[:, T:T + 1], pen_same[0][:, 0:T], AX.X))
            link(ts(t1[:, 0:T], t1[:, 0:T], -1.0, 1.0, ALU.mult, ALU.add))
            link(tt(valid[:, 0:T], t0[:, 0:T], t1[:, 0:T], ALU.mult))
            ts(t0[:, 0:T], dst_x[:, 1:T + 1], float(NODES), None, ALU.is_lt)
            link(ts(t0[:, T:T + 1], dst_x[:, 1:2], float(NODES), None, ALU.is_lt))
            link(tt(valid[:, :], valid[:, :], t0[:, :], ALU.mult))
            ts(t0[:, 0:T], dst_x[:, 1:T + 1], float(-NODES), None, ALU.add)
            link(ts(t0[:, T:T + 1], dst_x[:, 1:2], float(-NODES), None, ALU.add))
            link(tt(t0[:, :], t0[:, :], valid[:, :], ALU.mult))
            link(ts(t0[:, :], t0[:, :], float(NODES), None, ALU.add))
            link(cp(scatter_idx[:, 0:T + 1], t0[:, :]))
            dve.wait_ge(s_pool_done, 1)
            cp(m["iota_rel"][:, :], iota_i[:, :])
            dve.wait_ge(s_ends_in, 16)
            flat = ends_all[:, :, :].rearrange("p q c -> p (q c)")
            for q, mine in enumerate((dst_x[:, 1:2], dst_x[:, T:T + 1])):
                ts(same[q][:, :], flat, mine, None, ALU.is_equal)
            link(ts(base_tmp[:, 0:P], ends_all[:, :, 0], dst_x[:, T:T + 1], None, ALU.is_equal))
            link(tt(carried_by[:, :], carried_by[:, :], base_tmp[:, 0:P], ALU.mult))
            for q in range(2):
                ts(pen_same[q][:, :], same[q][:, :], -1.0, FAR, ALU.add, ALU.mult)
            dve.wait_ge(s_mm, 1)
            link(tt(base_tmp[:, :].rearrange("i (b o) -> i b o", b=BASES),
                    m["bases_sb"][:, :].rearrange("i (b o) -> i b o", b=BASES),
                    ps[:, 0, 0:D].unsqueeze(1).to_broadcast([D, BASES, D]), ALU.mult))
            nc.vector.tensor_reduce(base_att[:, :], base_tmp[:, :].rearrange("i (b o) -> i b o", b=BASES),
                                    AX.X, ALU.add).then_inc(s_base, 1)
            cp(m["wkv_sb"][:, D:2 * D], ps[:, 1, 0:D])
            cp(m["wkv_sb"][:, 2 * D:2 * D + HEADS], ps[:, 1, D:D + HEADS])
            cp(m["bkv_row"][:, D:2 * D], ps[0:1, 2, 0:D])
            cp(m["bkv_row"][:, 2 * D:2 * D + HEADS], ps[0:1, 2, D:D + HEADS])
            dve.wait_ge(s_bt, 1)
            cp(base_att_t[:, :], ps[0:BASES, 3, 0:D]).then_inc(s_base_t, 1)
            dve.wait_ge(s_fold, 1)
            cp(m["a_sb"][:, :], ps[:, 3, 256:256 + RELS])

        @block.tensor
        def _(pe):
            pe.wait_ge(s_weights, 16 * 15)
            pe.wait_ge(s_blocks, 16 * N_BLOCKS)
            pe.wait_ge(s_pool_done, 1)
            mm = nc.tensor.matmul
            mm(ps[:, 0, 0:D], m["ones_row"][:, :], att_row[:, :], start=True, stop=True)
            mm(ps[:, 1, 0:D], wv_nat[:, :], msg_blocks[:, :], start=True, stop=True)
            mm(ps[:, 1, D:D + HEADS], wk_nat[:, :], att_blocks[:, :], start=True, stop=True)
            mm(ps[0:1, 2, 0:D], bv_col[:, :], msg_blocks[:, :], start=True, stop=True)
            mm(ps[0:1, 2, D:D + HEADS], bk_col[:, :], att_blocks[:, :], start=True, stop=True).then_inc(s_mm, 1)
            pe.wait_ge(s_base, 1)
            nc.tensor.transpose(ps[0:BASES, 3, 0:D], base_att[:, :], ident[:, :]).then_inc(s_bt, 1)
            pe.wait_ge(s_base_t, 1)
            mm(ps[:, 3, 256:256 + RELS], base_att_t[:, :], coef_t[:, :], start=True, stop=True).then_inc(s_fold, 1)


def project(nc, m):
    rows, ident, att, gather_idx = m["rows"], m["ident"], m["att"], m["gather_idx"]
    with ExitStack() as c:
        new_sem = c.enter_context(phase_sems(nc))

        def sb(name, shape, dt=F32):
            return c.enter_context(nc.sbuf_tensor(name, shape, dt))

        def sems(name, n=2):
            return [new_sem(f"{name}{k}") for k in range(n)]

        def ps(name, shape):
            return c.enter_context(nc.psum_tensor(name, shape, F32))

        idx = sb("idx", [P, 2, 2 * G], I32)
        ends = sb("gathered", [P, 2, 2, G, D])
        ends_t = sb("gathered_t", [P, 2, 2, G * P])
        k_sb = sb("k_sb", [P, 2, G * D])
        prod = sb("prod", [P, 2, G * D])
        qk = sb("qk", [P, 2, G, HEADS])
        wkr = sb("wkr", [P, 2, G, HEADS])
        xin = sb("xin", [P, 2, CH, D])
        xout = sb("xout", [P, 2, CH, D])
        st = sb("st", [P, 2, CH, 6])
        mv = sb("mv", [P, 2, 3, CH])
        sd = sb("sd", [P, 2, CH])
        rstd = sb("rstd", [P, 2, CH])
        shift = sb("shift", [P, 2, CH])
        ps_t = ps("ps_t", [P, 2, G * P])
        ps_q = ps("ps_q", [P, 2, G * D])
        ps_k = ps("ps_k", [P, 2, G * D])
        ps_v = ps("ps_v", [P, G * D])
        ps_r = ps("ps_r", [P, G, HEADS])
        idx_ready, = sems("idx_ready", 1)
        fetched, saved, turned, turned_sb, projected, k_ready, att_done = (
            sems(n) for n in ("fetched", "saved", "turned", "turned_sb", "projected", "k_ready", "att_done"))
        v_done, = sems("v_done", 1)
        x_in, x_stats, sd_ready, scale_ready, x_normed, x_out = (
            sems(n) for n in ("x_in", "x_stats", "sd_ready", "scale_ready", "x_normed", "x_out"))
        s_chain, = sems("project_chain", 1)
        block = c.enter_context(nc.Block())

        @block.gpsimd
        def _(pool):
            def gather(i, k):
                g = 2 * i + k
                pool.wait_ge(fetched[k], 128 * i)
                pool.wait_ge(turned[k], i)
                pool.wait_ge(saved[k], 16 * i)
                nc.gpsimd.tensor_copy(idx[:, k, :], gather_idx[:, ds(g, 1), :].rearrange("p a j -> p (a j)"))\
                    .then_inc(idx_ready, 1)
                pool.wait_ge(idx_ready, g + 1)
                carry_wait(nc, m)
                for e in range(2):
                    for j in range(G):
                        nc.gpsimd.indirect_dma_start(
                            out=ends[:, k, e, j, :], out_offset=None, in_=m["x"][:, :],
                            in_offset=bass.IndirectOffsetOnAxis(ap=idx[:, k, e * G + j:e * G + j + 1], axis=0),
                        ).then_inc(fetched[k], 16)
            in_pairs(pool, gather)

        @block.sync
        def _(sp):
            def load(i, k, np=P):
                g = 2 * i + k
                sp.wait_ge(x_normed[k], i)
                sp.dma_start(xin[0:np, k, :, :], m["x"][ds(g * CHUNK, np * CH), :]
                             .rearrange("(p j) d -> p j d", j=CH)).then_inc(x_in[k], 16)

            def keep(i, k):
                g = 2 * i + k
                sp.wait_ge(fetched[k], 128 * (i + 1))
                sp.dma_start(m["xd_kept"][0][:, ds(G * g, G), :], ends[:, k, 1, :, :]).then_inc(saved[k], 16)

            def store(i, k, np=P):
                g = 2 * i + k
                sp.wait_ge(x_normed[k], i + 1)
                sp.dma_start(m["x1_table"][ds(g * CHUNK, np * CH), :].rearrange("(p j) d -> p j d", j=CH),
                             xout[0:np, k, :, :]).then_inc(x_out[k], 16)

            def pair(i):
                load(i, 1)
                keep(i, 0)
                store(i, 0)
                load(i + 1, 0)
                keep(i, 1)
                store(i, 1)
            load(0, 0)
            pair(0)
            with sp.Fori(1, PAIRS - 1) as i:
                pair(i)
            i = PAIRS - 1
            load(i, 1)
            keep(i, 0)
            store(i, 0)
            load(i + 1, 0, LASTP)
            keep(i, 1)
            store(i, 1)
            keep(PAIRS, 0)
            store(PAIRS, 0, LASTP)
            for k, n in ((0, PAIRS + 1), (1, PAIRS)):
                sp.wait_ge(saved[k], 16 * n)
                sp.wait_ge(x_out[k], 16 * n)

        @block.tensor
        def _(pe):
            def turn(i, k):
                g = 2 * i + k
                pe.wait_ge(fetched[k], 128 * (i + 1))
                pe.wait_ge(turned_sb[0], i + k)
                pe.wait_ge(turned_sb[1], i)
                for e in range(2):
                    for j in range(G):
                        last = nc.tensor.transpose(ps_t[:, e, j * P:(j + 1) * P], ends[:, k, e, j, :], ident[:, :])
                last.then_inc(turned[k], 1)

            def mult(i, k, ahead):
                if ahead is not None:
                    turn(*ahead)
                g = 2 * i + k
                mm = nc.tensor.matmul
                ones = m["ones_row"][:, :]
                pe.wait_ge(turned_sb[k], i + 1)
                pe.wait_ge(att_done[k], i)
                for j in range(G):
                    s_t = ends_t[:, k, 0, j * P:(j + 1) * P]
                    d_t = ends_t[:, k, 1, j * P:(j + 1) * P]
                    mm(ps_k[:, k, j * D:(j + 1) * D], s_t, m["wkv_sb"][:, 0:D], start=True, stop=False)
                    mm(ps_k[:, k, j * D:(j + 1) * D], ones, m["bkv_row"][:, 0:D], start=False, stop=True)
                    mm(ps_q[:, k, j * D:(j + 1) * D], d_t, m["wq_sb"][:, :], start=True, stop=False)
                    mm(ps_q[:, k, j * D:(j + 1) * D], ones, m["bq_row"][:, :], start=False, stop=True)
                pe.wait_ge(att_done[0], i + k)
                pe.wait_ge(att_done[1], i)
                pe.wait_ge(v_done, g)
                for j in range(G):
                    s_t = ends_t[:, k, 0, j * P:(j + 1) * P]
                    mm(ps_r[:, j, :], s_t, m["wkv_sb"][:, 2 * D:2 * D + HEADS], start=True, stop=False)
                    mm(ps_r[:, j, :], ones, m["bkv_row"][:, 2 * D:2 * D + HEADS], start=False, stop=True)
                    mm(ps_v[:, j * D:(j + 1) * D], s_t, m["wkv_sb"][:, D:2 * D], start=True, stop=False)
                    last = mm(ps_v[:, j * D:(j + 1) * D], ones, m["bkv_row"][:, D:2 * D], start=False, stop=True)
                last.then_inc(projected[k], 1)
            in_pairs_ahead(pe, turn, mult)

        @block.scalar
        def _(act):
            def turned_out(i, k):
                act.wait_ge(turned[k], i + 1)
                act.wait_ge(projected[k], i)
                nc.scalar.activation(ends_t[:, k, 0, :], ps_t[:, 0, :], ACT.Copy)
                nc.scalar.activation(ends_t[:, k, 1, :], ps_t[:, 1, :], ACT.Copy).then_inc(turned_sb[k], 1)

            def deviation(i, k, np):
                act.wait_ge(x_stats[k], i + 1)
                nc.scalar.activation(sd[0:np, k, :], mv[0:np, k, 1, :], ACT.Sqrt, bias=m["eps_col"][0:np, :],
                                     scale=1.0 / D)\
                    .then_inc(sd_ready[k], 1)

            def normalise(i, k, np):
                act.wait_ge(scale_ready[k], i + 1)
                act.wait_ge(x_out[k], 16 * i)
                for j in range(CH):
                    last = nc.scalar.activation(xout[0:np, k, j, :], xin[0:np, k, j, :], ACT.Identity,
                                                bias=shift[0:np, k, j:j + 1], scale=rstd[0:np, k, j:j + 1])
                last.then_inc(x_normed[k], 1)

            def body(i, k, ahead):
                g = 2 * i + k
                np = P if ahead is not None else LASTP
                if ahead is not None:
                    turned_out(*ahead)
                deviation(i, k, np)
                act.wait_ge(projected[k], i + 1)
                act.wait_ge(att_done[k], i)
                nc.scalar.activation(k_sb[:, k, :], ps_k[:, k, :], ACT.Copy).then_inc(k_ready[k], 1)
                nc.scalar.activation(rows[:, ds(1 + G * g, G), :].rearrange("p j d -> p (j d)"), ps_v[:, :],
                                     ACT.Copy).then_inc(v_done, 1)
                normalise(i, k, np)
            in_pairs_ahead(act, turned_out, body)

        @block.vector
        def _(dve):
            def body(i, k, np=P):
                g = 2 * i + k
                link = LoopChain(dve, s_chain, PER, g)
                dve.wait_ge(x_in[k], 16 * (i + 1))
                dve.wait_ge(x_normed[k], i)
                row_stats(nc, link, st[:, k, :, :], mv[:, k, :, :], np, xin[:, k, :, :], CH).then_inc(x_stats[k], 1)
                dve.wait_ge(k_ready[k], i + 1)
                link(nc.vector.tensor_tensor(prod[:, k, :], ps_q[:, k, :], k_sb[:, k, :], ALU.mult))
                link(nc.vector.tensor_reduce(qk[:, k, :, :], prod[:, k, :].rearrange("p (j h d) -> p j h d", j=G, h=HEADS),
                                             AX.X, ALU.add), wait=False)
                link(nc.vector.tensor_tensor(wkr[:, k, :, :], ps_r[:, :, :],
                                             m["ew_sb"][:, ds(G * g, G)].unsqueeze(2).to_broadcast([P, G, HEADS]),
                                             ALU.mult))
                nc.vector.tensor_tensor(att[:, :, ds(G * g, G)].rearrange("p h j -> p j h"), qk[:, k, :, :],
                                        wkr[:, k, :, :], ALU.add).then_inc(att_done[k], 1)
                dve.wait_ge(sd_ready[k], i + 1)
                link(nc.vector.reciprocal(rstd[0:np, k, :], sd[0:np, k, :]))
                nc.vector.scalar_tensor_tensor(shift[0:np, k, :], mv[0:np, k, 2, :], -0.5, rstd[0:np, k, :],
                                               ALU.mult, ALU.mult).then_inc(scale_ready[k], 1)
                link.end()
            PER = 7
            body(0, 0)
            body(0, 1)
            with dve.Fori(1, PAIRS) as i:
                body(i, 0)
                body(i, 1)
            body(PAIRS, 0, LASTP)


def segment_softmax(nc, m, layer):
    att, weight = m["att"], m["weight"]
    H = HEADS if layer == 0 else 1
    HS = H + 1 if layer == 0 else 1
    scale = float(DK) ** -0.5 if layer == 0 else 1.0
    b_dram = [nc.dram_tensor(f"boundary{layer}{n}", [P, 2 * h], F32).ap() for n, h in enumerate((H, HS))]
    with ExitStack() as c:
        new_sem = c.enter_context(phase_sems(nc))

        def sb(name, shape, dt=F32):
            return c.enter_context(nc.sbuf_tensor(f"{name}_l{layer}", shape, dt))

        def sem(name):
            return new_sem(f"{name}_l{layer}")

        a = sb("scan_a", [P, HS, T])
        b = sb("scan_b", [P, HS, T])
        mine = sb("mine", [P, 2, 2, HS])
        all_ = sb("all", [P, 2 * P, HS])
        tmp = sb("tmp", [P, HS, 2 * P])
        whole = sb("whole", [P, 2, 2, HS])
        s_dve, s_mine, s_out, s_in, s_diff, s_exp, s_deg = (sem(n) for n in (
            "s_dve", "s_mine", "s_out", "s_in", "s_diff", "s_exp", "s_deg"))
        block = c.enter_context(nc.Block())

        @block.sync
        def _(sp):
            for n, h in enumerate((H, HS)):
                sp.wait_ge(s_mine, n + 1)
                src = mine[:, n, :, 0:h]
                sp.dma_start(b_dram[n].rearrange("p (c h) -> p c h", c=2), src).then_inc(s_out, 16)
                sp.wait_ge(s_out, 16 * (n + 1))
                sp.dma_start(all_[:, :, 0:h], b_dram[n].rearrange("p (c h) -> (p c) h", c=2).partition_broadcast(P))\
                    .then_inc(s_in, 16)

        @block.scalar
        def _(act):
            act.wait_ge(s_diff, 1)
            nc.scalar.activation(a[:, 0:H, :], a[:, 0:H, :], ACT.Exp, scale=scale).then_inc(s_exp, 1)
            if layer == 0:
                act.wait_ge(s_deg, 1)
                nc.scalar.activation(m["norm"][:, :], b[:, H, :], ACT.Sqrt)

        @block.vector
        def _(dve):
            link = Chain(dve, s_dve)
            tt, stt, cp = nc.vector.tensor_tensor, nc.vector.scalar_tensor_tensor, nc.vector.tensor_copy
            scan = nc.vector.tensor_tensor_scan

            def over_heads(v, h):
                return v.unsqueeze(1).to_broadcast([P, h, v.shape[-1]])

            def boundary(n, h, masks, op, combine):
                dve.wait_ge(s_in, 16 * (n + 1))
                for q in range(2):
                    link(tt(tmp[:, 0:h, :], all_[:, :, 0:h].rearrange("p k h -> p h k"), over_heads(masks[q][:, :], h),
                            combine))
                    link(nc.vector.tensor_reduce(whole[:, n, q, 0:h], tmp[:, 0:h, :], AX.X, op))

            if layer == 1:
                link(nc.vector.tensor_scalar(a[:, 0, :], att[:, 0, :], SLOPE, None, ALU.mult))
                link(tt(att[:, 0, :], att[:, 0, :], a[:, 0, :], ALU.max))
            for h in range(H):
                last = scan(a[:, h, :], m["pen_cont"][:, :], att[:, h, :], 0.0, ALU.add, ALU.max)
            link(last)
            for h in range(H):
                last = scan(b[:, h, ::-1], m["pen_more"][:, ::-1], a[:, h, ::-1], 0.0, ALU.add, ALU.max)
            link(last)
            cp(mine[:, 0, 0, 0:H], b[:, 0:H, 0])
            cp(mine[:, 0, 1, 0:H], b[:, 0:H, T - 1]).then_inc(s_mine, 1)
            boundary(0, H, m["pen_same"], ALU.max, ALU.add)
            for q, pen in enumerate((m["pen_first"], m["pen_last"])):
                for h in range(H):
                    last = stt(b[:, h, :], pen[:, :], whole[:, 0, q, h:h + 1], b[:, h, :], ALU.add, ALU.max)
                link(last)
            tt(a[:, 0:H, :], att[:, 0:H, :], b[:, 0:H, :], ALU.subtract).then_inc(s_diff, 1)
            if layer == 0:
                link(nc.vector.memset(a[:, H, :], 1.0))
            dve.wait_ge(s_exp, 1)
            for h in range(HS):
                last = scan(b[:, h, :], m["cont"][:, :], a[:, h, :], 0.0, ALU.mult, ALU.add)
            link(last)
            link(tt(b[:, 0:HS, :], b[:, 0:HS, :], over_heads(m["stops"][:, :], HS), ALU.mult))
            for h in range(HS):
                last = scan(weight[:, h, ::-1], m["more"][:, ::-1], b[:, h, ::-1], 0.0, ALU.mult, ALU.add)
            link(last)
            nc.vector.tensor_scalar(mine[:, 1, 0, 0:HS], weight[:, 0:HS, 0], m["apart"][:, 0:1], None, ALU.mult)
            cp(mine[:, 1, 1, 0:HS], weight[:, 0:HS, T - 1]).then_inc(s_mine, 1)
            boundary(1, HS, m["same"], ALU.add, ALU.mult)
            link(tt(weight[:, 0:HS, :], weight[:, 0:HS, :], over_heads(m["inside"][:, :], HS), ALU.mult))
            for q, mask in enumerate((m["in_first"], m["in_last"])):
                for h in range(HS):
                    last = stt(weight[:, h, :], mask[:, :], whole[:, 1, q, h:h + 1], weight[:, h, :], ALU.mult, ALU.add)
                link(last)
            if layer == 0:
                link(nc.vector.tensor_scalar(weight[:, H, :], weight[:, H, :], 1.0, None, ALU.max))
            link(nc.vector.reciprocal(b[:, :, :], weight[:, 0:HS, :]))
            if layer == 0:
                tt(weight[:, 0:H, :], a[:, 0:H, :], b[:, 0:H, :], ALU.mult).then_inc(s_deg, 1)
            else:
                link(tt(weight[:, 0, :], a[:, 0, :], b[:, 0, :], ALU.mult))
                tt(weight[:, 0, :], weight[:, 0, :], m["norm"][:, :], ALU.mult)


def running_sums(nc, m, link, g, before):
    rows, head = m["rows"], m["head_sum"]

    def row(j):
        return rows[:, ds(1 + G * g + j, 1), :].rearrange("p a d -> p (a d)")

    start = link.n

    def add(j):
        link(nc.vector.scalar_tensor_tensor(row(j), before if j == 0 else row(j - 1), m["cont"][:, ds(G * g + j, 1)],
                                            row(j), ALU.mult, ALU.add), wait=False)

    def head_add(j):
        link(nc.vector.scalar_tensor_tensor(head[:, :], row(j), m["head_end"][:, ds(G * g + j, 1)], head[:, :],
                                            ALU.mult, ALU.add), wait=False)
    add(0)
    for j in range(G):
        link.wait(link.n)
        if j + 1 < G:
            add(j + 1)
        head_add(j)
    link.wait(link.n)
    assert link.n == start + 2 * G


def sum_layer0(nc, m):
    rows, ident, weight, coef = m["rows"], m["ident"], m["weight"], m["coef"]
    with ExitStack() as c:
        new_sem = c.enter_context(phase_sems(nc))

        def sb(name, shape, dt=F32):
            return c.enter_context(nc.sbuf_tensor(f"{name}_s0", shape, dt))

        def sems(name, n=2):
            return [new_sem(f"{name}_s0{k}") for k in range(n)]

        xd = sb("xd", [P, 2, G, D])
        z = sb("z", [P, 2, G, D])
        x1 = sb("x1", [P, 2, G, D])
        st = sb("st", [P, 2, G, 6])
        mv = sb("mv", [P, 2, 3, G])
        sd = sb("sd", [P, 2, G])
        rstd = sb("rstd", [P, 2, G])
        shift = sb("shift", [P, 2, G])
        idx = sb("idx", [P, 2, G], I32)
        hot = sb("hot", [P, 2, G, RELS])
        hot_t = sb("hot_t", [P, 2, P])
        ps_h = c.enter_context(nc.psum_tensor("ps_h_s0", [P, 2, 512], F32))
        ps_c = c.enter_context(nc.psum_tensor("ps_c_s0", [P, 2, 512], F32))
        ps_f = c.enter_context(nc.psum_tensor("ps_f_s0", [P, 512], F32))
        xd_in, zed, sd_ready, scale_ready, normed, sent, hot_ready, hot_turned, hot_sb, coef_ps, coef_done = (
            sems(n) for n in ("xd_in", "zed", "sd_ready", "scale_ready", "normed", "sent", "hot_ready",
                              "hot_turned", "hot_sb", "coef_ps", "coef_done"))
        s_chain, s_idx, s_tail, s_carried, s_fix = (sems(n, 1)[0] for n in (
            "chain", "idx_ready", "tail", "carried", "fix"))
        block = c.enter_context(nc.Block())
        PER = 1 + 2 * G + 5

        @block.sync
        def _(sp):
            def load(i, k):
                g = 2 * i + k
                sp.wait_ge(zed[k], i)
                sp.dma_start(xd[:, k, :, :], m["xd_kept"][0][:, ds(G * g, G), :]).then_inc(xd_in[k], 16)
            in_pairs(sp, load)
            sp.wait_ge(zed[1], PAIRS)
            sp.dma_start(xd[:, 1, 0, :], m["xd_kept"][0][:, 0, :]).then_inc(xd_in[1], 16)

        def layernorm(dve, link, i, k, n):
            row_stats(nc, link, st[:, k, :, :], mv[:, k, :, :], P, z[:, k, :, :], n).then_inc(zed[k], 1)
            dve.wait_ge(sd_ready[k], i + 1)
            link(nc.vector.reciprocal(rstd[:, k, 0:n], sd[:, k, 0:n]))
            nc.vector.scalar_tensor_tensor(shift[:, k, 0:n], mv[:, k, 2, 0:n], -0.5, rstd[:, k, 0:n],
                                           ALU.mult, ALU.mult).then_inc(scale_ready[k], 1)

        @block.vector
        def _(dve):
            def body(i, k):
                g = 2 * i + k
                link = LoopChain(dve, s_chain, PER, g)
                dve.wait_ge(hot_turned[k], i)
                nc.vector.tensor_tensor(hot[:, k, :, :], m["iota_rel"][:, :].unsqueeze(1).to_broadcast([P, G, RELS]),
                                        m["rel_f"][:, ds(G * g, G)].unsqueeze(2).to_broadcast([P, G, RELS]),
                                        ALU.is_equal).then_inc(hot_ready[k], 1)
                wv = rows[:, ds(1 + G * g, G), :].rearrange("p j (h d) -> p j h d", h=HEADS)
                link(nc.vector.tensor_tensor(
                    wv, wv, weight[:, 0:HEADS, ds(G * g, G)].rearrange("p h j -> p j h").unsqueeze(3)
                    .to_broadcast([P, G, HEADS, DK]), ALU.mult))
                running_sums(nc, m, link, g, rows[:, ds(G * g, 1), :].rearrange("p a d -> p (a d)"))
                dve.wait_ge(xd_in[k], 16 * (i + 1))
                dve.wait_ge(normed[k], i)
                link(nc.vector.scalar_tensor_tensor(z[:, k, :, :], rows[:, ds(1 + G * g, G), :], 0.0, xd[:, k, :, :],
                                                    ALU.max, ALU.add))
                layernorm(dve, link, i, k, G)
                dve.wait_ge(coef_ps[k], i + 1)
                nc.vector.tensor_scalar(coef[:, ds(G * g, G), :], ps_c[:, k, 0:G * BASES]
                                        .rearrange("p (j b) -> p j b", j=G), 1.0, None, ALU.mult)\
                    .then_inc(coef_done[k], 1)
                link.end()
            in_pairs(dve, body)
            dve.wait_ge(s_carried, 1)
            nc.vector.tensor_tensor(rows[:, FIX, :], ps_f[:, 0:D], m["head_sum"][:, :], ALU.add).then_inc(s_fix, 1)
            dve.wait_ge(s_fix, 1)
            link = Chain(dve, s_tail)
            dve.wait_ge(xd_in[1], 16 * (PAIRS + 1))
            dve.wait_ge(normed[1], PAIRS)
            link(nc.vector.scalar_tensor_tensor(z[:, 1, 0, :], rows[:, FIX, :], 0.0, xd[:, 1, 0, :], ALU.max, ALU.add))
            layernorm(dve, link, PAIRS, 1, 1)
            link(nc.vector.memset(m["head_sum"][:, :], 0.0))

        @block.tensor
        def _(pe):
            def body(i, k):
                pe.wait_ge(hot_ready[k], i + 1)
                pe.wait_ge(hot_sb[k], i)
                nc.tensor.transpose(ps_h[:, k, 0:P], hot[:, k, :, :].rearrange("p j r -> p (j r)"), ident[:, :])\
                    .then_inc(hot_turned[k], 1)
                pe.wait_ge(hot_sb[k], i + 1)
                pe.wait_ge(coef_done[k], i)
                nc.tensor.matmul(ps_c[:, k, 0:G * BASES], hot_t[:, k, :], m["coef_blocks"][:, :], start=True,
                                 stop=True).then_inc(coef_ps[k], 1)
            in_pairs(pe, body)
            pe.wait_ge(s_chain, PER * NG)
            nc.tensor.matmul(ps_f[:, 0:D], m["carried_by"][:, :], rows[:, T, :], start=True, stop=True)\
                .then_inc(s_carried, 1)

        @block.scalar
        def _(act):
            def normalise(i, k, n):
                act.wait_ge(zed[k], i + 1)
                nc.scalar.activation(sd[:, k, 0:n], mv[:, k, 1, 0:n], ACT.Sqrt, bias=m["eps_col"][:, :],
                                     scale=1.0 / D)\
                    .then_inc(sd_ready[k], 1)
                act.wait_ge(scale_ready[k], i + 1)
                act.wait_ge(sent[k], 16 * G * i)
                for j in range(n):
                    last = nc.scalar.activation(x1[:, k, j, :], z[:, k, j, :], ACT.Identity,
                                                bias=shift[:, k, j:j + 1], scale=rstd[:, k, j:j + 1])
                last.then_inc(normed[k], 1)

            def body(i, k):
                act.wait_ge(hot_turned[k], i + 1)
                act.wait_ge(coef_ps[k], i)
                nc.scalar.activation(hot_t[:, k, :], ps_h[:, k, 0:P], ACT.Copy).then_inc(hot_sb[k], 1)
                normalise(i, k, G)
            in_pairs(act, body)
            normalise(PAIRS, 1, 1)

        @block.gpsimd
        def _(pool):
            def scatter(i, k, n=G):
                g = 2 * i + k
                col = T if n < G else G * g
                turn = NG if n < G else g
                pool.wait_ge(sent[k], 16 * G * i)
                carry_wait(nc, m)
                nc.gpsimd.tensor_copy(idx[:, k, 0:n], m["scatter_idx"][:, ds(col, n)]).then_inc(s_idx, 1)
                pool.wait_ge(s_idx, turn + 1)
                pool.wait_ge(normed[k], i + 1)
                carry_wait(nc, m, 1)
                for j in range(n):
                    nc.gpsimd.indirect_dma_start(
                        out=m["x1_table"][:, :],
                        out_offset=bass.IndirectOffsetOnAxis(ap=idx[:, k, j:j + 1], axis=0),
                        in_=x1[:, k, j, :], in_offset=None, bounds_check=NODES - 1, oob_is_err=False,
                    ).then_inc(sent[k], 16)
            in_pairs(pool, scatter)
            scatter(PAIRS, 1, 1)
            pool.wait_ge(sent[0], 16 * G * (PAIRS + 1))
            pool.wait_ge(sent[1], 16 * (G * PAIRS + 1))


def messages(nc, m):
    rows, ident, att, gather_idx, coef = m["rows"], m["ident"], m["att"], m["gather_idx"], m["coef"]
    with ExitStack() as c:
        new_sem = c.enter_context(phase_sems(nc))

        def sb(name, shape, dt=F32):
            return c.enter_context(nc.sbuf_tensor(f"{name}_m", shape, dt))

        def sems(name, n=2):
            return [new_sem(f"{name}_m{k}") for k in range(n)]

        def ps(name, shape):
            return c.enter_context(nc.psum_tensor(f"{name}_m", shape, F32))

        idx = sb("idx", [P, 2, 2 * G], I32)
        ends = sb("gathered", [P, 2, 2, G, D])
        ends_t = sb("gathered_t", [P, 2, 2, G * P])
        hot = sb("hot", [P, 2, G, RELS])
        sel = sb("sel", [P, 2, G, RELS])
        xg = sb("xg", [P, 2, CH, D + 1])
        zeros = sb("zeros", [P, P])
        ps_t = ps("ps_t", [P, 2, G * P])
        ps_p = ps("ps_p", [P, 2, BASES * D])
        ps_s = ps("ps_s", [P, G, RELS])
        ps_g = ps("ps_g", [P, 512])
        fetched, saved, turned, turned_sb, based, p_free, scored, score_done, x_in, grammed = (
            sems(n) for n in ("fetched", "saved", "turned", "turned_sb", "based", "p_free", "scored", "score_done",
                              "x_in", "grammed"))
        idx_ready, s_chain, s_set, s_gram = (sems(n, 1)[0] for n in ("idx_ready", "chain", "set", "gram"))
        block = c.enter_context(nc.Block())
        PER = G * (BASES - 1) + 2

        @block.gpsimd
        def _(pool):
            def gather(i, k):
                g = 2 * i + k
                pool.wait_ge(fetched[k], 128 * i)
                pool.wait_ge(turned[k], i)
                pool.wait_ge(saved[k], 16 * i)
                nc.gpsimd.tensor_copy(idx[:, k, :], gather_idx[:, ds(g, 1), :].rearrange("p a j -> p (a j)"))\
                    .then_inc(idx_ready, 1)
                pool.wait_ge(idx_ready, g + 1)
                carry_wait(nc, m)
                for e in range(2):
                    for j in range(G):
                        nc.gpsimd.indirect_dma_start(
                            out=ends[:, k, e, j, :], out_offset=None, in_=m["x1_table"][:, :],
                            in_offset=bass.IndirectOffsetOnAxis(ap=idx[:, k, e * G + j:e * G + j + 1], axis=0),
                        ).then_inc(fetched[k], 16)
            in_pairs(pool, gather)

        @block.sync
        def _(sp):
            def load(i, k, np=P):
                g = 2 * i + k
                sp.wait_ge(grammed[k], i)
                sp.dma_start(xg[0:np, k, :, 0:D], m["x1_table"][ds(g * CHUNK, np * CH), :]
                             .rearrange("(p j) d -> p j d", j=CH)).then_inc(x_in[k], 16)

            def keep(i, k):
                g = 2 * i + k
                sp.wait_ge(fetched[k], 128 * (i + 1))
                sp.dma_start(m["xd_kept"][1][:, ds(G * g, G), :], ends[:, k, 1, :, :]).then_inc(saved[k], 16)

            def pair(i):
                load(i, 1)
                keep(i, 0)
                load(i + 1, 0)
                keep(i, 1)
            load(0, 0)
            pair(0)
            with sp.Fori(1, PAIRS - 1) as i:
                pair(i)
            load(PAIRS - 1, 1)
            keep(PAIRS - 1, 0)
            load(PAIRS, 0, LASTP)
            keep(PAIRS - 1, 1)
            keep(PAIRS, 0)
            sp.wait_ge(saved[0], 16 * (PAIRS + 1))
            sp.wait_ge(saved[1], 16 * PAIRS)

        @block.tensor
        def _(pe):
            mm = nc.tensor.matmul

            def turn(i, k):
                g = 2 * i + k
                pe.wait_ge(fetched[k], 128 * (i + 1))
                pe.wait_ge(turned_sb[0], i + k)
                pe.wait_ge(turned_sb[1], i)
                for e in range(2):
                    for j in range(G):
                        last = nc.tensor.transpose(ps_t[:, e, j * P:(j + 1) * P], ends[:, k, e, j, :], ident[:, :])
                last.then_inc(turned[k], 1)

            def body(i, k, ahead):
                np = P if ahead is not None else LASTP
                if ahead is not None:
                    turn(*ahead)
                pe.wait_ge(turned_sb[k], i + 1)
                pe.wait_ge(score_done[0], i + k)
                pe.wait_ge(score_done[1], i)
                for j in range(G):
                    s_t = ends_t[:, k, 0, j * P:(j + 1) * P]
                    d_t = ends_t[:, k, 1, j * P:(j + 1) * P]
                    mm(ps_s[:, j, :], s_t, m["a_sb"][:, :], start=True, stop=False)
                    last = mm(ps_s[:, j, :], d_t, m["a_sb"][:, :], start=False, stop=True)
                last.then_inc(scored[k], 1)
                for j in range(G):
                    s_t = ends_t[:, k, 0, j * P:(j + 1) * P]
                    uses = (2 * i + k) * (G // 2) + j // 2
                    pe.wait_ge(p_free[j % 2], uses)
                    for half in range(2):
                        last = mm(ps_p[:, j % 2, half * 512:(half + 1) * 512], s_t,
                                  m["bases_sb"][:, half * 512:(half + 1) * 512], start=True, stop=True)
                    last.then_inc(based[j % 2], 1)
                pe.wait_ge(x_in[k], 16 * (i + 1))
                for j in range(CH):
                    last = mm(ps_g[:, 0:D + 1], xg[0:np, k, j, 0:D], xg[0:np, k, j, :], start=False,
                              stop=False, skip_group_check=True)
                last.then_inc(grammed[k], 1)

            pe.wait_ge(s_set, 1)
            mm(ps_g[:, 0:D + 1], zeros[:, :], zeros129(m), start=True, stop=False,
               skip_group_check=True)
            in_pairs_ahead(pe, turn, body)
            mm(ps_g[:, 0:D + 1], zeros[:, :], zeros129(m), start=False, stop=True,
               skip_group_check=True).then_inc(s_gram, 1)

        @block.scalar
        def _(act):
            def turned_out(i, k):
                act.wait_ge(turned[k], i + 1)
                act.wait_ge(grammed[k], i)
                nc.scalar.activation(ends_t[:, k, 0, :], ps_t[:, 0, :], ACT.Copy)
                nc.scalar.activation(ends_t[:, k, 1, :], ps_t[:, 1, :], ACT.Copy).then_inc(turned_sb[k], 1)

            def body(i, k, ahead):
                if ahead is not None:
                    turned_out(*ahead)
            in_pairs_ahead(act, turned_out, body)

        @block.vector
        def _(dve):
            nc.vector.memset(zeros[:, :], 0.0)
            nc.vector.memset(xg[:, 0, :, D:D + 1], 1.0)
            nc.vector.memset(xg[:, 1, :, D:D + 1], 1.0).then_inc(s_set, 1)

            def body(i, k):
                g = 2 * i + k
                link = LoopChain(dve, s_chain, PER, g)
                link(nc.vector.tensor_tensor(hot[:, k, :, :],
                                             m["iota_rel"][:, :].unsqueeze(1).to_broadcast([P, G, RELS]),
                                             m["rel_f"][:, ds(G * g, G)].unsqueeze(2).to_broadcast([P, G, RELS]),
                                             ALU.is_equal))
                dve.wait_ge(scored[k], i + 1)
                link(nc.vector.tensor_tensor(sel[:, k, :, :], ps_s[:, :, :], hot[:, k, :, :], ALU.mult))
                nc.vector.tensor_reduce(att[:, 0, ds(G * g, G)], sel[:, k, :, :], AX.X, ALU.add)\
                    .then_inc(score_done[k], 1)
                for j in range(G):
                    row = rows[:, ds(1 + G * g + j, 1), :].rearrange("p a d -> p (a d)")
                    dve.wait_ge(based[j % 2], g * (G // 2) + j // 2 + 1)

                    def cf(b):
                        return coef[:, ds(G * g + j, 1), b:b + 1].rearrange("p a b -> p (a b)")
                    link(nc.vector.tensor_scalar(row, ps_p[:, j % 2, 0:D], cf(0), None, ALU.mult))
                    for b in range(1, BASES):
                        ins = nc.vector.scalar_tensor_tensor(row, ps_p[:, j % 2, b * D:(b + 1) * D], cf(b), row,
                                                             ALU.mult, ALU.add)
                        if b < BASES - 1:
                            link(ins)
                        else:
                            ins.then_inc(p_free[j % 2], 1)
                link.end()
            in_pairs(dve, body)
            dve.wait_ge(s_gram, 1)
            nc.vector.tensor_copy(m["gram_sb"][:, :], ps_g[:, 0:D + 1])


def zeros129(m):
    return m["rows"][:, 0, 0:1].to_broadcast([P, D + 1])


def centre(nc, m):
    with ExitStack() as c:
        new_sem = c.enter_context(phase_sems(nc))

        def sb(name, shape, dt=F32):
            return c.enter_context(nc.sbuf_tensor(f"{name}_c", shape, dt))

        def sem(name):
            return new_sem(f"{name}_c")

        mean_col = sb("mean_col", [D, 1])
        mean_row = sb("mean_row", [1, D])
        gram_n = sb("gram_n", [D, D])
        cov = sb("cov", [D, D])
        cw = sb("cw", [D, D])
        mu = sb("mu", [1, D])
        ps = c.enter_context(nc.psum_tensor("ps_c", [P, 4, 512], F32))
        s_dve, s_mean, s_row, s_row_sb, s_outer, s_cov, s_cw, s_cw_sb, s_var = (sem(n) for n in (
            "s_dve", "s_mean", "s_row", "s_row_sb", "s_outer", "s_cov", "s_cw", "s_cw_sb", "s_var"))
        block = c.enter_context(nc.Block())

        @block.vector
        def _(dve):
            link = Chain(dve, s_dve)
            ts, tt = nc.vector.tensor_scalar, nc.vector.tensor_tensor
            ts(mean_col[:, :], m["gram_sb"][:, D:D + 1], 1.0 / NODES, None, ALU.mult).then_inc(s_mean, 1)
            link(ts(gram_n[:, :], m["gram_sb"][:, 0:D], 1.0 / NODES, None, ALU.mult))
            dve.wait_ge(s_row, 1)
            nc.vector.tensor_copy(mean_row[:, :], ps[0:1, 0, 0:D]).then_inc(s_row_sb, 1)
            link(tt(mu[:, :], ps[0:1, 1, 0:D], m["vec_rows"][:, 0, :], ALU.add))
            tt(m["centre_row"][:, :], m["vec_rows"][:, 0, :], mu[:, :], ALU.subtract)
            dve.wait_ge(s_outer, 1)
            tt(cov[:, :], gram_n[:, :], ps[:, 2, 0:D], ALU.subtract).then_inc(s_cov, 1)
            dve.wait_ge(s_cw, 1)
            tt(cw[:, :], ps[:, 3, 0:D], m["wloop_sb"][:, :], ALU.mult).then_inc(s_cw_sb, 1)
            dve.wait_ge(s_var, 1)
            nc.vector.tensor_copy(m["var_row"][:, :], ps[0:1, 0, 256:256 + D])

        @block.tensor
        def _(pe):
            mm = nc.tensor.matmul
            pe.wait_ge(s_mean, 1)
            nc.tensor.transpose(ps[0:1, 0, 0:D], mean_col[:, :], m["ident"][:, :])
            mm(ps[0:1, 1, 0:D], mean_col[:, :], m["wloop_sb"][:, :], start=True, stop=True).then_inc(s_row, 1)
            pe.wait_ge(s_row_sb, 1)
            mm(ps[:, 2, 0:D], mean_row[:, :], mean_row[:, :], start=True, stop=True).then_inc(s_outer, 1)
            pe.wait_ge(s_cov, 1)
            mm(ps[:, 3, 0:D], cov[:, :], m["wloop_sb"][:, :], start=True, stop=True).then_inc(s_cw, 1)
            pe.wait_ge(s_cw_sb, 1)
            mm(ps[0:1, 0, 256:256 + D], m["ones_col"][:, :], cw[:, :], start=True, stop=True).then_inc(s_var, 1)


def sum_layer1(nc, m):
    rows, ident, weight = m["rows"], m["ident"], m["weight"]
    with ExitStack() as c:
        new_sem = c.enter_context(phase_sems(nc))

        def sb(name, shape, dt=F32):
            return c.enter_context(nc.sbuf_tensor(f"{name}_s1", shape, dt))

        def sems(name, n=2):
            return [new_sem(f"{name}_s1{k}") for k in range(n)]

        def ps(name, shape):
            return c.enter_context(nc.psum_tensor(f"{name}_s1", shape, F32))

        xd = sb("xd", [P, 2, G, D])
        xd_t = sb("xd_t", [P, 2, G * P])
        carry = sb("carry", [P, 2, D])
        both = sb("both", [P, 2, G, 2, D])
        twice = sb("twice", [P, 2, G, D])
        mask = sb("mask", [P, 2, G])
        ps_t = ps("ps_t", [P, G * P])
        ps_u = ps("ps_u", [P, 2, G * D])
        ps_sum = ps("ps_sum", [1, 512])
        ps_f = ps("ps_f", [P, 512])
        xd_in, turned, turned_sb, lin, ready, summed = (
            sems(n) for n in ("xd_in", "turned", "turned_sb", "lin", "ready", "summed"))
        s_chain, s_set, s_delta, s_copied, s_carried, s_tail, s_all = (sems(n, 1)[0] for n in (
            "chain", "set", "delta", "copied", "carried", "tail", "all"))
        block = c.enter_context(nc.Block())
        PER = 1 + 2 * G + 1 + 1

        @block.sync
        def _(sp):
            def load(i, k):
                g = 2 * i + k
                sp.wait_ge(turned[k], i)
                sp.dma_start(xd[:, k, :, :], m["xd_kept"][1][:, ds(G * g, G), :]).then_inc(xd_in[k], 16)
            in_pairs(sp, load)
            sp.wait_ge(turned[1], PAIRS)
            sp.dma_start(xd[:, 1, 0, :], m["xd_kept"][1][:, 0, :]).then_inc(xd_in[1], 16)

        @block.tensor
        def _(pe):
            mm = nc.tensor.matmul

            def turn(i, k, n=G):
                pe.wait_ge(xd_in[k], 16 * (i + 1))
                pe.wait_ge(turned_sb[0], i + k)
                pe.wait_ge(turned_sb[1], i)
                for j in range(n):
                    last = nc.tensor.transpose(ps_t[:, j * P:(j + 1) * P], xd[:, k, j, :], ident[:, :])
                last.then_inc(turned[k], 1)

            def linear(i, k, n=G):
                pe.wait_ge(turned_sb[k], i + 1)
                pe.wait_ge(ready[k], i)
                for j in range(n):
                    u = ps_u[:, k, j * D:(j + 1) * D]
                    mm(u, xd_t[:, k, j * P:(j + 1) * P], m["wloop_sb"][:, :], start=True, stop=False)
                    last = mm(u, m["ones_row"][:, :], m["centre_row"][:, :], start=False, stop=True)
                last.then_inc(lin[k], 1)

            def total(i, k, n=G):
                pe.wait_ge(ready[k], i + 1)
                for j in range(n):
                    last = mm(ps_sum[:, 0:2 * D], mask[:, k, j:j + 1],
                              both[:, k, j, :, :].rearrange("p a d -> p (a d)"), start=False, stop=False,
                              skip_group_check=True)
                last.then_inc(summed[k], 1)

            def body(i, k, ahead):
                if ahead is not None:
                    turn(*ahead)
                    linear(*ahead)
                total(i, k)

            def first(i, k):
                turn(i, k)
                linear(i, k)
            pe.wait_ge(s_set, 1)
            mm(ps_sum[:, 0:2 * D], rows[:, 0, 0:1], rows[:, 0, 0:1].to_broadcast([P, 2 * D]), start=True,
               stop=False, skip_group_check=True)
            in_pairs_ahead(pe, first, body)
            turn(PAIRS, 1, 1)
            linear(PAIRS, 1, 1)
            pe.wait_ge(s_chain, PER * NG)
            mm(ps_f[:, 0:D], m["carried_by"][:, :], carry[:, 1, :], start=True, stop=True).then_inc(s_carried, 1)
            total(PAIRS, 1, 1)
            mm(ps_sum[:, 0:2 * D], m["rows"][:, 0, 0:1], rows[:, 0, 0:1].to_broadcast([P, 2 * D]), start=False,
               stop=True, skip_group_check=True).then_inc(s_all, 1)

        @block.scalar
        def _(act):
            def out(i, k, n=G):
                act.wait_ge(turned[k], i + 1)
                act.wait_ge(lin[k], i)
                nc.scalar.activation(xd_t[:, k, 0:n * P], ps_t[:, 0:n * P], ACT.Copy).then_inc(turned_sb[k], 1)

            def keep_delta(i, k):
                g = 2 * i + k
                act.wait_ge(s_delta, g + 1)
                act.wait_ge(summed[k], i)
                nc.scalar.activation(both[:, k, :, 1, :], rows[:, ds(1 + G * g, G), :], ACT.Copy).then_inc(s_copied, 1)

            def body(i, k, ahead):
                if ahead is not None:
                    out(*ahead)
                keep_delta(i, k)
            in_pairs_ahead(act, out, body)
            out(PAIRS, 1, 1)

        @block.vector
        def _(dve):
            nc.vector.memset(carry[:, 0, :], 0.0)
            nc.vector.memset(mask[:, :, :], 0.0).then_inc(s_set, 1)
            dve.wait_ge(s_set, 1)

            def body(i, k):
                g = 2 * i + k
                link = LoopChain(dve, s_chain, PER, g)
                mine = rows[:, ds(1 + G * g, G), :]
                link(nc.vector.tensor_tensor(mine, mine, weight[:, 0, ds(G * g, G)].unsqueeze(2)
                                             .to_broadcast([P, G, D]), ALU.mult))
                running_sums(nc, m, link, g, carry[:, k, :])
                link(nc.vector.tensor_scalar(carry[:, 1 - k, :], rows[:, ds(G * g + G, 1), :]
                                             .rearrange("p a d -> p (a d)"), 1.0, None, ALU.mult), wait=False)
                dve.wait_ge(summed[k], i)
                nc.vector.tensor_scalar(mask[:, k, :], m["valid"][:, ds(G * g, G)], 1.0, None, ALU.mult)\
                    .then_inc(s_delta, 1)
                dve.wait_ge(lin[k], i + 1)
                u = ps_u[:, k, :].rearrange("p (j d) -> p j d", j=G)
                link(nc.vector.scalar_tensor_tensor(twice[:, k, :, :], u, 2.0, mine, ALU.mult, ALU.add))
                nc.vector.tensor_tensor(both[:, k, :, 0, :], twice[:, k, :, :], mine, ALU.mult)
                dve.wait_ge(s_copied, g + 1)
                nc.vector.tensor_tensor(mine, u, mine, ALU.add).then_inc(ready[k], 1)
                link.end()
            in_pairs(dve, body)
            link = Chain(dve, s_tail)
            dve.wait_ge(s_carried, 1)
            fix = rows[:, FIX, :]
            dve.wait_ge(summed[1], PAIRS)
            nc.vector.tensor_copy(mask[:, 1, 0:1], m["valid"][:, T:T + 1])
            link(nc.vector.tensor_tensor(fix, ps_f[:, 0:D], m["head_sum"][:, :], ALU.add))
            dve.wait_ge(lin[1], PAIRS + 1)
            nc.vector.tensor_copy(both[:, 1, 0, 1, :], fix)
            link(nc.vector.scalar_tensor_tensor(twice[:, 1, 0, :], ps_u[:, 1, 0:D], 2.0, fix, ALU.mult, ALU.add))
            link(nc.vector.tensor_tensor(both[:, 1, 0, 0, :], twice[:, 1, 0, :], fix, ALU.mult))
            nc.vector.tensor_tensor(fix, ps_u[:, 1, 0:D], fix, ALU.add).then_inc(ready[1], 1)
            dve.wait_ge(s_all, 1)
            nc.vector.tensor_copy(m["sums_row"][:, :], ps_sum[:, 0:2 * D])


def output(nc, m):
    rows, ident = m["rows"], m["ident"]
    with ExitStack() as c:
        new_sem = c.enter_context(phase_sems(nc))

        def sb(name, shape, dt=F32):
            return c.enter_context(nc.sbuf_tensor(f"{name}_o", shape, dt))

        def sems(name, n=2):
            return [new_sem(f"{name}_o{k}") for k in range(n)]

        def ps(name, shape):
            return c.enter_context(nc.psum_tensor(f"{name}_o", shape, F32))

        ab_row = sb("ab_row", [1, 2, D])
        base_row = sb("base_row", [1, CH // 2, D])
        r = sb("r", [1, 6, D])
        ab = sb("ab", [P, 2, D])
        w_scaled = sb("w_scaled", [D, D])
        x1 = sb("x1", [P, 2, CH, D])
        x1_t = sb("x1_t", [P, 2, CH * P])
        z = sb("z", [P, 2, CH, D])
        y = sb("y", [P, 2, CH, D])
        st = sb("st", [P, 2, CH, 6])
        mv = sb("mv", [P, 2, 3, CH])
        sd = sb("sd", [P, 2, CH])
        rstd = sb("rstd", [P, 2, CH])
        shift = sb("shift", [P, 2, CH])
        idx = sb("idx", [P, 2, G], I32)
        ps_t = ps("ps_t", [P, CH * P])
        ps_u = ps("ps_u", [P, 2, CH * D])
        ps_ab = ps("ps_ab", [P, 512])
        x_in, turned, turned_sb, lin, zed, sd_ready, scale_ready, normed, x_out = (
            sems(n) for n in ("x_in", "turned", "turned_sb", "lin", "zed", "sd_ready", "scale_ready", "normed",
                              "x_out"))
        e_in, e_zed, e_sd, e_scale, e_normed, e_sent = (
            sems(n) for n in ("e_in", "e_zed", "e_sd", "e_scale", "e_normed", "e_sent"))
        s_chain, s_echain, s_rows, s_sqrt, s_sqrt_done, s_ab, s_bc, s_ready, s_idx, s_tail = (
            sems(n, 1)[0] for n in ("chain", "echain", "rows", "sqrt", "sqrt_done", "ab", "bc", "ready",
                                    "idx_ready", "tail"))
        block = c.enter_context(nc.Block())

        @block.sync
        def _(sp):
            def load(i, k, np=P):
                g = 2 * i + k
                sp.wait_ge(zed[k], i)
                sp.dma_start(x1[0:np, k, :, :], m["x1_table"][ds(g * CHUNK, np * CH), :]
                             .rearrange("(p j) d -> p j d", j=CH)).then_inc(x_in[k], 16)

            def store(i, k, np=P):
                g = 2 * i + k
                sp.wait_ge(normed[k], i + 1)
                sp.dma_start(m["out"][ds(g * CHUNK, np * CH), :].rearrange("(p j) d -> p j d", j=CH),
                             y[0:np, k, :, :]).then_inc(x_out[k], 16)

            def pair(i):
                load(i, 1)
                store(i, 0)
                load(i + 1, 0)
                store(i, 1)
            load(0, 0)
            pair(0)
            with sp.Fori(1, PAIRS - 1) as i:
                pair(i)
            load(PAIRS - 1, 1)
            store(PAIRS - 1, 0)
            load(PAIRS, 0, LASTP)
            store(PAIRS - 1, 1)
            store(PAIRS, 0, LASTP)
            sp.wait_ge(zed[0], PAIRS + 1)
            sp.wait_ge(zed[1], PAIRS)

            def load_edges(i, k):
                g = 2 * i + k
                sp.wait_ge(e_zed[k], i)
                sp.dma_start(x1[:, k, 0:G, :], m["xd_kept"][1][:, ds(G * g, G), :]).then_inc(e_in[k], 16)
            in_pairs(sp, load_edges)
            sp.wait_ge(e_zed[1], PAIRS)
            sp.dma_start(x1[:, 1, 0, :], m["xd_kept"][1][:, 0, :]).then_inc(e_in[1], 16)
            sp.wait_ge(x_out[0], 16 * (PAIRS + 1))
            sp.wait_ge(x_out[1], 16 * PAIRS)

        @block.tensor
        def _(pe):
            mm = nc.tensor.matmul

            def turn(i, k, np):
                pe.wait_ge(x_in[k], 16 * (i + 1))
                pe.wait_ge(turned_sb[0], i + k)
                pe.wait_ge(turned_sb[1], i)
                for j in range(CH):
                    last = nc.tensor.transpose(ps_t[:, j * P:j * P + np], x1[0:np, k, j, :], ident[0:np, 0:np])
                last.then_inc(turned[k], 1)

            def linear(i, k, np):
                pe.wait_ge(turned_sb[k], i + 1)
                pe.wait_ge(zed[k], i)
                for j in range(CH):
                    u = ps_u[0:np, k, j * D:(j + 1) * D]
                    mm(u, x1_t[:, k, j * P:j * P + np], w_scaled[:, :], start=True, stop=False)
                    last = mm(u, m["ones_row"][:, 0:np], base_row[:, 0, :], start=False, stop=True)
                last.then_inc(lin[k], 1)

            pe.wait_ge(s_ab, 1)
            mm(ps_ab[:, 0:2 * D], m["ones_row"][:, :], ab_row[:, :, :].rearrange("p a d -> p (a d)"),
               start=True, stop=True).then_inc(s_bc, 1)
            def pair(i):
                turn(i, 1, P)
                linear(i, 0, P)
                turn(i + 1, 0, P)
                linear(i, 1, P)
            turn(0, 0, P)
            pe.wait_ge(s_ready, 1)
            pair(0)
            with pe.Fori(1, PAIRS - 1) as i:
                pair(i)
            turn(PAIRS - 1, 1, P)
            linear(PAIRS - 1, 0, P)
            turn(PAIRS, 0, LASTP)
            linear(PAIRS - 1, 1, P)
            linear(PAIRS, 0, LASTP)

        @block.scalar
        def _(act):
            def out(i, k, np):
                act.wait_ge(turned[k], i + 1)
                act.wait_ge(lin[k], i)
                for half in range(2):
                    v = slice(half * G * P, (half + 1) * G * P)
                    if np == P:
                        a, b = x1_t[:, k, v], ps_t[:, v]
                    else:
                        a, b = (t.rearrange("p (j q) -> p j q", j=G)[:, :, 0:np] for t in (x1_t[:, k, v], ps_t[:, v]))
                    last = nc.scalar.activation(a, b, ACT.Copy)
                last.then_inc(turned_sb[k], 1)

            def normalise(i, k, np, n, zed, sd_ready, scale_ready, normed, gone):
                act.wait_ge(zed[k], i + 1)
                nc.scalar.activation(sd[0:np, k, 0:n], mv[0:np, k, 1, 0:n], ACT.Sqrt, bias=m["eps_col"][0:np, :],
                                     scale=1.0 / D)\
                    .then_inc(sd_ready[k], 1)
                act.wait_ge(scale_ready[k], i + 1)
                act.wait_ge(*gone)
                for j in range(n):
                    last = nc.scalar.activation(y[0:np, k, j, :], z[0:np, k, j, :], ACT.Identity,
                                                bias=shift[0:np, k, j:j + 1], scale=rstd[0:np, k, j:j + 1])
                last.then_inc(normed[k], 1)

            def nodes(i, k, np=P):
                normalise(i, k, np, CH, zed, sd_ready, scale_ready, normed, (x_out[k], 16 * i))

            act.wait_ge(s_sqrt, 1)
            nc.scalar.activation(r[:, 3, :], r[:, 2, :], ACT.Sqrt).then_inc(s_sqrt_done, 1)
            def pair(i):
                out(i, 1, P)
                nodes(i, 0)
                out(i + 1, 0, P)
                nodes(i, 1)
            out(0, 0, P)
            pair(0)
            with act.Fori(1, PAIRS - 1) as i:
                pair(i)
            out(PAIRS - 1, 1, P)
            nodes(PAIRS - 1, 0)
            out(PAIRS, 0, LASTP)
            nodes(PAIRS - 1, 1)
            nodes(PAIRS, 0, LASTP)
            act.wait_ge(x_out[0], 16 * (PAIRS + 1))
            act.wait_ge(x_out[1], 16 * PAIRS)

            def edges(i, k, n=G):
                normalise(i, k, P, n, e_zed, e_sd, e_scale, e_normed, (e_sent[k], 16 * G * i))
            in_pairs(act, edges)
            edges(PAIRS, 1, 1)

        @block.vector
        def _(dve):
            link = Chain(dve, s_rows)
            ts, tt, stt = nc.vector.tensor_scalar, nc.vector.tensor_tensor, nc.vector.scalar_tensor_tensor
            link(ts(r[:, 0:2, :], m["sums_row"][:, :].rearrange("p (a d) -> p a d", a=2), 1.0 / NODES, None, ALU.mult))
            link(tt(r[:, 2, :], r[:, 1, :], r[:, 1, :], ALU.mult))
            link(tt(r[:, 2, :], r[:, 0, :], r[:, 2, :], ALU.subtract))
            link(tt(r[:, 2, :], r[:, 2, :], m["var_row"][:, :], ALU.add))
            ts(r[:, 2, :], r[:, 2, :], EPS, None, ALU.add).then_inc(s_sqrt, 1)
            dve.wait_ge(s_sqrt_done, 1)
            link(nc.vector.reciprocal(r[:, 4, :], r[:, 3, :]))
            link(tt(ab_row[:, 0, :], m["vec_rows"][:, 1, :], r[:, 4, :], ALU.mult))
            link(tt(r[:, 5, :], r[:, 1, :], ab_row[:, 0, :], ALU.mult))
            link(tt(ab_row[:, 1, :], m["vec_rows"][:, 2, :], r[:, 5, :], ALU.subtract))
            link(tt(r[:, 0, :], m["centre_row"][:, :], ab_row[:, 0, :], ALU.mult))
            tt(base_row[:, 0, :], r[:, 0, :], ab_row[:, 1, :], ALU.add).then_inc(s_ab, 1)
            dve.wait_ge(s_bc, 1)
            link(nc.vector.tensor_copy(ab[:, :, :], ps_ab[:, 0:2 * D].rearrange("p (a d) -> p a d", a=2)))
            tt(w_scaled[:, :], m["wloop_sb"][:, :], ab[:, 0, :], ALU.mult).then_inc(s_ready, 1)

            def stats(link, i, k, np, n, zed, sd_ready, scale_ready):
                row_stats(nc, link, st[:, k, :, :], mv[:, k, :, :], np, z[:, k, :, :], n).then_inc(zed[k], 1)

            def scales(link, i, k, np, n, sd_ready, scale_ready):
                dve.wait_ge(sd_ready[k], i + 1)
                link(nc.vector.reciprocal(rstd[0:np, k, 0:n], sd[0:np, k, 0:n]))
                stt(shift[0:np, k, 0:n], mv[0:np, k, 2, 0:n], -0.5, rstd[0:np, k, 0:n], ALU.mult, ALU.mult)\
                    .then_inc(scale_ready[k], 1)

            def nodes(i, k, np=P):
                link = LoopChain(dve, s_chain, 5, 2 * i + k)
                dve.wait_ge(lin[k], i + 1)
                dve.wait_ge(normed[k], i)
                for half in range(2):
                    v = slice(half * G, (half + 1) * G)
                    last = stt(z[0:np, k, v, :], ps_u[0:np, k, half * G * D:(half + 1) * G * D]
                               .rearrange("p (j d) -> p j d", j=G), 0.0, x1[0:np, k, v, :], ALU.max, ALU.add)
                link(last)
                stats(link, i, k, np, CH, zed, sd_ready, scale_ready)
                scales(link, i, k, np, CH, sd_ready, scale_ready)
                link.end()
            nodes(0, 0)
            nodes(0, 1)
            with dve.Fori(1, PAIRS) as i:
                nodes(i, 0)
                nodes(i, 1)
            nodes(PAIRS, 0, LASTP)
            dve.wait_ge(normed[0], PAIRS + 1)
            dve.wait_ge(normed[1], PAIRS)

            def edges(i, k):
                g = 2 * i + k
                link = LoopChain(dve, s_echain, 7, g)
                mine = rows[:, ds(1 + G * g, G), :]
                dve.wait_ge(e_normed[k], i)
                zz = z[:, k, 0:G, :]
                link(tt(zz, mine, ab[:, 0, :].unsqueeze(1).to_broadcast([P, G, D]), ALU.mult))
                link(tt(zz, zz, ab[:, 1, :].unsqueeze(1).to_broadcast([P, G, D]), ALU.add))
                dve.wait_ge(e_in[k], 16 * (i + 1))
                link(stt(zz, zz, 0.0, x1[:, k, 0:G, :], ALU.max, ALU.add))
                stats(link, i, k, P, G, e_zed, e_sd, e_scale)
                scales(link, i, k, P, G, e_sd, e_scale)
                link.end()
            in_pairs(dve, edges)
            link = Chain(dve, s_tail)
            dve.wait_ge(e_normed[1], PAIRS)
            zz = z[:, 1, 0, :]
            link(tt(zz, rows[:, FIX, :], ab[:, 0, :], ALU.mult))
            link(tt(zz, zz, ab[:, 1, :], ALU.add))
            dve.wait_ge(e_in[1], 16 * (PAIRS + 1))
            link(stt(zz, zz, 0.0, x1[:, 1, 0, :], ALU.max, ALU.add))
            stats(link, PAIRS, 1, P, 1, e_zed, e_sd, e_scale)
            scales(link, PAIRS, 1, P, 1, e_sd, e_scale)

        @block.gpsimd
        def _(pool):
            pool.wait_ge(x_out[0], 16 * (PAIRS + 1))
            pool.wait_ge(x_out[1], 16 * PAIRS)

            def scatter(i, k, n=G):
                g = 2 * i + k
                col = T if n < G else G * g
                turn = NG if n < G else g
                pool.wait_ge(e_sent[k], 16 * G * i)
                carry_wait(nc, m)
                nc.gpsimd.tensor_copy(idx[:, k, 0:n], m["scatter_idx"][:, ds(col, n)]).then_inc(s_idx, 1)
                pool.wait_ge(s_idx, turn + 1)
                pool.wait_ge(e_normed[k], i + 1)
                carry_wait(nc, m, 1)
                for j in range(n):
                    nc.gpsimd.indirect_dma_start(
                        out=m["out"][:, :], out_offset=bass.IndirectOffsetOnAxis(ap=idx[:, k, j:j + 1], axis=0),
                        in_=y[:, k, j, :], in_offset=None, bounds_check=NODES - 1, oob_is_err=False,
                    ).then_inc(e_sent[k], 16)
            in_pairs(pool, scatter)
            scatter(PAIRS, 1, 1)
            pool.wait_ge(e_sent[0], 16 * G * (PAIRS + 1))
            pool.wait_ge(e_sent[1], 16 * (G * PAIRS + 1))


def kernel(**inputs):
    import numpy as np
    import concourse.bacc as bacc
    from concourse.bass_utils import run_bass_kernel_spmd as run

    fill = P * T - EDGES
    a = {n: np.asarray(v) for n, v in inputs.items()}
    pad = lambda v: np.concatenate([v, np.zeros(fill, v.dtype)])
    dst = a["dst"]
    dst = np.concatenate([np.full(1, -1, dst.dtype), dst, np.full(fill, NODES, dst.dtype),
                          np.full(1, NODES + 1, dst.dtype)])
    arrays = {
        "x": a["x"], "src": pad(a["src"]), "dst": dst[1:-1], "near": np.stack([dst[0:P * T:T], dst[T + 1::T]], 1), "rel": pad(a["edge_type_32"]), "ew": pad(a["edge_weight"]),
        "wk": a["L0_gnn_Wk"], "wk_t": a["L0_gnn_Wk"].T, "bk": a["L0_gnn_bk"], "wq_t": a["L0_gnn_Wq"].T,
        "bq": a["L0_gnn_bq"], "wv": a["L0_gnn_Wv"], "bv": a["L0_gnn_bv"], "rel_att": a["L0_gnn_rel_att"],
        "rel_msg": a["L0_gnn_rel_msg"], "w_loop": a["L1_gnn_w_loop"], "w_bases": a["L1_gnn_w_bases"],
        "w_coef": a["L1_gnn_w_rel_coef"], "w_coef_t": a["L1_gnn_w_rel_coef"].T, "att_l": a["L1_gnn_att_l_w"],
        "w_bias": a["L1_gnn_w_bias"], "gamma": a["L1_gnn_bn_gamma"], "beta": a["L1_gnn_bn_beta"],
    }
    arrays = {n: np.ascontiguousarray(v) for n, v in arrays.items()}
    nc = bacc.Bacc("TRN2", target_bir_lowering=False, num_devices=1)
    args = {n: nc.dram_tensor(f"in_{n}", v.shape, mybir.dt.from_np(v.dtype), kind="ExternalInput").ap()
            for n, v in arrays.items()}
    out = nc.dram_tensor("out_0", (NODES, D), F32, kind="ExternalOutput").ap()
    program(nc, out=out, **args)
    r = run(nc, [{f"in_{n}": v for n, v in arrays.items()}], core_ids=[0])
    return r.results[0]["out_0"]
```

```python
from contextlib import ExitStack, contextmanager

import concourse.bass as bass
from concourse import mybir

ALU = mybir.AluOpType
ACT = mybir.ActivationFunctionType
AX = mybir.AxisListType
F32 = mybir.dt.float32
BF16 = mybir.dt.bfloat16
I32 = mybir.dt.int32

NODES = 50000
EDGES = 25000
D = 128
HEADS = 8
DK = D // HEADS
RELS = 32
BASES = 8
P = 128
T = -(-EDGES // P)
G = 4
NG = T // G
UNROLL = 4
CH = 8
CHUNK = P * CH
NCH = -(-NODES // CHUNK)
LASTP = (NODES - (NCH - 1) * CHUNK) // CH
FIX = T + 1
FAR = 3.0e38
EPS = 1e-5
SLOPE = 0.01
assert NG * G == T and NG % UNROLL == 1 and NCH == NG and (NCH - 1) * CHUNK + LASTP * CH == NODES
ds = bass.ds


class Turn:

    def __init__(self, i, k):
        self.i, self.k = i, k
        self.g = UNROLL * i + k
        self.starts = isinstance(i, int) and i == 0
        self.last = isinstance(i, int) and self.g == NG - 1
        self.np = LASTP if self.last else P

    def slot(self, n=2):
        return self.k % n

    def uses(self, n=2):
        return UNROLL // n * self.i + self.k // n

    def next(self):
        return None if self.last else Turn(self.i, self.k + 1) if self.k + 1 < UNROLL else Turn(self.i + 1, 0)


def in_turns(eng, body):
    for k in range(UNROLL):
        body(Turn(0, k))
    with eng.Fori(1, NG // UNROLL) as i:
        for k in range(UNROLL):
            body(Turn(i, k))
    body(Turn(NG // UNROLL, 0))


FIX_TURN = Turn(NG // UNROLL, 1)
FIX_TURN_USES = [len(range(s, NG, 2)) for s in range(2)]


class Chain:

    def __init__(self, eng, sem):
        self.eng, self.sem, self.n = eng, sem, 0

    def __call__(self, ins):
        self.n += 1
        ins.then_inc(self.sem, 1)
        self.eng.wait_ge(self.sem, self.n)


class LoopChain:

    def __init__(self, eng, sem, per, turn):
        self.eng, self.sem, self.per, self.turn, self.n = eng, sem, per, turn, 0

    def __call__(self, ins, wait=True):
        self.n += 1
        ins.then_inc(self.sem, 1)
        if wait:
            self.wait(self.n)

    def wait(self, n):
        self.eng.wait_ge(self.sem, self.turn * self.per + n)

    def end(self):
        assert self.n == self.per, (self.n, self.per)


def program(nc, x, src, dst, near, rel, ew, wk, wk_t, bk, wq_t, bq, wv, bv, rel_att, rel_msg, w_loop, w_bases,
            w_coef, w_coef_t, att_l, w_bias, gamma, beta, out):
    x1_table = nc.dram_tensor("x1_table", [NODES, D], F32).ap()
    xd_kept = [nc.dram_tensor(f"xd_kept{n}", [P, T, D], F32).ap() for n in range(2)]
    ctx = ExitStack()

    def sb(name, shape, dt=F32, c=ctx):
        return c.enter_context(nc.sbuf_tensor(name, shape, dt))

    with ctx:
        rows = sb("rows", [P, T + 2, D])
        ident = sb("ident", [P, P])
        ones_row = sb("ones_row", [1, P])
        ones_col = sb("ones_col", [P, 1])
        carried_by = sb("carried_by", [P, P])
        dst_x = sb("dst_x", [P, T + 2])
        cont = sb("cont", [P, T])
        more = sb("more", [P, T])
        pen_cont = sb("pen_cont", [P, T])
        pen_more = sb("pen_more", [P, T])
        stops = sb("stops", [P, T])
        in_first = sb("in_first", [P, T])
        in_last = sb("in_last", [P, T])
        inside = sb("inside", [P, T])
        pen_first = sb("pen_first", [P, T])
        pen_last = sb("pen_last", [P, T])
        head_end = sb("head_end", [P, T])
        valid = sb("valid", [P, T + 1])
        apart = sb("apart", [P, 1])
        same = [sb(f"same{q}", [P, 2 * P]) for q in range(2)]
        pen_same = [sb(f"pen_same{q}", [P, 2 * P]) for q in range(2)]
        gather_idx = sb("gather_idx", [P, NG, 2 * G], I32)
        scatter_idx = sb("scatter_idx", [P, T + G], I32)
        ew_sb = sb("ew_sb", [P, T])
        rel_f = sb("rel_f", [P, T])
        iota_rel = sb("iota_rel", [P, RELS])
        coef = sb("coef", [P, T, BASES])
        att = sb("att", [P, HEADS, T])
        weight = sb("weight", [P, HEADS + 1, T])
        norm = sb("norm", [P, T])
        head_sum = sb("head_sum", [P, D])
        eps_col = sb("eps_col", [P, 1])
        scrap = sb("scrap", [P, 2])
        wq_sb = sb("wq_sb", [D, D])
        wkv_sb = sb("wkv_sb", [D, 2 * D])
        bq_parts = sb("bq_parts", [3, D], BF16)
        bkv_parts = sb("bkv_parts", [3, 2 * D], BF16)
        centre_parts = sb("centre_parts", [3, D], BF16)
        ones3 = sb("ones3", [3, P], BF16)
        split_f = sb("split_f", [3, 2 * D])
        split_b = sb("split_b", [3, 3, 2 * D], BF16)
        rel_att_all = sb("rel_att_all", [P, D])
        wloop_sb = sb("wloop_sb", [D, D])
        bases_sb = sb("bases_sb", [D, BASES * D])
        a_sb = sb("a_sb", [D, RELS])
        coef_blocks = sb("coef_blocks", [P, G * BASES])
        vec_rows = sb("vec_rows", [3, 3, D])
        centre_row = sb("centre_row", [3, D])
        var_row = sb("var_row", [3, D])
        gram_sb = sb("gram_sb", [P, D + 1])
        sums_row = sb("sums_row", [3, 2 * D])

        setup(nc, locals())
        m = locals()
        project(nc, m)
        segment_softmax(nc, m, 0)
        sum_layer0(nc, m)
        messages(nc, m)
        segment_softmax(nc, m, 1)
        centre(nc, m)
        sum_layer1(nc, m)
        output(nc, m)


@contextmanager
def phase_sems(nc):
    made = []

    def sem(name):
        made.append(nc.alloc_semaphore(name))
        return made[-1]
    yield sem
    nc.clear_and_free_semaphores(made)
    nc.all_engine_barrier()


def carry_wait(nc, m, n=0):
    nc.gpsimd.tensor_tensor(m["scrap"][:, n:n + 1], m["eps_col"][:, :], m["eps_col"][:, :], ALU.add)


def row_stats(nc, link, st, part, np, x, n):
    for j in range(n):
        last = nc.vector.bn_stats(st[0:np, j, :], x[0:np, j, :])
    link(last)
    s, p = st[0:np, 0:n, :], part[0:np]
    tt = nc.vector.tensor_tensor
    tt(p[:, 2, 0:n], s[:, :, 1], s[:, :, 4], ALU.add)
    tt(p[:, 1, 0:n], s[:, :, 2], s[:, :, 5], ALU.add)
    link(tt(p[:, 0, 0:n], s[:, :, 1], s[:, :, 4], ALU.subtract))
    link(tt(p[:, 0, 0:n], p[:, 0, 0:n], p[:, 0, 0:n], ALU.mult))
    return nc.vector.scalar_tensor_tensor(p[:, 1, 0:n], p[:, 0, 0:n], D / 4.0, p[:, 1, 0:n], ALU.mult, ALU.add)


def split3(nc, m, link, out, x, t):
    f, b = t
    n = x.shape[-1]
    f, b, pick = f[:, 0:n], b[:, :, 0:n], m["ident"]
    cp, tt = nc.vector.tensor_copy, nc.vector.tensor_tensor
    link(cp(b[:, 0, :], x))
    link(tt(f, x, b[:, 0, :], ALU.subtract))
    link(cp(b[:, 1, :], f))
    link(tt(f, f, b[:, 1, :], ALU.subtract))
    link(cp(b[:, 2, :], f))
    link(nc.vector.tensor_scalar(out, b[:, 0, :], pick[0:3, 0:1], None, ALU.mult))
    for k in (1, 2):
        link(nc.vector.scalar_tensor_tensor(out, b[:, k, :], pick[0:3, k:k + 1], out, ALU.mult, ALU.add))


def setup(nc, m):
    (dst_x, cont, more, pen_cont, pen_more, stops, in_first, in_last, inside, pen_first, pen_last, head_end, valid,
     apart, same, pen_same, ident) = (m[n] for n in (
        "dst_x", "cont", "more", "pen_cont", "pen_more", "stops", "in_first", "in_last", "inside", "pen_first",
        "pen_last", "head_end", "valid", "apart", "same", "pen_same", "ident"))
    gather_idx, scatter_idx, carried_by, rows = m["gather_idx"], m["scatter_idx"], m["carried_by"], m["rows"]
    ends_dram = nc.dram_tensor("ends_dram", [P, 2], F32).ap()
    with ExitStack() as c:
        new_sem = c.enter_context(phase_sems(nc))

        def sb(name, shape, dt=F32):
            return c.enter_context(nc.sbuf_tensor(name, shape, dt))

        def sem(name):
            return new_sem(name)

        edge_i = sb("edge_i", [P, 3, T], I32)
        near_i = sb("near_i", [P, 2], I32)
        iota_i = sb("iota_i", [P, RELS], I32)
        equal = sb("equal", [P, T + 1])
        t0 = sb("t0", [P, T + 1])
        t1 = sb("t1", [P, T + 1])
        ends = sb("ends", [P, 2])
        ends_all = sb("ends_all", [P, P, 2])
        wv_nat = sb("wv_nat", [D, D])
        msg_blocks = sb("msg_blocks", [D, D])
        bias3 = sb("bias3", [3, 3, D])
        bv_col = sb("bv_col", [D, 1])
        att_row = sb("att_row", [1, D])
        coef_t = sb("coef_t", [BASES, RELS])
        base_att = sb("base_att", [D, BASES])
        base_tmp = sb("base_tmp", [D, BASES * D])
        base_att_t = sb("base_att_t", [BASES, D])
        ps = c.enter_context(nc.psum_tensor("ps_setup", [P, 4, 512], F32))
        s_zero, s_blocks, s_edges, s_weights = sem("s_zero"), sem("s_blocks"), sem("s_edges"), sem("s_weights")
        s_pool, s_pool_done, s_dve, s_mm, s_base, s_bt = (sem(n) for n in (
            "s_pool", "s_pool_done", "s_dve", "s_mm", "s_base", "s_bt"))
        s_ends, s_ends_out, s_ends_in, s_fold, s_base_t = (sem(n) for n in (
            "s_ends", "s_ends_out", "s_ends_in", "s_fold", "s_base_t"))
        block = c.enter_context(nc.Block())
        N_BLOCKS = HEADS + G

        @block.sync
        def _(sp):
            n_edges = 0
            for a, b in ((m["src"].rearrange("(p t) -> p t", t=T), edge_i[:, 0, :]),
                         (m["dst"].rearrange("(p t) -> p t", t=T), edge_i[:, 1, :]),
                         (m["rel"].rearrange("(p t) -> p t", t=T), edge_i[:, 2, :]),
                         (m["near"], near_i[:, :]),
                         (m["ew"].rearrange("(p t) -> p t", t=T), m["ew_sb"][:, :])):
                sp.dma_start(b, a).then_inc(s_edges, 16)
                n_edges += 1
            assert n_edges == 5
            col = lambda v: v.rearrange("(n a) -> n a", a=1)
            for a, b in ((m["wv"], wv_nat[:, :]), (m["wk_t"], m["wkv_sb"][:, 0:D]),
                         (m["wq_t"], m["wq_sb"][:, :]), (m["bq"].partition_broadcast(3), bias3[:, 2, :]),
                         (m["bk"].partition_broadcast(3), bias3[:, 0, :]),
                         (m["rel_att"].rearrange("h d -> (h d)").partition_broadcast(P), m["rel_att_all"][:, :]),
                         (col(m["bv"]), bv_col[:, :]), (m["w_loop"], m["wloop_sb"][:, :]),
                         (m["w_bases"].rearrange("b i o -> i b o"),
                          m["bases_sb"][:, :].rearrange("i (b o) -> i b o", b=BASES)),
                         (m["w_coef_t"], coef_t[:, :]), (m["att_l"], att_row[:, :]),
                         (m["w_bias"].partition_broadcast(3), m["vec_rows"][:, 0, :]),
                         (m["gamma"].partition_broadcast(3), m["vec_rows"][:, 1, :]),
                         (m["beta"].partition_broadcast(3), m["vec_rows"][:, 2, :])):
                sp.dma_start(b, a).then_inc(s_weights, 16)
            sp.wait_ge(s_ends, 1)
            sp.dma_start(ends_dram, ends[:, :]).then_inc(s_ends_out, 16)
            sp.wait_ge(s_ends_out, 16)
            sp.dma_start(ends_all[:, :, :], ends_dram.partition_broadcast(P)).then_inc(s_ends_in, 16)

        @block.scalar
        def _(act):
            act.wait_ge(s_zero, 1)
            for h in range(HEADS):
                a, b = h * DK, (h + 1) * DK
                act.dma_start(msg_blocks[a:b, a:b], m["rel_msg"][h]).then_inc(s_blocks, 16)
            for j in range(G):
                act.dma_start(m["coef_blocks"][j * RELS:(j + 1) * RELS, j * BASES:(j + 1) * BASES],
                              m["w_coef"]).then_inc(s_blocks, 16)

        @block.gpsimd
        def _(pool):
            nc.gpsimd.memset(msg_blocks[:, :], 0.0)
            nc.gpsimd.memset(m["coef_blocks"][:, :], 0.0).then_inc(s_zero, 1)
            nc.gpsimd.memset(m["ones_row"][:, :], 1.0)
            nc.gpsimd.memset(m["ones_col"][:, :], 1.0)
            nc.gpsimd.memset(m["ones3"][:, :], 1.0)
            nc.gpsimd.memset(m["eps_col"][:, :], EPS)
            nc.gpsimd.memset(m["head_sum"][:, :], 0.0)
            nc.gpsimd.memset(rows[:, 0, :], 0.0)
            nc.gpsimd.iota(iota_i[:, :], pattern=[[1, RELS]], base=0, channel_multiplier=0)
            nc.gpsimd.memset(carried_by[:, :], 1.0)
            nc.gpsimd.memset(ident[:, :], 0.0).then_inc(s_pool, 1)
            pool.wait_ge(s_pool, 1)
            nc.gpsimd.affine_select(out=ident[:, :], in_=ident[:, :], compare_op=ALU.not_equal, fill=1.0, base=0,
                                    pattern=[[-1, P]], channel_multiplier=1)
            nc.gpsimd.affine_select(out=carried_by[:, :], in_=carried_by[:, :], compare_op=ALU.is_gt, fill=0.0,
                                    base=0, pattern=[[1, P]], channel_multiplier=-1).then_inc(s_pool_done, 1)

        @block.vector
        def _(dve):
            link = Chain(dve, s_dve)
            ts, tt, cp = nc.vector.tensor_scalar, nc.vector.tensor_tensor, nc.vector.tensor_copy
            dve.wait_ge(s_edges, 16 * 5)
            cp(dst_x[:, 1:T + 1], edge_i[:, 1, :])
            cp(dst_x[:, 0:1], near_i[:, 0:1])
            cp(dst_x[:, T + 1:T + 2], near_i[:, 1:2])
            cp(m["rel_f"][:, :], edge_i[:, 2, :])
            cp(gather_idx[:, :, 0:G], edge_i[:, 0, :].rearrange("p (g j) -> p g j", j=G))
            link(cp(ends[:, 0:1], edge_i[:, 1, 0:1]))
            cp(ends[:, 1:2], edge_i[:, 1, T - 1:T]).then_inc(s_ends, 1)
            link(ts(t0[:, 0:T], dst_x[:, 1:T + 1], float(NODES - 1), None, ALU.min))
            link(cp(gather_idx[:, :, G:2 * G], t0[:, 0:T].rearrange("p (g j) -> p g j", j=G)))
            link(tt(equal[:, :], dst_x[:, 0:T + 1], dst_x[:, 1:T + 2], ALU.is_equal))
            nc.vector.memset(cont[:, 0:1], 0.0)
            cp(cont[:, 1:T], equal[:, 1:T])
            cp(more[:, 0:T - 1], equal[:, 1:T])
            link(nc.vector.memset(more[:, T - 1:T], 0.0))
            ts(pen_cont[:, :], cont[:, :], -1.0, FAR, ALU.add, ALU.mult)
            ts(pen_more[:, :], more[:, :], -1.0, FAR, ALU.add, ALU.mult)
            ts(stops[:, :], more[:, :], -1.0, 1.0, ALU.mult, ALU.add)
            ts(in_first[:, :], dst_x[:, 1:T + 1], dst_x[:, 1:2], None, ALU.is_equal)
            ts(in_last[:, :], dst_x[:, 1:T + 1], dst_x[:, T:T + 1], None, ALU.is_equal)
            link(tt(apart[:, :], dst_x[:, 1:2], dst_x[:, T:T + 1], ALU.not_equal))
            ts(pen_first[:, :], in_first[:, :], -1.0, FAR, ALU.add, ALU.mult)
            link(ts(pen_last[:, :], in_last[:, :], -1.0, FAR, ALU.add, ALU.mult))
            link(ts(in_last[:, :], in_last[:, :], apart[:, 0:1], None, ALU.mult))
            link(tt(t1[:, 0:T], in_first[:, :], in_last[:, :], ALU.add))
            link(ts(inside[:, :], t1[:, 0:T], -1.0, 1.0, ALU.mult, ALU.add))
            link(ts(t1[:, 0:T], in_first[:, :], equal[:, 0:1], None, ALU.mult))
            link(tt(head_end[:, :], t1[:, 0:T], stops[:, :], ALU.mult))
            link(ts(t0[:, 0:T], equal[:, 1:T + 1], -1.0, 1.0, ALU.mult, ALU.add))
            link(tt(pen_same[0][:, 0:T], t0[:, 0:T], head_end[:, :], ALU.mult))
            link(nc.vector.reduce_sum(valid[:, T:T + 1], pen_same[0][:, 0:T], AX.X))
            link(ts(t1[:, 0:T], t1[:, 0:T], -1.0, 1.0, ALU.mult, ALU.add))
            link(tt(valid[:, 0:T], t0[:, 0:T], t1[:, 0:T], ALU.mult))
            ts(t0[:, 0:T], dst_x[:, 1:T + 1], float(NODES), None, ALU.is_lt)
            link(ts(t0[:, T:T + 1], dst_x[:, 1:2], float(NODES), None, ALU.is_lt))
            link(tt(valid[:, :], valid[:, :], t0[:, :], ALU.mult))
            ts(t0[:, 0:T], dst_x[:, 1:T + 1], float(-NODES), None, ALU.add)
            link(ts(t0[:, T:T + 1], dst_x[:, 1:2], float(-NODES), None, ALU.add))
            link(tt(t0[:, :], t0[:, :], valid[:, :], ALU.mult))
            link(ts(t0[:, :], t0[:, :], float(NODES), None, ALU.add))
            link(cp(scatter_idx[:, 0:T + 1], t0[:, :]))
            dve.wait_ge(s_pool_done, 1)
            cp(m["iota_rel"][:, :], iota_i[:, :])
            dve.wait_ge(s_ends_in, 16)
            flat = ends_all[:, :, :].rearrange("p q c -> p (q c)")
            for q, mine in enumerate((dst_x[:, 1:2], dst_x[:, T:T + 1])):
                ts(same[q][:, :], flat, mine, None, ALU.is_equal)
            link(ts(base_tmp[:, 0:P], ends_all[:, :, 0], dst_x[:, T:T + 1], None, ALU.is_equal))
            link(tt(carried_by[:, :], carried_by[:, :], base_tmp[:, 0:P], ALU.mult))
            for q in range(2):
                ts(pen_same[q][:, :], same[q][:, :], -1.0, FAR, ALU.add, ALU.mult)
            dve.wait_ge(s_mm, 1)
            link(tt(base_tmp[:, :].rearrange("i (b o) -> i b o", b=BASES),
                    m["bases_sb"][:, :].rearrange("i (b o) -> i b o", b=BASES),
                    ps[:, 0, 0:D].unsqueeze(1).to_broadcast([D, BASES, D]), ALU.mult))
            nc.vector.tensor_reduce(base_att[:, :], base_tmp[:, :].rearrange("i (b o) -> i b o", b=BASES),
                                    AX.X, ALU.add).then_inc(s_base, 1)
            cp(m["wkv_sb"][:, D:2 * D], ps[:, 1, 0:D])
            link(cp(bias3[:, 1, :], ps[0:3, 2, 0:D]))
            t = (m["split_f"], m["split_b"])
            split3(nc, m, link, m["bkv_parts"][:, :], bias3[:, 0:2, :].rearrange("p a d -> p (a d)"), t)
            split3(nc, m, link, m["bq_parts"][:, :], bias3[:, 2, :], t)
            dve.wait_ge(s_bt, 1)
            cp(base_att_t[:, :], ps[0:BASES, 3, 0:D]).then_inc(s_base_t, 1)
            dve.wait_ge(s_fold, 1)
            cp(m["a_sb"][:, :], ps[:, 3, 256:256 + RELS])

        @block.tensor
        def _(pe):
            pe.wait_ge(s_weights, 16 * 14)
            pe.wait_ge(s_blocks, 16 * N_BLOCKS)
            pe.wait_ge(s_pool_done, 1)
            mm = nc.tensor.matmul
            mm(ps[:, 0, 0:D], m["ones_row"][:, :], att_row[:, :], start=True, stop=True)
            mm(ps[:, 1, 0:D], wv_nat[:, :], msg_blocks[:, :], start=True, stop=True)
            mm(ps[0:3, 2, 0:D], bv_col[:, :].to_broadcast([D, 3]), msg_blocks[:, :], start=True, stop=True)\
                .then_inc(s_mm, 1)
            pe.wait_ge(s_base, 1)
            nc.tensor.transpose(ps[0:BASES, 3, 0:D], base_att[:, :], ident[:, :]).then_inc(s_bt, 1)
            pe.wait_ge(s_base_t, 1)
            mm(ps[:, 3, 256:256 + RELS], base_att_t[:, :], coef_t[:, :], start=True, stop=True).then_inc(s_fold, 1)


def project(nc, m):
    rows, ident, att, gather_idx = m["rows"], m["ident"], m["att"], m["gather_idx"]
    with ExitStack() as c:
        new_sem = c.enter_context(phase_sems(nc))

        def sb(name, shape, dt=F32):
            return c.enter_context(nc.sbuf_tensor(name, shape, dt))

        def sems(name, n=2):
            return [new_sem(f"{name}{k}") for k in range(n)]

        def ps(name, shape):
            return c.enter_context(nc.psum_tensor(name, shape, F32))

        idx = sb("idx", [P, 2, 2 * G], I32)
        ends = sb("gathered", [P, 2, 2, G, D])
        ends_t = sb("gathered_t", [P, 2, 2, G * P])
        q_sb = sb("q_sb", [P, 2, G, D])
        prod = sb("prod", [P, 2, G, D])
        xin = sb("xin", [P, 4, CH, D])
        xout = sb("xout", [P, 2, CH, D])
        st = sb("st", [P, 2, CH, 6])
        mv = sb("mv", [P, 2, 3, CH])
        sd = sb("sd", [P, 2, CH])
        rstd = sb("rstd", [P, 2, CH])
        shift = sb("shift", [P, 2, CH])
        ps_t = ps("ps_t", [P, 2, G * P])
        ps_q = ps("ps_q", [P, 2, G, D])
        ps_kv = ps("ps_kv", [P, 2, G, 2 * D])
        idx_ready, s_chain = sems("idx_ready", 1)[0], sems("project_chain", 1)[0]
        fetched, saved, turned, turned_sb, projected, v_done, att_done = (
            sems(n) for n in ("fetched", "saved", "turned", "turned_sb", "projected", "v_done", "att_done"))
        x_stats, sd_ready, scale_ready, x_normed, x_out = (
            sems(n) for n in ("x_stats", "sd_ready", "scale_ready", "x_normed", "x_out"))
        x_in = sems("x_in", 4)
        block = c.enter_context(nc.Block())

        @block.gpsimd
        def _(pool):
            def gather(t):
                s, u = t.slot(), t.uses()
                pool.wait_ge(fetched[s], 128 * u)
                pool.wait_ge(turned[s], u)
                pool.wait_ge(saved[s], 16 * u)
                nc.gpsimd.tensor_copy(idx[:, s, :], gather_idx[:, ds(t.g, 1), :].rearrange("p a j -> p (a j)"))\
                    .then_inc(idx_ready, 1)
                pool.wait_ge(idx_ready, t.g + 1)
                carry_wait(nc, m)
                for e in range(2):
                    for j in range(G):
                        nc.gpsimd.indirect_dma_start(
                            out=ends[:, s, e, j, :], out_offset=None, in_=m["x"][:, :],
                            in_offset=bass.IndirectOffsetOnAxis(ap=idx[:, s, e * G + j:e * G + j + 1], axis=0),
                        ).then_inc(fetched[s], 16)
            in_turns(pool, gather)

        @block.sync
        def _(sp):
            def move(t):
                s, u, s4, u4 = t.slot(), t.uses(), t.slot(4), t.uses(4)
                if not t.starts:
                    sp.wait_ge(x_normed[s], u - 1)
                sp.dma_start(xin[0:t.np, s4, :, :], m["x"][ds(t.g * CHUNK, t.np * CH), :]
                             .rearrange("(p j) d -> p j d", j=CH)).then_inc(x_in[s4], 16)
                sp.wait_ge(fetched[s], 128 * (u + 1))
                sp.dma_start(m["xd_kept"][0][:, ds(G * t.g, G), :], ends[:, s, 1, :, :]).then_inc(saved[s], 16)
            in_turns(sp, move)
            for s in range(2):
                sp.wait_ge(saved[s], 16 * FIX_TURN_USES[s])

        @block.tensor
        def _(pe):
            mm = nc.tensor.matmul

            def turn_rows(t):
                s, u = t.slot(), t.uses()
                pe.wait_ge(fetched[s], 128 * (u + 1))
                pe.wait_ge(turned_sb[1 - s], t.uses() + s)
                for e in range(2):
                    for j in range(G):
                        last = nc.tensor.transpose(ps_t[:, e, j * P:(j + 1) * P], ends[:, s, e, j, :], ident[:, :])
                last.then_inc(turned[s], 1)

            def body(t):
                s, u = t.slot(), t.uses()
                if t.next():
                    turn_rows(t.next())
                pe.wait_ge(turned_sb[s], u + 1)
                pe.wait_ge(att_done[s], u)
                pe.wait_ge(v_done[s], u)
                mm(ps_q[:, s, :, :], m["ones3"][:, :], m["bq_parts"][:, :].unsqueeze(1).to_broadcast([3, G, D]),
                   start=True, stop=False, skip_group_check=True)
                for j in range(G):
                    mm(ps_q[:, s, j, :], ends_t[:, s, 1, j * P:(j + 1) * P], m["wq_sb"][:, :], start=False,
                       stop=True, skip_group_check=True)
                for j in range(G):
                    if j % 2 == 0:
                        mm(ps_kv[:, s, j:j + 2, :], m["ones3"][:, :],
                           m["bkv_parts"][:, :].unsqueeze(1).to_broadcast([3, 2, 2 * D]), start=True, stop=False,
                           skip_group_check=True)
                    last = mm(ps_kv[:, s, j, :], ends_t[:, s, 0, j * P:(j + 1) * P], m["wkv_sb"][:, :],
                              start=False, stop=True, skip_group_check=True)
                last.then_inc(projected[s], 1)
            turn_rows(Turn(0, 0))
            in_turns(pe, body)

        @block.scalar
        def _(act):
            def turned_out(t):
                s, u = t.slot(), t.uses()
                act.wait_ge(turned[s], u + 1)
                act.wait_ge(projected[s], u)
                nc.scalar.activation(ends_t[:, s, 0, :], ps_t[:, 0, :], ACT.Copy)
                nc.scalar.activation(ends_t[:, s, 1, :], ps_t[:, 1, :], ACT.Copy).then_inc(turned_sb[s], 1)

            def body(t):
                s, u, s4, np = t.slot(), t.uses(), t.slot(4), t.np
                if t.next():
                    turned_out(t.next())
                act.wait_ge(x_stats[s], u + 1)
                nc.scalar.activation(sd[0:np, s, :], mv[0:np, s, 1, :], ACT.Sqrt, bias=m["eps_col"][0:np, :],
                                     scale=1.0 / D).then_inc(sd_ready[s], 1)
                act.wait_ge(projected[s], u + 1)
                nc.scalar.activation(m["scrap"][:, 1:2], m["eps_col"][:, :], ACT.Copy)
                nc.scalar.activation(rows[:, ds(1 + G * t.g, G), :], ps_kv[:, s, :, D:2 * D], ACT.Copy)\
                    .then_inc(v_done[s], 1)
                act.wait_ge(scale_ready[s], u + 1)
                act.wait_ge(x_out[s], 16 * u)
                for j in range(CH):
                    last = nc.scalar.activation(xout[0:np, s, j, :], xin[0:np, s4, j, :], ACT.Identity,
                                                bias=shift[0:np, s, j:j + 1], scale=rstd[0:np, s, j:j + 1])
                last.then_inc(x_normed[s], 1)
                act.wait_ge(x_normed[s], u + 1)
                act.dma_start(m["x1_table"][ds(t.g * CHUNK, np * CH), :].rearrange("(p j) d -> p j d", j=CH),
                              xout[0:np, s, :, :]).then_inc(x_out[s], 16)
            turned_out(Turn(0, 0))
            in_turns(act, body)
            for s in range(2):
                act.wait_ge(x_out[s], 16 * FIX_TURN_USES[s])

        @block.vector
        def _(dve):
            PER = 9

            def body(t):
                s, u, s4, u4, np = t.slot(), t.uses(), t.slot(4), t.uses(4), t.np
                link = LoopChain(dve, s_chain, PER, t.g)
                dve.wait_ge(x_in[s4], 16 * (u4 + 1))
                dve.wait_ge(x_normed[s], u)
                row_stats(nc, link, st[:, s, :, :], mv[:, s, :, :], np, xin[:, s4, :, :], CH).then_inc(x_stats[s], 1)
                dve.wait_ge(projected[s], u + 1)
                for j in range(G):
                    link(nc.vector.scalar_tensor_tensor(q_sb[:, s, j, :], m["rel_att_all"][:, :],
                                                        m["ew_sb"][:, ds(G * t.g + j, 1)], ps_q[:, s, j, :],
                                                        ALU.mult, ALU.add), wait=j == G - 1)
                dve.wait_ge(v_done[s], u + 1)
                link(nc.vector.tensor_tensor(prod[:, s, :, :], q_sb[:, s, :, :], ps_kv[:, s, :, 0:D], ALU.mult))
                nc.vector.tensor_reduce(att[:, :, ds(G * t.g, G)].rearrange("p h j -> p j h"),
                                        prod[:, s, :, :].rearrange("p j (h d) -> p j h d", h=HEADS),
                                        AX.X, ALU.add).then_inc(att_done[s], 1)
                dve.wait_ge(sd_ready[s], u + 1)
                link(nc.vector.reciprocal(rstd[0:np, s, :], sd[0:np, s, :]))
                nc.vector.scalar_tensor_tensor(shift[0:np, s, :], mv[0:np, s, 2, :], -0.5, rstd[0:np, s, :],
                                               ALU.mult, ALU.mult).then_inc(scale_ready[s], 1)
                link.end()
            in_turns(dve, body)


def segment_softmax(nc, m, layer):
    att, weight = m["att"], m["weight"]
    H = HEADS if layer == 0 else 1
    HS = H + 1 if layer == 0 else 1
    scale = float(DK) ** -0.5 if layer == 0 else 1.0
    b_dram = [nc.dram_tensor(f"boundary{layer}{n}", [P, 2 * h], F32).ap() for n, h in enumerate((H, HS))]
    with ExitStack() as c:
        new_sem = c.enter_context(phase_sems(nc))

        def sb(name, shape, dt=F32):
            return c.enter_context(nc.sbuf_tensor(f"{name}_l{layer}", shape, dt))

        def sem(name):
            return new_sem(f"{name}_l{layer}")

        a = sb("scan_a", [P, HS, T])
        b = sb("scan_b", [P, HS, T])
        mine = sb("mine", [P, 2, 2, HS])
        all_ = sb("all", [P, 2 * P, HS])
        tmp = sb("tmp", [P, HS, 2 * P])
        whole = sb("whole", [P, 2, 2, HS])
        s_dve, s_mine, s_out, s_in, s_diff, s_exp, s_deg = (sem(n) for n in (
            "s_dve", "s_mine", "s_out", "s_in", "s_diff", "s_exp", "s_deg"))
        block = c.enter_context(nc.Block())

        @block.sync
        def _(sp):
            for n, h in enumerate((H, HS)):
                sp.wait_ge(s_mine, n + 1)
                src = mine[:, n, :, 0:h]
                sp.dma_start(b_dram[n].rearrange("p (c h) -> p c h", c=2), src).then_inc(s_out, 16)
                sp.wait_ge(s_out, 16 * (n + 1))
                sp.dma_start(all_[:, :, 0:h], b_dram[n].rearrange("p (c h) -> (p c) h", c=2).partition_broadcast(P))\
                    .then_inc(s_in, 16)

        @block.scalar
        def _(act):
            act.wait_ge(s_diff, 1)
            nc.scalar.activation(a[:, 0:H, :], a[:, 0:H, :], ACT.Exp, scale=scale).then_inc(s_exp, 1)
            if layer == 0:
                act.wait_ge(s_deg, 1)
                nc.scalar.activation(m["norm"][:, :], b[:, H, :], ACT.Sqrt)

        @block.vector
        def _(dve):
            link = Chain(dve, s_dve)
            tt, stt, cp = nc.vector.tensor_tensor, nc.vector.scalar_tensor_tensor, nc.vector.tensor_copy
            scan = nc.vector.tensor_tensor_scan

            def over_heads(v, h):
                return v.unsqueeze(1).to_broadcast([P, h, v.shape[-1]])

            def boundary(n, h, masks, op, combine):
                dve.wait_ge(s_in, 16 * (n + 1))
                for q in range(2):
                    link(tt(tmp[:, 0:h, :], all_[:, :, 0:h].rearrange("p k h -> p h k"), over_heads(masks[q][:, :], h),
                            combine))
                    link(nc.vector.tensor_reduce(whole[:, n, q, 0:h], tmp[:, 0:h, :], AX.X, op))

            if layer == 1:
                link(nc.vector.tensor_scalar(a[:, 0, :], att[:, 0, :], SLOPE, None, ALU.mult))
                link(tt(att[:, 0, :], att[:, 0, :], a[:, 0, :], ALU.max))
            for h in range(H):
                last = scan(a[:, h, :], m["pen_cont"][:, :], att[:, h, :], 0.0, ALU.add, ALU.max)
            link(last)
            for h in range(H):
                last = scan(b[:, h, ::-1], m["pen_more"][:, ::-1], a[:, h, ::-1], 0.0, ALU.add, ALU.max)
            link(last)
            cp(mine[:, 0, 0, 0:H], b[:, 0:H, 0])
            cp(mine[:, 0, 1, 0:H], b[:, 0:H, T - 1]).then_inc(s_mine, 1)
            boundary(0, H, m["pen_same"], ALU.max, ALU.add)
            for q, pen in enumerate((m["pen_first"], m["pen_last"])):
                for h in range(H):
                    last = stt(b[:, h, :], pen[:, :], whole[:, 0, q, h:h + 1], b[:, h, :], ALU.add, ALU.max)
                link(last)
            tt(a[:, 0:H, :], att[:, 0:H, :], b[:, 0:H, :], ALU.subtract).then_inc(s_diff, 1)
            if layer == 0:
                link(nc.vector.memset(a[:, H, :], 1.0))
            dve.wait_ge(s_exp, 1)
            for h in range(HS):
                last = scan(b[:, h, :], m["cont"][:, :], a[:, h, :], 0.0, ALU.mult, ALU.add)
            link(last)
            link(tt(b[:, 0:HS, :], b[:, 0:HS, :], over_heads(m["stops"][:, :], HS), ALU.mult))
            for h in range(HS):
                last = scan(weight[:, h, ::-1], m["more"][:, ::-1], b[:, h, ::-1], 0.0, ALU.mult, ALU.add)
            link(last)
            nc.vector.tensor_scalar(mine[:, 1, 0, 0:HS], weight[:, 0:HS, 0], m["apart"][:, 0:1], None, ALU.mult)
            cp(mine[:, 1, 1, 0:HS], weight[:, 0:HS, T - 1]).then_inc(s_mine, 1)
            boundary(1, HS, m["same"], ALU.add, ALU.mult)
            link(tt(weight[:, 0:HS, :], weight[:, 0:HS, :], over_heads(m["inside"][:, :], HS), ALU.mult))
            for q, mask in enumerate((m["in_first"], m["in_last"])):
                for h in range(HS):
                    last = stt(weight[:, h, :], mask[:, :], whole[:, 1, q, h:h + 1], weight[:, h, :], ALU.mult, ALU.add)
                link(last)
            if layer == 0:
                link(nc.vector.tensor_scalar(weight[:, H, :], weight[:, H, :], 1.0, None, ALU.max))
            link(nc.vector.reciprocal(b[:, :, :], weight[:, 0:HS, :]))
            if layer == 0:
                tt(weight[:, 0:H, :], a[:, 0:H, :], b[:, 0:H, :], ALU.mult).then_inc(s_deg, 1)
            else:
                link(tt(weight[:, 0, :], a[:, 0, :], b[:, 0, :], ALU.mult))
                tt(weight[:, 0, :], weight[:, 0, :], m["norm"][:, :], ALU.mult)


def running_sums(nc, m, link, g, before):
    rows, head = m["rows"], m["head_sum"]

    def row(j):
        return rows[:, ds(1 + G * g + j, 1), :].rearrange("p a d -> p (a d)")

    start = link.n

    def add(j):
        link(nc.vector.scalar_tensor_tensor(row(j), before if j == 0 else row(j - 1), m["cont"][:, ds(G * g + j, 1)],
                                            row(j), ALU.mult, ALU.add), wait=False)

    def head_add(j):
        link(nc.vector.scalar_tensor_tensor(head[:, :], row(j), m["head_end"][:, ds(G * g + j, 1)], head[:, :],
                                            ALU.mult, ALU.add), wait=False)
    add(0)
    for j in range(G):
        link.wait(link.n)
        if j + 1 < G:
            add(j + 1)
        head_add(j)
    link.wait(link.n)
    assert link.n == start + 2 * G


def sum_layer0(nc, m):
    rows, ident, weight, coef = m["rows"], m["ident"], m["weight"], m["coef"]
    with ExitStack() as c:
        new_sem = c.enter_context(phase_sems(nc))

        def sb(name, shape, dt=F32):
            return c.enter_context(nc.sbuf_tensor(f"{name}_s0", shape, dt))

        def sems(name, n=2):
            return [new_sem(f"{name}_s0{k}") for k in range(n)]

        xd = sb("xd", [P, 4, G, D])
        z = sb("z", [P, 2, G, D])
        x1 = sb("x1", [P, 4, G, D])
        st = sb("st", [P, 2, G, 6])
        mv = sb("mv", [P, 2, 3, G])
        sd = sb("sd", [P, 2, G])
        rstd = sb("rstd", [P, 2, G])
        shift = sb("shift", [P, 2, G])
        idx = sb("idx", [P, 4, G], I32)
        hot = sb("hot", [P, 2, G, RELS])
        hot_t = sb("hot_t", [P, 2, P])
        ps_h = c.enter_context(nc.psum_tensor("ps_h_s0", [P, 2, 512], F32))
        ps_c = c.enter_context(nc.psum_tensor("ps_c_s0", [P, 2, 512], F32))
        ps_f = c.enter_context(nc.psum_tensor("ps_f_s0", [P, 512], F32))
        zed, stats_ready, sd_ready, scale_ready, normed, hot_ready, hot_turned, hot_sb, coef_ps, coef_done = (
            sems(n) for n in ("zed", "stats_ready", "sd_ready", "scale_ready", "normed", "hot_ready",
                              "hot_turned", "hot_sb", "coef_ps", "coef_done"))
        xd_in, xd_used, sent = sems("xd_in", 4), sems("xd_used", 4), sems("sent", 4)
        s_chain, s_idx, s_tail, s_carried, s_fix = (sems(n, 1)[0] for n in (
            "chain", "idx_ready", "tail", "carried", "fix"))
        block = c.enter_context(nc.Block())
        SUMS = 1 + 2 * G
        PER = SUMS + 4

        @block.sync
        def _(sp):
            def load(t):
                s4, u4 = t.slot(4), t.uses(4)
                sp.wait_ge(xd_used[s4], u4)
                sp.dma_start(xd[:, s4, :, :], m["xd_kept"][0][:, ds(G * t.g, G), :]).then_inc(xd_in[s4], 16)
            in_turns(sp, load)
            f4, n4 = FIX_TURN.slot(4), FIX_TURN.uses(4)
            sp.wait_ge(xd_used[f4], n4)
            sp.dma_start(xd[:, f4, 0, :], m["xd_kept"][0][:, 0, :]).then_inc(xd_in[f4], 16)

        @block.vector
        def _(dve):
            def begin(t, link, link_z, row, n):
                s, u, s4, u4 = t.slot(), t.uses(), t.slot(4), t.uses(4)
                dve.wait_ge(xd_in[s4], 16 * (u4 + 1))
                dve.wait_ge(normed[s], u)
                zz = z[:, s, 0:n, :]
                nc.vector.scalar_tensor_tensor(zz, row, 0.0, xd[:, s4, 0:n, :], ALU.max, ALU.add)\
                    .then_inc(xd_used[s4], 1)
                dve.wait_ge(xd_used[s4], u4 + 1)
                row_stats(nc, link, st[:, s, :, :], mv[:, s, :, :], P, z[:, s, :, :], n).then_inc(stats_ready[s], 1)

            def end(t, link, n):
                s, u = t.slot(), t.uses()
                dve.wait_ge(sd_ready[s], u + 1)
                link(nc.vector.reciprocal(rstd[:, s, 0:n], sd[:, s, 0:n]))
                nc.vector.scalar_tensor_tensor(shift[:, s, 0:n], mv[:, s, 2, 0:n], -0.5, rstd[:, s, 0:n],
                                               ALU.mult, ALU.mult).then_inc(scale_ready[s], 1)

            def body(t):
                s, u, g = t.slot(), t.uses(), t.g
                link = LoopChain(dve, s_chain, PER, g)
                wv = rows[:, ds(1 + G * g, G), :].rearrange("p j (h d) -> p j h d", h=HEADS)
                link(nc.vector.tensor_tensor(
                    wv, wv, weight[:, 0:HEADS, ds(G * g, G)].rearrange("p h j -> p j h").unsqueeze(3)
                    .to_broadcast([P, G, HEADS, DK]), ALU.mult))
                running_sums(nc, m, link, g, rows[:, ds(G * g, 1), :].rearrange("p a d -> p (a d)"))
                begin(t, link, link, rows[:, ds(1 + G * g, G), :], G)
                dve.wait_ge(hot_turned[s], u)
                nc.vector.tensor_tensor(hot[:, s, :, :], m["iota_rel"][:, :].unsqueeze(1).to_broadcast([P, G, RELS]),
                                        m["rel_f"][:, ds(G * g, G)].unsqueeze(2).to_broadcast([P, G, RELS]),
                                        ALU.is_equal).then_inc(hot_ready[s], 1)
                end(t, link, G)
                dve.wait_ge(coef_ps[s], u + 1)
                nc.vector.tensor_scalar(coef[:, ds(G * g, G), :], ps_c[:, s, 0:G * BASES]
                                        .rearrange("p (j b) -> p j b", j=G), 1.0, None, ALU.mult)\
                    .then_inc(coef_done[s], 1)
                link.end()
            in_turns(dve, body)
            dve.wait_ge(s_carried, 1)
            link = Chain(dve, s_tail)
            link(nc.vector.tensor_tensor(rows[:, FIX, :], ps_f[:, 0:D], m["head_sum"][:, :], ALU.add))
            begin(FIX_TURN, link, link, rows[:, FIX:FIX + 1, :], 1)
            end(FIX_TURN, link, 1)
            nc.vector.memset(m["head_sum"][:, :], 0.0)

        @block.tensor
        def _(pe):
            def body(t):
                s, u = t.slot(), t.uses()
                pe.wait_ge(hot_ready[s], u + 1)
                pe.wait_ge(hot_sb[s], u)
                nc.tensor.transpose(ps_h[:, s, 0:P], hot[:, s, :, :].rearrange("p j r -> p (j r)"), ident[:, :])\
                    .then_inc(hot_turned[s], 1)
                pe.wait_ge(hot_sb[s], u + 1)
                pe.wait_ge(coef_done[s], u)
                nc.tensor.matmul(ps_c[:, s, 0:G * BASES], hot_t[:, s, :], m["coef_blocks"][:, :], start=True,
                                 stop=True).then_inc(coef_ps[s], 1)
            in_turns(pe, body)
            pe.wait_ge(s_chain, PER * (NG - 1) + SUMS)
            nc.tensor.matmul(ps_f[:, 0:D], m["carried_by"][:, :], rows[:, T, :], start=True, stop=True)\
                .then_inc(s_carried, 1)

        @block.scalar
        def _(act):
            def normalise(t, n):
                s, u, s4, u4 = t.slot(), t.uses(), t.slot(4), t.uses(4)
                act.wait_ge(scale_ready[s], u + 1)
                act.wait_ge(sent[s4], 16 * G * u4)
                for j in range(n):
                    last = nc.scalar.activation(x1[:, s4, j, :], z[:, s, j, :], ACT.Identity,
                                                bias=shift[:, s, j:j + 1], scale=rstd[:, s, j:j + 1])
                last.then_inc(normed[s], 1)

            def deviation(t, n):
                s, u = t.slot(), t.uses()
                act.wait_ge(stats_ready[s], u + 1)
                nc.scalar.activation(sd[:, s, 0:n], mv[:, s, 1, 0:n], ACT.Sqrt, bias=m["eps_col"][:, :],
                                     scale=1.0 / D).then_inc(sd_ready[s], 1)

            def body(t):
                s, u = t.slot(), t.uses()
                deviation(t, G)
                act.wait_ge(hot_turned[s], u + 1)
                act.wait_ge(coef_ps[s], u)
                nc.scalar.activation(hot_t[:, s, :], ps_h[:, s, 0:P], ACT.Copy).then_inc(hot_sb[s], 1)
                normalise(t, G)
            in_turns(act, body)
            deviation(FIX_TURN, 1)
            normalise(FIX_TURN, 1)

        @block.gpsimd
        def _(pool):
            def scatter(t, col, n):
                s, u, s4, u4 = t.slot(), t.uses(), t.slot(4), t.uses(4)
                pool.wait_ge(sent[s4], 16 * G * u4)
                carry_wait(nc, m)
                nc.gpsimd.tensor_copy(idx[:, s4, 0:n], m["scatter_idx"][:, ds(col, n)]).then_inc(s_idx, 1)
                pool.wait_ge(s_idx, t.g + 1)
                pool.wait_ge(normed[s], u + 1)
                carry_wait(nc, m, 1)
                for j in range(n):
                    nc.gpsimd.indirect_dma_start(
                        out=m["x1_table"][:, :],
                        out_offset=bass.IndirectOffsetOnAxis(ap=idx[:, s4, j:j + 1], axis=0),
                        in_=x1[:, s4, j, :], in_offset=None, bounds_check=NODES - 1, oob_is_err=False,
                    ).then_inc(sent[s4], 16)
            in_turns(pool, lambda t: scatter(t, G * t.g, G))
            scatter(FIX_TURN, T, 1)
            for s in range(4):
                groups, fix = len(range(s, NG, 4)), s == FIX_TURN.slot(4)
                pool.wait_ge(sent[s], 16 * (G * groups + fix))


def messages(nc, m):
    rows, ident, att, gather_idx, coef = m["rows"], m["ident"], m["att"], m["gather_idx"], m["coef"]
    with ExitStack() as c:
        new_sem = c.enter_context(phase_sems(nc))

        def sb(name, shape, dt=F32):
            return c.enter_context(nc.sbuf_tensor(f"{name}_m", shape, dt))

        def sems(name, n=2):
            return [new_sem(f"{name}_m{k}") for k in range(n)]

        def ps(name, shape):
            return c.enter_context(nc.psum_tensor(f"{name}_m", shape, F32))

        idx = sb("idx", [P, 2, 2 * G], I32)
        ends = sb("gathered", [P, 2, 2, G, D])
        ends_t = sb("gathered_t", [P, 2, 2, G * P])
        hot = sb("hot", [P, 2, G, RELS])
        sel = sb("sel", [P, 2, G, RELS])
        even = sb("even", [P, 2, D])
        odd = sb("odd", [P, 2, D])
        coef_g = sb("coef_g", [P, 2, G, BASES])
        xg = sb("xg", [P, 2, CH, D + 1])
        zeros = sb("zeros", [P, P])
        ps_t = ps("ps_t", [P, 2, G * P])
        ps_p = ps("ps_p", [P, 2, 2, BASES // 2, D])
        ps_s = ps("ps_s", [P, G, RELS])
        ps_g = ps("ps_g", [P, 512])
        fetched, saved, turned, turned_sb, scored, score_done, x_in, grammed, coef_ready, begun, row_done = (
            sems(n) for n in ("fetched", "saved", "turned", "turned_sb", "scored", "score_done", "x_in", "grammed",
                              "coef_ready", "begun", "row_done"))
        based = [sems(f"based{h}_") for h in range(2)]
        p_free = [sems(f"p_free{h}_") for h in range(2)]
        idx_ready, s_chain, s_set, s_gram = (sems(n, 1)[0] for n in ("idx_ready", "chain", "set", "gram"))
        block = c.enter_context(nc.Block())
        PER = 2 + G * 4

        @block.gpsimd
        def _(pool):
            def gather(t):
                s, u = t.slot(), t.uses()
                pool.wait_ge(fetched[s], 128 * u)
                pool.wait_ge(turned[s], u)
                pool.wait_ge(saved[s], 16 * u)
                nc.gpsimd.tensor_copy(idx[:, s, :], gather_idx[:, ds(t.g, 1), :].rearrange("p a j -> p (a j)"))\
                    .then_inc(idx_ready, 1)
                pool.wait_ge(idx_ready, t.g + 1)
                carry_wait(nc, m)
                for e in range(2):
                    for j in range(G):
                        nc.gpsimd.indirect_dma_start(
                            out=ends[:, s, e, j, :], out_offset=None, in_=m["x1_table"][:, :],
                            in_offset=bass.IndirectOffsetOnAxis(ap=idx[:, s, e * G + j:e * G + j + 1], axis=0),
                        ).then_inc(fetched[s], 16)
            in_turns(pool, gather)

        @block.sync
        def _(sp):
            def move(t):
                s, u = t.slot(), t.uses()
                sp.wait_ge(grammed[s], u)
                sp.dma_start(xg[0:t.np, s, :, 0:D], m["x1_table"][ds(t.g * CHUNK, t.np * CH), :]
                             .rearrange("(p j) d -> p j d", j=CH)).then_inc(x_in[s], 16)
                sp.wait_ge(fetched[s], 128 * (u + 1))
                sp.dma_start(m["xd_kept"][1][:, ds(G * t.g, G), :], ends[:, s, 1, :, :]).then_inc(saved[s], 16)
            in_turns(sp, move)
            for s in range(2):
                sp.wait_ge(saved[s], 16 * FIX_TURN_USES[s])

        @block.tensor
        def _(pe):
            mm = nc.tensor.matmul

            def turn_rows(t):
                s, u = t.slot(), t.uses()
                pe.wait_ge(fetched[s], 128 * (u + 1))
                pe.wait_ge(turned_sb[1 - s], t.uses() + s)
                for e in range(2):
                    for j in range(G):
                        last = nc.tensor.transpose(ps_t[:, e, j * P:(j + 1) * P], ends[:, s, e, j, :], ident[:, :])
                last.then_inc(turned[s], 1)

            def body(t):
                s, u, np = t.slot(), t.uses(), t.np
                pe.wait_ge(turned_sb[s], u + 1)
                pe.wait_ge(score_done[1 - s], t.uses() + s)
                for j in range(G):
                    s_t = ends_t[:, s, 0, j * P:(j + 1) * P]
                    d_t = ends_t[:, s, 1, j * P:(j + 1) * P]
                    mm(ps_s[:, j, :], s_t, m["a_sb"][:, :], start=True, stop=False)
                    last = mm(ps_s[:, j, :], d_t, m["a_sb"][:, :], start=False, stop=True)
                last.then_inc(scored[s], 1)
                for j in range(G):
                    if j == G // 2:
                        if t.next():
                            turn_rows(t.next())
                    s_t = ends_t[:, s, 0, j * P:(j + 1) * P]
                    for half in range(2):
                        pe.wait_ge(p_free[half][j % 2], t.g * (G // 2) + j // 2)
                        last = mm(ps_p[:, j % 2, half, :, :], s_t, m["bases_sb"][:, half * 512:(half + 1) * 512],
                                  start=True, stop=True)
                        last.then_inc(based[half][j % 2], 1)
                pe.wait_ge(x_in[s], 16 * (u + 1))
                for j in range(CH):
                    last = mm(ps_g[:, 0:D + 1], xg[0:np, s, j, 0:D], xg[0:np, s, j, :], start=False,
                              stop=False, skip_group_check=True)
                last.then_inc(grammed[s], 1)

            pe.wait_ge(s_set, 1)
            mm(ps_g[:, 0:D + 1], zeros[:, :], zeros[:, 0:1].to_broadcast([P, D + 1]), start=True, stop=False,
               skip_group_check=True)
            turn_rows(Turn(0, 0))
            in_turns(pe, body)
            mm(ps_g[:, 0:D + 1], zeros[:, :], zeros[:, 0:1].to_broadcast([P, D + 1]), start=False, stop=True,
               skip_group_check=True).then_inc(s_gram, 1)

        def coefs(t, j, b):
            return coef_g[:, t.slot(), j, b:b + 1]

        def row_of(g, j):
            return rows[:, ds(1 + G * g + j, 1), :].rearrange("p a d -> p (a d)")

        @block.scalar
        def _(act):
            def turned_out(t):
                s, u = t.slot(), t.uses()
                act.wait_ge(turned[s], u + 1)
                act.wait_ge(grammed[s], u)
                nc.scalar.activation(ends_t[:, s, 0, :], ps_t[:, 0, :], ACT.Copy)
                nc.scalar.activation(ends_t[:, s, 1, :], ps_t[:, 1, :], ACT.Copy).then_inc(turned_sb[s], 1)

            def body(t):
                act.wait_ge(coef_ready[t.slot()], t.uses() + 1)
                for j in range(G):
                    if j == G // 2 and t.next():
                        turned_out(t.next())
                    n = t.g * (G // 2) + j // 2
                    act.wait_ge(based[0][j % 2], n + 1)
                    act.wait_ge(row_done[j % 2], n)
                    nc.scalar.activation(even[:, j % 2, :], ps_p[:, j % 2, 0, 0, :], ACT.Copy, scale=coefs(t, j, 0))
                    nc.scalar.activation(odd[:, j % 2, :], ps_p[:, j % 2, 0, 1, :], ACT.Copy,
                                         scale=coefs(t, j, 1)).then_inc(begun[j % 2], 1)
            turned_out(Turn(0, 0))
            in_turns(act, body)

        @block.vector
        def _(dve):
            nc.vector.memset(zeros[:, :], 0.0)
            nc.vector.memset(xg[:, 0, :, D:D + 1], 1.0)
            nc.vector.memset(xg[:, 1, :, D:D + 1], 1.0).then_inc(s_set, 1)

            def copy_coefs(t):
                nc.vector.tensor_scalar(coef_g[:, t.slot(), :, :], coef[:, ds(G * t.g, G), :], 1.0, None, ALU.mult)\
                    .then_inc(coef_ready[t.slot()], 1)

            def body(t):
                s, u, g = t.slot(), t.uses(), t.g
                link = LoopChain(dve, s_chain, PER, g)
                dve.wait_ge(coef_ready[s], u + 1)
                link(nc.vector.tensor_tensor(hot[:, s, :, :],
                                             m["iota_rel"][:, :].unsqueeze(1).to_broadcast([P, G, RELS]),
                                             m["rel_f"][:, ds(G * g, G)].unsqueeze(2).to_broadcast([P, G, RELS]),
                                             ALU.is_equal))
                dve.wait_ge(scored[s], u + 1)
                link(nc.vector.tensor_tensor(sel[:, s, :, :], ps_s[:, :, :], hot[:, s, :, :], ALU.mult))
                nc.vector.tensor_reduce(att[:, 0, ds(G * g, G)], sel[:, s, :, :], AX.X, ALU.add)\
                    .then_inc(score_done[s], 1)
                for j in range(G):
                    if j == G // 2 and t.next():
                        copy_coefs(t.next())
                    n = g * (G // 2) + j // 2
                    sums = (even[:, j % 2, :], odd[:, j % 2, :])

                    def add(b):
                        return nc.vector.scalar_tensor_tensor(
                            sums[b % 2], ps_p[:, j % 2, b // 4, b % 4, :], coefs(t, j, b), sums[b % 2],
                            ALU.mult, ALU.add)
                    dve.wait_ge(begun[j % 2], n + 1)
                    link(add(2), wait=False)
                    add(3).then_inc(p_free[0][j % 2], 1)
                    dve.wait_ge(based[1][j % 2], n + 1)
                    link.wait(link.n)
                    link(add(4), wait=False)
                    dve.wait_ge(p_free[0][j % 2], n + 1)
                    link(add(5), wait=False)
                    link.wait(link.n - 1)
                    link(add(6), wait=False)
                    link.wait(link.n - 1)
                    add(7).then_inc(p_free[1][j % 2], 1)
                    dve.wait_ge(p_free[1][j % 2], n + 1)
                    nc.vector.tensor_tensor(row_of(g, j), sums[0], sums[1], ALU.add).then_inc(row_done[j % 2], 1)
                link.end()
            copy_coefs(Turn(0, 0))
            in_turns(dve, body)
            dve.wait_ge(s_gram, 1)
            nc.vector.tensor_copy(m["gram_sb"][:, :], ps_g[:, 0:D + 1])


def centre(nc, m):
    with ExitStack() as c:
        new_sem = c.enter_context(phase_sems(nc))

        def sb(name, shape, dt=F32):
            return c.enter_context(nc.sbuf_tensor(f"{name}_c", shape, dt))

        def sem(name):
            return new_sem(f"{name}_c")

        mean_col = sb("mean_col", [D, 1])
        mean_row = sb("mean_row", [1, D])
        gram_n = sb("gram_n", [D, D])
        cov = sb("cov", [D, D])
        cw = sb("cw", [D, D])
        mu = sb("mu", [3, D])
        ps = c.enter_context(nc.psum_tensor("ps_c", [P, 4, 512], F32))
        s_dve, s_mean, s_row, s_row_sb, s_outer, s_cov, s_cw, s_cw_sb, s_var = (sem(n) for n in (
            "s_dve", "s_mean", "s_row", "s_row_sb", "s_outer", "s_cov", "s_cw", "s_cw_sb", "s_var"))
        block = c.enter_context(nc.Block())

        @block.vector
        def _(dve):
            link = Chain(dve, s_dve)
            ts, tt = nc.vector.tensor_scalar, nc.vector.tensor_tensor
            ts(mean_col[:, :], m["gram_sb"][:, D:D + 1], 1.0 / NODES, None, ALU.mult).then_inc(s_mean, 1)
            link(ts(gram_n[:, :], m["gram_sb"][:, 0:D], 1.0 / NODES, None, ALU.mult))
            dve.wait_ge(s_row, 1)
            nc.vector.tensor_copy(mean_row[:, :], ps[0:1, 0, 0:D]).then_inc(s_row_sb, 1)
            link(tt(mu[:, :], ps[0:3, 1, 0:D], m["vec_rows"][:, 0, :], ALU.add))
            dve.wait_ge(s_outer, 1)
            tt(cov[:, :], gram_n[:, :], ps[:, 2, 0:D], ALU.subtract).then_inc(s_cov, 1)
            link(tt(m["centre_row"][:, :], m["vec_rows"][:, 0, :], mu[:, :], ALU.subtract))
            split3(nc, m, link, m["centre_parts"][:, :], m["centre_row"][:, :], (m["split_f"], m["split_b"]))
            dve.wait_ge(s_cw, 1)
            tt(cw[:, :], ps[:, 3, 0:D], m["wloop_sb"][:, :], ALU.mult).then_inc(s_cw_sb, 1)
            dve.wait_ge(s_var, 1)
            nc.vector.tensor_copy(m["var_row"][:, :], ps[0:3, 0, 256:256 + D])

        @block.tensor
        def _(pe):
            mm = nc.tensor.matmul
            pe.wait_ge(s_mean, 1)
            nc.tensor.transpose(ps[0:1, 0, 0:D], mean_col[:, :], m["ident"][:, :])
            mm(ps[0:3, 1, 0:D], mean_col[:, :].to_broadcast([D, 3]), m["wloop_sb"][:, :], start=True, stop=True)\
                .then_inc(s_row, 1)
            pe.wait_ge(s_row_sb, 1)
            mm(ps[:, 2, 0:D], mean_row[:, :], mean_row[:, :], start=True, stop=True).then_inc(s_outer, 1)
            pe.wait_ge(s_cov, 1)
            mm(ps[:, 3, 0:D], cov[:, :], m["wloop_sb"][:, :], start=True, stop=True).then_inc(s_cw, 1)
            pe.wait_ge(s_cw_sb, 1)
            mm(ps[0:3, 0, 256:256 + D], m["ones_col"][:, :].to_broadcast([P, 3]), cw[:, :], start=True, stop=True)\
                .then_inc(s_var, 1)


def sum_layer1(nc, m):
    rows, ident, weight = m["rows"], m["ident"], m["weight"]
    with ExitStack() as c:
        new_sem = c.enter_context(phase_sems(nc))

        def sb(name, shape, dt=F32):
            return c.enter_context(nc.sbuf_tensor(f"{name}_s1", shape, dt))

        def sems(name, n=2):
            return [new_sem(f"{name}_s1{k}") for k in range(n)]

        def ps(name, shape):
            return c.enter_context(nc.psum_tensor(f"{name}_s1", shape, F32))

        xd = sb("xd", [P, 4, G, D])
        xd_t = sb("xd_t", [P, 2, G * P])
        carry = sb("carry", [P, 2, D])
        both = sb("both", [P, 2, G, 2, D])
        twice = sb("twice", [P, 2, G, D])
        mask = sb("mask", [P, 2, G, 3])
        ps_t = ps("ps_t", [P, 2, G * P])
        ps_u = ps("ps_u", [P, 2, G, D])
        ps_sum = ps("ps_sum", [P, 512])
        ps_f = ps("ps_f", [P, 512])
        turned, turned_sb, lin, masked, weighed, ready, summed = (
            sems(n) for n in ("turned", "turned_sb", "lin", "masked", "weighed", "ready", "summed"))
        xd_in, xd_used = sems("xd_in", 4), sems("xd_used", 4)
        s_chain, s_set, s_copied, s_carried, s_tail, s_all = (sems(n, 1)[0] for n in (
            "chain", "set", "copied", "carried", "tail", "all"))
        block = c.enter_context(nc.Block())
        SUMS = 2 * G
        PER = SUMS + 2
        f2, f4 = FIX_TURN.slot(), FIX_TURN.slot(4)

        @block.sync
        def _(sp):
            def load(t):
                s4, u4 = t.slot(4), t.uses(4)
                sp.wait_ge(xd_used[s4], u4)
                sp.dma_start(xd[:, s4, :, :], m["xd_kept"][1][:, ds(G * t.g, G), :]).then_inc(xd_in[s4], 16)
            in_turns(sp, load)
            sp.wait_ge(xd_used[f4], FIX_TURN.uses(4))
            sp.dma_start(xd[:, f4, 0, :], m["xd_kept"][1][:, 0, :]).then_inc(xd_in[f4], 16)

        @block.tensor
        def _(pe):
            mm = nc.tensor.matmul

            def turn_rows(t, n=G):
                s, u, s4, u4 = t.slot(), t.uses(), t.slot(4), t.uses(4)
                pe.wait_ge(xd_in[s4], 16 * (u4 + 1))
                pe.wait_ge(turned_sb[s], u)
                for j in range(n):
                    last = nc.tensor.transpose(ps_t[:, s, j * P:(j + 1) * P], xd[:, s4, j, :], ident[:, :])
                last.then_inc(xd_used[s4], 1)

            def linear(t, n=G):
                s, u = t.slot(), t.uses()
                pe.wait_ge(turned_sb[s], u + 1)
                pe.wait_ge(ready[s], u)
                mm(ps_u[:, s, :, :], m["ones3"][:, :], m["centre_parts"][:, :].unsqueeze(1).to_broadcast([3, G, D]),
                   start=True, stop=False, skip_group_check=True)
                for j in range(n):
                    last = mm(ps_u[:, s, j, :], xd_t[:, s, j * P:(j + 1) * P], m["wloop_sb"][:, :], start=False,
                              stop=True, skip_group_check=True)
                last.then_inc(lin[s], 1)

            def total(t, n=G):
                s, u = t.slot(), t.uses()
                pe.wait_ge(ready[s], u + 1)
                for j in range(n):
                    last = mm(ps_sum[0:3, 0:2 * D], mask[:, s, j, :],
                              both[:, s, j, :, :].rearrange("p a d -> p (a d)"), start=False, stop=False,
                              skip_group_check=True)
                last.then_inc(summed[s], 1)

            def body(t):
                if t.next():
                    turn_rows(t.next())
                    linear(t.next())
                total(t)

            def zeros(start, stop):
                return mm(ps_sum[0:3, 0:2 * D], rows[:, 0, 0:3], rows[:, 0, 0:1].to_broadcast([P, 2 * D]),
                          start=start, stop=stop, skip_group_check=True)
            zeros(True, False)
            turn_rows(Turn(0, 0))
            linear(Turn(0, 0))
            in_turns(pe, body)
            turn_rows(FIX_TURN, 1)
            linear(FIX_TURN, 1)
            pe.wait_ge(s_chain, PER * (NG - 1) + SUMS + 1)
            mm(ps_f[:, 0:D], m["carried_by"][:, :], carry[:, 1, :], start=True, stop=True).then_inc(s_carried, 1)
            total(FIX_TURN, 1)
            zeros(False, True).then_inc(s_all, 1)

        @block.scalar
        def _(act):
            def weigh(t):
                for j in range(G):
                    row = rows[:, ds(1 + G * t.g + j, 1), :].rearrange("p a d -> p (a d)")
                    last = nc.scalar.activation(row, row, ACT.Copy, scale=weight[:, 0, ds(G * t.g + j, 1)])
                last.then_inc(weighed[t.slot()], 1)

            def turned_out(t, n=G):
                s, u, s4, u4 = t.slot(), t.uses(), t.slot(4), t.uses(4)
                act.wait_ge(xd_used[s4], u4 + 1)
                act.wait_ge(lin[s], u)
                nc.scalar.activation(xd_t[:, s, 0:n * P], ps_t[:, s, 0:n * P], ACT.Copy).then_inc(turned_sb[s], 1)

            def body(t):
                s, u = t.slot(), t.uses()
                if t.next():
                    turned_out(t.next())
                    weigh(t.next())
                act.wait_ge(masked[s], u + 1)
                nc.scalar.activation(m["scrap"][:, 1:2], m["eps_col"][:, :], ACT.Copy)
                nc.scalar.activation(both[:, s, :, 1, :], rows[:, ds(1 + G * t.g, G), :], ACT.Copy).then_inc(s_copied, 1)
            turned_out(Turn(0, 0))
            weigh(Turn(0, 0))
            in_turns(act, body)
            turned_out(FIX_TURN, 1)

        @block.vector
        def _(dve):
            nc.vector.memset(carry[:, 0, :], 0.0).then_inc(s_set, 1)
            dve.wait_ge(s_set, 1)

            def body(t):
                s, u, g = t.slot(), t.uses(), t.g
                link = LoopChain(dve, s_chain, PER, g)
                mine = rows[:, ds(1 + G * g, G), :]
                dve.wait_ge(weighed[s], u + 1)
                running_sums(nc, m, link, g, carry[:, s, :])
                link(nc.vector.tensor_scalar(carry[:, 1 - s, :], rows[:, ds(G * g + G, 1), :]
                                             .rearrange("p a d -> p (a d)"), 1.0, None, ALU.mult), wait=False)
                dve.wait_ge(summed[s], u)
                nc.vector.tensor_scalar(mask[:, s, :, :], m["valid"][:, ds(G * g, G)].unsqueeze(2)
                                        .to_broadcast([P, G, 3]), 1.0, None, ALU.mult).then_inc(masked[s], 1)
                dve.wait_ge(lin[s], u + 1)
                link(nc.vector.scalar_tensor_tensor(twice[:, s, :, :], ps_u[:, s, :, :], 2.0, mine,
                                                    ALU.mult, ALU.add))
                nc.vector.tensor_tensor(both[:, s, :, 0, :], twice[:, s, :, :], mine, ALU.mult)
                dve.wait_ge(s_copied, g + 1)
                nc.vector.tensor_tensor(mine, ps_u[:, s, :, :], mine, ALU.add).then_inc(ready[s], 1)
                link.end()
            in_turns(dve, body)
            link = Chain(dve, s_tail)
            dve.wait_ge(s_carried, 1)
            fix = rows[:, FIX, :]
            dve.wait_ge(summed[f2], FIX_TURN.uses())
            nc.vector.tensor_copy(mask[:, f2, 0, :], m["valid"][:, T:T + 1].to_broadcast([P, 3]))
            link(nc.vector.tensor_tensor(fix, ps_f[:, 0:D], m["head_sum"][:, :], ALU.add))
            dve.wait_ge(lin[f2], FIX_TURN.uses() + 1)
            nc.vector.tensor_copy(both[:, f2, 0, 1, :], fix)
            link(nc.vector.scalar_tensor_tensor(twice[:, f2, 0, :], ps_u[:, f2, 0, :], 2.0, fix, ALU.mult, ALU.add))
            link(nc.vector.tensor_tensor(both[:, f2, 0, 0, :], twice[:, f2, 0, :], fix, ALU.mult))
            nc.vector.tensor_tensor(fix, ps_u[:, f2, 0, :], fix, ALU.add).then_inc(ready[f2], 1)
            dve.wait_ge(s_all, 1)
            nc.vector.tensor_copy(m["sums_row"][:, :], ps_sum[0:3, 0:2 * D])


def output(nc, m):
    rows, ident = m["rows"], m["ident"]
    POOL_ROWS = 3
    with ExitStack() as c:
        new_sem = c.enter_context(phase_sems(nc))

        def sb(name, shape, dt=F32):
            return c.enter_context(nc.sbuf_tensor(f"{name}_o", shape, dt))

        def sems(name, n=2):
            return [new_sem(f"{name}_o{k}") for k in range(n)]

        def ps(name, shape):
            return c.enter_context(nc.psum_tensor(f"{name}_o", shape, F32))

        ab_row = sb("ab_row", [3, 2, D])
        base_row = sb("base_row", [3, D])
        base_parts = sb("base_parts", [3, D], BF16)
        r = sb("r", [3, 6, D])
        ab = sb("ab", [P, 2, D])
        w_scaled = sb("w_scaled", [D, D])
        x1 = sb("x1", [P, 4, CH, D])
        x1_t = sb("x1_t", [P, 2, CH * P])
        z = sb("z", [P, 2, CH, D])
        y = sb("y", [P, 2, CH, D])
        st = sb("st", [P, 2, CH, 6])
        mv = sb("mv", [P, 2, 3, CH])
        sd = sb("sd", [P, 2, CH])
        rstd = sb("rstd", [P, 2, CH])
        shift = sb("shift", [P, 2, CH])
        idx = sb("idx", [P, 2, G], I32)
        ps_t = ps("ps_t", [P, 2, G * P])
        ps_u = ps("ps_u", [P, 2, CH, D])
        ps_ab = ps("ps_ab", [P, 512])
        turned, turned_sb, lin, zed, sd_ready, scale_ready, normed, pooled, x_out = (
            sems(n) for n in ("turned", "turned_sb", "lin", "zed", "sd_ready", "scale_ready", "normed", "pooled",
                              "x_out"))
        e_zed, e_sd, e_scale, e_normed, e_sent = (
            sems(n) for n in ("e_zed", "e_sd", "e_scale", "e_normed", "e_sent"))
        x_in, x_used, e_in, e_used = sems("x_in", 4), sems("x_used", 4), sems("e_in", 4), sems("e_used", 4)
        s_chain, s_echain, s_rows, s_sqrt, s_sqrt_done, s_ab, s_bc, s_ready, s_idx, s_tail = (
            sems(n, 1)[0] for n in ("chain", "echain", "rows", "sqrt", "sqrt_done", "ab", "bc", "ready",
                                    "idx_ready", "tail"))
        block = c.enter_context(nc.Block())
        f2, f4 = FIX_TURN.slot(), FIX_TURN.slot(4)

        @block.sync
        def _(sp):
            def load(t):
                s4, u4 = t.slot(4), t.uses(4)
                sp.wait_ge(x_used[s4], u4)
                sp.dma_start(x1[0:t.np, s4, :, :], m["x1_table"][ds(t.g * CHUNK, t.np * CH), :]
                             .rearrange("(p j) d -> p j d", j=CH)).then_inc(x_in[s4], 16)
            in_turns(sp, load)
            for s in range(4):
                sp.wait_ge(x_used[s], len(range(s, NG, 4)))

            def load_edges(t):
                s4, u4 = t.slot(4), t.uses(4)
                sp.wait_ge(e_used[s4], u4)
                sp.dma_start(x1[:, s4, 0:G, :], m["xd_kept"][1][:, ds(G * t.g, G), :]).then_inc(e_in[s4], 16)
            in_turns(sp, load_edges)
            sp.wait_ge(e_used[f4], FIX_TURN.uses(4))
            sp.dma_start(x1[:, f4, 0, :], m["xd_kept"][1][:, 0, :]).then_inc(e_in[f4], 16)

        @block.tensor
        def _(pe):
            mm = nc.tensor.matmul

            def turn_rows(t):
                s, u, s4, u4 = t.slot(), t.uses(), t.slot(4), t.uses(4)
                pe.wait_ge(x_in[s4], 16 * (u4 + 1))
                for h in range(2):
                    pe.wait_ge(turned_sb[h], t.g)
                    for j in range(G):
                        last = nc.tensor.transpose(ps_t[:, h, j * P:(j + 1) * P], x1[:, s4, h * G + j, :], ident[:, :])
                    last.then_inc(turned[h], 1)

            def body(t):
                s, u = t.slot(), t.uses()
                if t.next():
                    turn_rows(t.next())
                pe.wait_ge(zed[s], u)
                for h in range(2):
                    pe.wait_ge(turned_sb[h], t.g + 1)
                    mm(ps_u[:, s, h * G:(h + 1) * G, :], m["ones3"][:, :],
                       base_parts[:, :].unsqueeze(1).to_broadcast([3, G, D]), start=True, stop=False,
                       skip_group_check=True)
                    for j in range(h * G, (h + 1) * G):
                        last = mm(ps_u[:, s, j, :], x1_t[:, s, j * P:(j + 1) * P], w_scaled[:, :], start=False,
                                  stop=True, skip_group_check=True)
                last.then_inc(lin[s], 1)

            pe.wait_ge(s_ab, 1)
            mm(ps_ab[:, 0:2 * D], m["ones_row"][:, :], ab_row[0:1, :, :].rearrange("p a d -> p (a d)"),
               start=True, stop=True).then_inc(s_bc, 1)
            turn_rows(Turn(0, 0))
            pe.wait_ge(s_ready, 1)
            in_turns(pe, body)

        @block.scalar
        def _(act):
            def turned_out(t):
                s, u = t.slot(), t.uses()
                act.wait_ge(lin[s], u)
                for h in range(2):
                    act.wait_ge(turned[h], t.g + 1)
                    nc.scalar.activation(x1_t[:, s, h * G * P:(h + 1) * G * P], ps_t[:, h, :], ACT.Copy)\
                        .then_inc(turned_sb[h], 1)

            def deviation(t, np, n, zed, sd_ready):
                s, u = t.slot(), t.uses()
                act.wait_ge(zed[s], u + 1)
                nc.scalar.activation(sd[0:np, s, 0:n], mv[0:np, s, 1, 0:n], ACT.Sqrt, bias=m["eps_col"][0:np, :],
                                     scale=1.0 / D).then_inc(sd_ready[s], 1)

            def normalise(t, np, n, scale_ready, normed):
                s, u = t.slot(), t.uses()
                act.wait_ge(scale_ready[s], u + 1)
                for j in range(n):
                    last = nc.scalar.activation(y[0:np, s, j, :], z[0:np, s, j, :], ACT.Identity,
                                                bias=shift[0:np, s, j:j + 1], scale=rstd[0:np, s, j:j + 1])
                last.then_inc(normed[s], 1)

            def store(t):
                s, u, np = t.slot(), t.uses(), t.np
                act.wait_ge(normed[s], u + 1)
                act.wait_ge(pooled[s], u + 1)
                act.dma_start(m["out"][ds(t.g * CHUNK, np * CH), :].rearrange("(p j) d -> p j d", j=CH),
                              y[0:np, s, :, :]).then_inc(x_out[s], 16)

            def nodes(t):
                s, u = t.slot(), t.uses()
                if t.next():
                    turned_out(t.next())
                deviation(t, P, CH, zed, sd_ready)
                act.wait_ge(x_out[s], 16 * u)
                normalise(t, P, CH - POOL_ROWS, scale_ready, normed)
                store(t)

            act.wait_ge(s_sqrt, 1)
            nc.scalar.activation(r[:, 3, :], r[:, 2, :], ACT.Sqrt).then_inc(s_sqrt_done, 1)
            turned_out(Turn(0, 0))
            in_turns(act, nodes)
            for s in range(2):
                act.wait_ge(x_out[s], 16 * FIX_TURN_USES[s])

            def edges(t, n=G):
                s, u = t.slot(), t.uses()
                deviation(t, P, n, e_zed, e_sd)
                act.wait_ge(e_sent[s], 16 * G * u)
                normalise(t, P, n, e_scale, e_normed)
            in_turns(act, edges)
            edges(FIX_TURN, 1)

        @block.vector
        def _(dve):
            link = Chain(dve, s_rows)
            ts, tt, stt = nc.vector.tensor_scalar, nc.vector.tensor_tensor, nc.vector.scalar_tensor_tensor
            link(ts(r[:, 0:2, :], m["sums_row"][:, :].rearrange("p (a d) -> p a d", a=2), 1.0 / NODES, None, ALU.mult))
            link(tt(r[:, 2, :], r[:, 1, :], r[:, 1, :], ALU.mult))
            link(tt(r[:, 2, :], r[:, 0, :], r[:, 2, :], ALU.subtract))
            link(tt(r[:, 2, :], r[:, 2, :], m["var_row"][:, :], ALU.add))
            ts(r[:, 2, :], r[:, 2, :], EPS, None, ALU.add).then_inc(s_sqrt, 1)
            dve.wait_ge(s_sqrt_done, 1)
            link(nc.vector.reciprocal(r[:, 4, :], r[:, 3, :]))
            link(tt(ab_row[:, 0, :], m["vec_rows"][:, 1, :], r[:, 4, :], ALU.mult))
            link(tt(r[:, 5, :], r[:, 1, :], ab_row[:, 0, :], ALU.mult))
            tt(ab_row[:, 1, :], m["vec_rows"][:, 2, :], r[:, 5, :], ALU.subtract).then_inc(s_ab, 1)
            dve.wait_ge(s_ab, 1)
            link(tt(r[:, 0, :], m["centre_row"][:, :], ab_row[:, 0, :], ALU.mult))
            link(tt(base_row[:, :], r[:, 0, :], ab_row[:, 1, :], ALU.add))
            split3(nc, m, link, base_parts[:, :], base_row[:, :], (m["split_f"], m["split_b"]))
            dve.wait_ge(s_bc, 1)
            link(nc.vector.tensor_copy(ab[:, :, :], ps_ab[:, 0:2 * D].rearrange("p (a d) -> p a d", a=2)))
            tt(w_scaled[:, :], m["wloop_sb"][:, :], ab[:, 0, :], ALU.mult).then_inc(s_ready, 1)

            def stats(t, link, n, zed):
                s = t.slot()
                row_stats(nc, link, st[:, s, :, :], mv[:, s, :, :], P, z[:, s, :, :], n).then_inc(zed[s], 1)

            def scales(t, link, n, sd_ready, scale_ready):
                s, u = t.slot(), t.uses()
                dve.wait_ge(sd_ready[s], u + 1)
                link(nc.vector.reciprocal(rstd[:, s, 0:n], sd[:, s, 0:n]))
                stt(shift[:, s, 0:n], mv[:, s, 2, 0:n], -0.5, rstd[:, s, 0:n], ALU.mult, ALU.mult)\
                    .then_inc(scale_ready[s], 1)

            def nodes(t):
                s, u, s4, u4 = t.slot(), t.uses(), t.slot(4), t.uses(4)
                link = LoopChain(dve, s_chain, 4, t.g)
                dve.wait_ge(lin[s], u + 1)
                dve.wait_ge(normed[s], u)
                dve.wait_ge(pooled[s], u)
                for h in range(2):
                    v = slice(h * G, (h + 1) * G)
                    last = stt(z[:, s, v, :], ps_u[:, s, v, :], 0.0, x1[:, s4, v, :], ALU.max, ALU.add)
                last.then_inc(x_used[s4], 1)
                dve.wait_ge(x_used[s4], u4 + 1)
                stats(t, link, CH, zed)
                scales(t, link, CH, sd_ready, scale_ready)
                link.end()
            in_turns(dve, nodes)
            for s in range(2):
                dve.wait_ge(normed[s], FIX_TURN_USES[s])
                dve.wait_ge(pooled[s], FIX_TURN_USES[s])

            def edge_rows(t, link, row, a, b, n):
                s, u, s4, u4 = t.slot(), t.uses(), t.slot(4), t.uses(4)
                zz = z[:, s, 0:n, :]
                dve.wait_ge(e_normed[s], u)
                link(tt(zz, row, a, ALU.mult))
                link(tt(zz, zz, b, ALU.add))
                dve.wait_ge(e_in[s4], 16 * (u4 + 1))
                stt(zz, zz, 0.0, x1[:, s4, 0:n, :], ALU.max, ALU.add).then_inc(e_used[s4], 1)
                dve.wait_ge(e_used[s4], u4 + 1)
                stats(t, link, n, e_zed)
                scales(t, link, n, e_sd, e_scale)

            def edges(t):
                link = LoopChain(dve, s_echain, 6, t.g)
                edge_rows(t, link, rows[:, ds(1 + G * t.g, G), :], ab[:, 0, :].unsqueeze(1).to_broadcast([P, G, D]),
                          ab[:, 1, :].unsqueeze(1).to_broadcast([P, G, D]), G)
                link.end()
            in_turns(dve, edges)
            edge_rows(FIX_TURN, Chain(dve, s_tail), rows[:, FIX:FIX + 1, :], ab[:, 0:1, :], ab[:, 1:2, :], 1)

        @block.gpsimd
        def _(pool):
            def nodes(t):
                s, u = t.slot(), t.uses()
                pool.wait_ge(scale_ready[s], u + 1)
                pool.wait_ge(x_out[s], 16 * u)
                carry_wait(nc, m)
                for j in range(CH - POOL_ROWS, CH):
                    last = nc.gpsimd.tensor_scalar(y[:, s, j, :], z[:, s, j, :], rstd[:, s, j:j + 1],
                                                   shift[:, s, j:j + 1], ALU.mult, ALU.add)
                last.then_inc(pooled[s], 1)
                pool.wait_ge(pooled[s], u + 1)
                carry_wait(nc, m, 1)
            in_turns(pool, nodes)
            for s in range(2):
                pool.wait_ge(x_out[s], 16 * FIX_TURN_USES[s])

            def scatter(t, col, n):
                s, u = t.slot(), t.uses()
                pool.wait_ge(e_sent[s], 16 * G * u)
                carry_wait(nc, m)
                nc.gpsimd.tensor_copy(idx[:, s, 0:n], m["scatter_idx"][:, ds(col, n)]).then_inc(s_idx, 1)
                pool.wait_ge(s_idx, t.g + 1)
                pool.wait_ge(e_normed[s], u + 1)
                carry_wait(nc, m, 1)
                for j in range(n):
                    nc.gpsimd.indirect_dma_start(
                        out=m["out"][:, :], out_offset=bass.IndirectOffsetOnAxis(ap=idx[:, s, j:j + 1], axis=0),
                        in_=y[:, s, j, :], in_offset=None, bounds_check=NODES - 1, oob_is_err=False,
                    ).then_inc(e_sent[s], 16)
            in_turns(pool, lambda t: scatter(t, G * t.g, G))
            scatter(FIX_TURN, T, 1)
            for s in range(2):
                groups, fix = FIX_TURN_USES[s], s == f2
                pool.wait_ge(e_sent[s], 16 * (G * groups + fix))


def kernel(**inputs):
    import numpy as np
    import concourse.bacc as bacc
    from concourse.bass_utils import run_bass_kernel_spmd as run

    fill = P * T - EDGES
    a = {n: np.asarray(v) for n, v in inputs.items()}
    pad = lambda v: np.concatenate([v, np.zeros(fill, v.dtype)])
    dst = a["dst"]
    dst = np.concatenate([np.full(1, -1, dst.dtype), dst, np.full(fill, NODES, dst.dtype),
                          np.full(1, NODES + 1, dst.dtype)])
    arrays = {
        "x": a["x"], "src": pad(a["src"]), "dst": dst[1:-1], "near": np.stack([dst[0:P * T:T], dst[T + 1::T]], 1), "rel": pad(a["edge_type_32"]), "ew": pad(a["edge_weight"]),
        "wk": a["L0_gnn_Wk"], "wk_t": a["L0_gnn_Wk"].T, "bk": a["L0_gnn_bk"], "wq_t": a["L0_gnn_Wq"].T,
        "bq": a["L0_gnn_bq"], "wv": a["L0_gnn_Wv"], "bv": a["L0_gnn_bv"], "rel_att": a["L0_gnn_rel_att"],
        "rel_msg": a["L0_gnn_rel_msg"], "w_loop": a["L1_gnn_w_loop"], "w_bases": a["L1_gnn_w_bases"],
        "w_coef": a["L1_gnn_w_rel_coef"], "w_coef_t": a["L1_gnn_w_rel_coef"].T, "att_l": a["L1_gnn_att_l_w"],
        "w_bias": a["L1_gnn_w_bias"], "gamma": a["L1_gnn_bn_gamma"], "beta": a["L1_gnn_bn_beta"],
    }
    arrays = {n: np.ascontiguousarray(v) for n, v in arrays.items()}
    nc = bacc.Bacc("TRN2", target_bir_lowering=False, num_devices=1)
    args = {n: nc.dram_tensor(f"in_{n}", v.shape, mybir.dt.from_np(v.dtype), kind="ExternalInput").ap()
            for n, v in arrays.items()}
    out = nc.dram_tensor("out_0", (NODES, D), F32, kind="ExternalOutput").ap()
    program(nc, out=out, **args)
    r = run(nc, [{f"in_{n}": v for n, v in arrays.items()}], core_ids=[0])
    return r.results[0]["out_0"]
```

```python
from contextlib import ExitStack, contextmanager

import concourse.bass as bass
from concourse import mybir

ALU = mybir.AluOpType
ACT = mybir.ActivationFunctionType
AX = mybir.AxisListType
F32 = mybir.dt.float32
BF16 = mybir.dt.bfloat16
I32 = mybir.dt.int32

NODES = 50000
EDGES = 25000
D = 128
HEADS = 8
DK = D // HEADS
RELS = 32
BASES = 8
P = 128
T = -(-EDGES // P)
G = 4
NG = T // G
UNROLL = 4
CH = 8
CHUNK = P * CH
NCH = -(-NODES // CHUNK)
LASTP = (NODES - (NCH - 1) * CHUNK) // CH
FIX = T + 1
FAR = 3.0e38
EPS = 1e-5
SLOPE = 0.01
assert NG * G == T and NG % UNROLL == 1 and NCH == NG and (NCH - 1) * CHUNK + LASTP * CH == NODES
ds = bass.ds


class Turn:

    def __init__(self, i, k):
        self.i, self.k = i, k
        self.g = UNROLL * i + k
        self.starts = isinstance(i, int) and i == 0
        self.last = isinstance(i, int) and self.g == NG - 1
        self.np = LASTP if self.last else P

    def slot(self, n=2):
        return self.k % n

    def uses(self, n=2):
        return UNROLL // n * self.i + self.k // n

    def prev(self):
        if self.k > 0:
            return Turn(self.i, self.k - 1)
        return None if self.starts else Turn(self.i - 1, UNROLL - 1)

    def back(self, n):
        turns = [self]
        for _ in range(n):
            turns.append(turns[-1] and turns[-1].prev())
        return turns

    def next(self):
        return None if self.last else Turn(self.i, self.k + 1) if self.k + 1 < UNROLL else Turn(self.i + 1, 0)


def in_turns(eng, body, peeled=1):
    for g in range(peeled * UNROLL):
        body(Turn(g // UNROLL, g % UNROLL))
    with eng.Fori(peeled, NG // UNROLL) as i:
        for k in range(UNROLL):
            body(Turn(i, k))
    body(Turn(NG // UNROLL, 0))


LAST = Turn(NG // UNROLL, 0)


def behind_last(n):
    return [[None] * k + LAST.back(n - k) for k in range(1, n + 1)]


FIX_TURN = Turn(NG // UNROLL, 1)
FIX_TURN_USES = [len(range(s, NG, 2)) for s in range(2)]


class Chain:

    def __init__(self, eng, sem):
        self.eng, self.sem, self.n = eng, sem, 0

    def __call__(self, ins):
        self.n += 1
        ins.then_inc(self.sem, 1)
        self.eng.wait_ge(self.sem, self.n)


class LoopChain:

    def __init__(self, eng, sem, per, turn):
        self.eng, self.sem, self.per, self.turn, self.n = eng, sem, per, turn, 0

    def __call__(self, ins, wait=True):
        self.n += 1
        ins.then_inc(self.sem, 1)
        if wait:
            self.wait(self.n)

    def wait(self, n):
        self.eng.wait_ge(self.sem, self.turn * self.per + n)

    def end(self):
        assert self.n == self.per, (self.n, self.per)


def program(nc, x, src, dst, near, rel, ew, wk, wk_t, bk, wq_t, bq, wv, bv, rel_att, rel_msg, w_loop, w_bases,
            w_coef, w_coef_t, att_l, w_bias, gamma, beta, out):
    x1_table = nc.dram_tensor("x1_table", [NODES, D], F32).ap()
    delta_table = nc.dram_tensor("delta_table", [NODES, D], F32).ap()
    xd_kept = [nc.dram_tensor(f"xd_kept{n}", [P, T + n, D], F32).ap() for n in range(2)]
    ctx = ExitStack()

    def sb(name, shape, dt=F32, c=ctx):
        return c.enter_context(nc.sbuf_tensor(name, shape, dt))

    with ctx:
        rows = sb("rows", [P, T + 2, D])
        ident = sb("ident", [P, P])
        ones_row = sb("ones_row", [1, P])
        ones_col = sb("ones_col", [P, 1])
        carried_by = sb("carried_by", [P, P])
        dst_x = sb("dst_x", [P, T + 2])
        cont = sb("cont", [P, T])
        more = sb("more", [P, T])
        pen_cont = sb("pen_cont", [P, T])
        pen_more = sb("pen_more", [P, T])
        stops = sb("stops", [P, T])
        in_first = sb("in_first", [P, T])
        in_last = sb("in_last", [P, T])
        inside = sb("inside", [P, T])
        pen_first = sb("pen_first", [P, T])
        pen_last = sb("pen_last", [P, T])
        head_end = sb("head_end", [P, T])
        valid = sb("valid", [P, T + 1])
        apart = sb("apart", [P, 1])
        same = [sb(f"same{q}", [P, 2 * P]) for q in range(2)]
        pen_same = [sb(f"pen_same{q}", [P, 2 * P]) for q in range(2)]
        gather_idx = sb("gather_idx", [P, NG, 2 * G], I32)
        scatter_idx = sb("scatter_idx", [P, T + G], I32)
        ew_sb = sb("ew_sb", [P, T])
        rel_f = sb("rel_f", [P, T])
        iota_rel = sb("iota_rel", [P, RELS])
        coef = sb("coef", [P, T, BASES])
        att = sb("att", [P, HEADS, T])
        weight = sb("weight", [P, HEADS + 1, T])
        norm = sb("norm", [P, T])
        eps_col = sb("eps_col", [P, 1])
        scrap = sb("scrap", [P, 4])
        wq_sb = sb("wq_sb", [D, D])
        wkv_sb = sb("wkv_sb", [D, 2 * D])
        bq_parts = sb("bq_parts", [3, D], BF16)
        bkv_parts = sb("bkv_parts", [3, 2 * D], BF16)
        ones3 = sb("ones3", [3, P], BF16)
        split_f = sb("split_f", [3, 2 * D])
        split_b = sb("split_b", [3, 3, 2 * D], BF16)
        rel_att_all = sb("rel_att_all", [P, D])
        wloop_sb = sb("wloop_sb", [D, D])
        bases_sb = sb("bases_sb", [D, BASES * D])
        a_sb = sb("a_sb", [D, RELS])
        coef_blocks = sb("coef_blocks", [P, G * BASES])
        vec_rows = sb("vec_rows", [3, 3, D])
        centre_row = sb("centre_row", [3, D])
        var_row = sb("var_row", [3, D])
        logits_fix = sb("logits_fix", [P, RELS])
        gram_sb = sb("gram_sb", [P, D + 1])
        xd_sb = sb("xd_sb", [D, D])
        dd_sb = sb("dd_sb", [D, D + 1])

        setup(nc, locals())
        m = locals()
        project(nc, m)
        segment_softmax(nc, m, 0)
        with nc.sbuf_tensor("dst_logits", [P, T, RELS], F32) as dst_logits:
            m["dst_logits"] = dst_logits
            sum_layer0(nc, m)
            messages(nc, m)
        segment_softmax(nc, m, 1)
        sum_layer1(nc, m)
        centre(nc, m)
        output(nc, m)


@contextmanager
def phase_sems(nc):
    made = []

    def sem(name):
        made.append(nc.alloc_semaphore(name))
        return made[-1]
    yield sem
    nc.clear_and_free_semaphores(made)
    nc.all_engine_barrier()


def carry_wait(nc, m, n=0):
    nc.gpsimd.tensor_tensor(m["scrap"][:, n:n + 1], m["eps_col"][:, :], m["eps_col"][:, :], ALU.add)


def row_stats_steps(nc, st, part, np, x, n):
    s, p = st[0:np, 0:n, :], part[0:np]
    tt = nc.vector.tensor_tensor

    def rows(a, b):
        for j in range(a, b):
            last = nc.vector.bn_stats(st[0:np, j, :], x[0:np, j, :])
        return last

    def combine():
        tt(p[:, 2, 0:n], s[:, :, 1], s[:, :, 4], ALU.add)
        tt(p[:, 1, 0:n], s[:, :, 2], s[:, :, 5], ALU.add)
        return tt(p[:, 0, 0:n], s[:, :, 1], s[:, :, 4], ALU.subtract)

    def square():
        return tt(p[:, 0, 0:n], p[:, 0, 0:n], p[:, 0, 0:n], ALU.mult)

    def finish():
        return nc.vector.scalar_tensor_tensor(p[:, 1, 0:n], p[:, 0, 0:n], D / 4.0, p[:, 1, 0:n], ALU.mult, ALU.add)
    return (rows, combine, square), finish


def row_stats(nc, link, st, part, np, x, n):
    (rows, combine, square), finish = row_stats_steps(nc, st, part, np, x, n)
    link(rows(0, n))
    link(combine())
    link(square())
    return finish()


def split3(nc, m, link, out, x, t):
    f, b = t
    n = x.shape[-1]
    f, b, pick = f[:, 0:n], b[:, :, 0:n], m["ident"]
    cp, tt = nc.vector.tensor_copy, nc.vector.tensor_tensor
    link(cp(b[:, 0, :], x))
    link(tt(f, x, b[:, 0, :], ALU.subtract))
    link(cp(b[:, 1, :], f))
    link(tt(f, f, b[:, 1, :], ALU.subtract))
    link(cp(b[:, 2, :], f))
    link(nc.vector.tensor_scalar(out, b[:, 0, :], pick[0:3, 0:1], None, ALU.mult))
    for k in (1, 2):
        link(nc.vector.scalar_tensor_tensor(out, b[:, k, :], pick[0:3, k:k + 1], out, ALU.mult, ALU.add))


def setup(nc, m):
    (dst_x, cont, more, pen_cont, pen_more, stops, in_first, in_last, inside, pen_first, pen_last, head_end, valid,
     apart, same, pen_same, ident) = (m[n] for n in (
        "dst_x", "cont", "more", "pen_cont", "pen_more", "stops", "in_first", "in_last", "inside", "pen_first",
        "pen_last", "head_end", "valid", "apart", "same", "pen_same", "ident"))
    gather_idx, scatter_idx, carried_by, rows = m["gather_idx"], m["scatter_idx"], m["carried_by"], m["rows"]
    ends_dram = nc.dram_tensor("ends_dram", [P, 2], F32).ap()
    with ExitStack() as c:
        new_sem = c.enter_context(phase_sems(nc))

        def sb(name, shape, dt=F32):
            return c.enter_context(nc.sbuf_tensor(name, shape, dt))

        def sem(name):
            return new_sem(name)

        edge_i = sb("edge_i", [P, 3, T], I32)
        near_i = sb("near_i", [P, 2], I32)
        iota_i = sb("iota_i", [P, RELS], I32)
        equal = sb("equal", [P, T + 1])
        t0 = sb("t0", [P, T + 1])
        t1 = sb("t1", [P, T + 1])
        ends = sb("ends", [P, 2])
        ends_all = sb("ends_all", [P, P, 2])
        wv_nat = sb("wv_nat", [D, D])
        msg_blocks = sb("msg_blocks", [D, D])
        bias3 = sb("bias3", [3, 3, D])
        bv_col = sb("bv_col", [D, 1])
        att_row = sb("att_row", [1, D])
        coef_t = sb("coef_t", [BASES, RELS])
        base_att = sb("base_att", [D, BASES])
        base_tmp = sb("base_tmp", [D, BASES * D])
        base_att_t = sb("base_att_t", [BASES, D])
        ps = c.enter_context(nc.psum_tensor("ps_setup", [P, 4, 512], F32))
        s_zero, s_blocks, s_edges, s_weights = sem("s_zero"), sem("s_blocks"), sem("s_edges"), sem("s_weights")
        s_pool, s_pool_done, s_dve, s_mm, s_base, s_bt = (sem(n) for n in (
            "s_pool", "s_pool_done", "s_dve", "s_mm", "s_base", "s_bt"))
        s_ends, s_ends_out, s_ends_in, s_fold, s_base_t = (sem(n) for n in (
            "s_ends", "s_ends_out", "s_ends_in", "s_fold", "s_base_t"))
        block = c.enter_context(nc.Block())
        N_BLOCKS = HEADS + G

        @block.sync
        def _(sp):
            n_edges = 0
            for a, b in ((m["src"].rearrange("(p t) -> p t", t=T), edge_i[:, 0, :]),
                         (m["dst"].rearrange("(p t) -> p t", t=T), edge_i[:, 1, :]),
                         (m["rel"].rearrange("(p t) -> p t", t=T), edge_i[:, 2, :]),
                         (m["near"], near_i[:, :]),
                         (m["ew"].rearrange("(p t) -> p t", t=T), m["ew_sb"][:, :])):
                sp.dma_start(b, a).then_inc(s_edges, 16)
                n_edges += 1
            assert n_edges == 5
            col = lambda v: v.rearrange("(n a) -> n a", a=1)
            for a, b in ((m["wv"], wv_nat[:, :]), (m["wk_t"], m["wkv_sb"][:, 0:D]),
                         (m["wq_t"], m["wq_sb"][:, :]), (m["bq"].partition_broadcast(3), bias3[:, 2, :]),
                         (m["bk"].partition_broadcast(3), bias3[:, 0, :]),
                         (m["rel_att"].rearrange("h d -> (h d)").partition_broadcast(P), m["rel_att_all"][:, :]),
                         (col(m["bv"]), bv_col[:, :]), (m["w_loop"], m["wloop_sb"][:, :]),
                         (m["w_bases"].rearrange("b i o -> i b o"),
                          m["bases_sb"][:, :].rearrange("i (b o) -> i b o", b=BASES)),
                         (m["w_coef_t"], coef_t[:, :]), (m["att_l"], att_row[:, :]),
                         (m["w_bias"].partition_broadcast(3), m["vec_rows"][:, 0, :]),
                         (m["gamma"].partition_broadcast(3), m["vec_rows"][:, 1, :]),
                         (m["beta"].partition_broadcast(3), m["vec_rows"][:, 2, :])):
                sp.dma_start(b, a).then_inc(s_weights, 16)
            sp.wait_ge(s_ends, 1)
            sp.dma_start(ends_dram, ends[:, :]).then_inc(s_ends_out, 16)
            sp.wait_ge(s_ends_out, 16)
            sp.dma_start(ends_all[:, :, :], ends_dram.partition_broadcast(P)).then_inc(s_ends_in, 16)

        @block.scalar
        def _(act):
            act.wait_ge(s_zero, 1)
            for h in range(HEADS):
                a, b = h * DK, (h + 1) * DK
                act.dma_start(msg_blocks[a:b, a:b], m["rel_msg"][h]).then_inc(s_blocks, 16)
            for j in range(G):
                act.dma_start(m["coef_blocks"][j * RELS:(j + 1) * RELS, j * BASES:(j + 1) * BASES],
                              m["w_coef"]).then_inc(s_blocks, 16)

        @block.gpsimd
        def _(pool):
            nc.gpsimd.memset(msg_blocks[:, :], 0.0)
            nc.gpsimd.memset(m["coef_blocks"][:, :], 0.0).then_inc(s_zero, 1)
            nc.gpsimd.memset(m["ones_row"][:, :], 1.0)
            nc.gpsimd.memset(m["ones_col"][:, :], 1.0)
            nc.gpsimd.memset(m["ones3"][:, :], 1.0)
            nc.gpsimd.memset(m["eps_col"][:, :], EPS)
            nc.gpsimd.memset(rows[:, 0, :], 0.0)
            nc.gpsimd.iota(iota_i[:, :], pattern=[[1, RELS]], base=0, channel_multiplier=0)
            nc.gpsimd.memset(carried_by[:, :], 1.0)
            nc.gpsimd.memset(ident[:, :], 0.0).then_inc(s_pool, 1)
            pool.wait_ge(s_pool, 1)
            nc.gpsimd.affine_select(out=ident[:, :], in_=ident[:, :], compare_op=ALU.not_equal, fill=1.0, base=0,
                                    pattern=[[-1, P]], channel_multiplier=1)
            nc.gpsimd.affine_select(out=carried_by[:, :], in_=carried_by[:, :], compare_op=ALU.is_gt, fill=0.0,
                                    base=0, pattern=[[1, P]], channel_multiplier=-1).then_inc(s_pool_done, 1)

        @block.vector
        def _(dve):
            link = Chain(dve, s_dve)
            ts, tt, cp = nc.vector.tensor_scalar, nc.vector.tensor_tensor, nc.vector.tensor_copy
            dve.wait_ge(s_edges, 16 * 5)
            cp(dst_x[:, 1:T + 1], edge_i[:, 1, :])
            cp(dst_x[:, 0:1], near_i[:, 0:1])
            cp(dst_x[:, T + 1:T + 2], near_i[:, 1:2])
            cp(m["rel_f"][:, :], edge_i[:, 2, :])
            cp(gather_idx[:, :, 0:G], edge_i[:, 0, :].rearrange("p (g j) -> p g j", j=G))
            link(cp(ends[:, 0:1], edge_i[:, 1, 0:1]))
            cp(ends[:, 1:2], edge_i[:, 1, T - 1:T]).then_inc(s_ends, 1)
            link(ts(t0[:, 0:T], dst_x[:, 1:T + 1], float(NODES - 1), None, ALU.min))
            link(cp(gather_idx[:, :, G:2 * G], t0[:, 0:T].rearrange("p (g j) -> p g j", j=G)))
            link(tt(equal[:, :], dst_x[:, 0:T + 1], dst_x[:, 1:T + 2], ALU.is_equal))
            nc.vector.memset(cont[:, 0:1], 0.0)
            cp(cont[:, 1:T], equal[:, 1:T])
            cp(more[:, 0:T - 1], equal[:, 1:T])
            link(nc.vector.memset(more[:, T - 1:T], 0.0))
            ts(pen_cont[:, :], cont[:, :], -1.0, FAR, ALU.add, ALU.mult)
            ts(pen_more[:, :], more[:, :], -1.0, FAR, ALU.add, ALU.mult)
            ts(stops[:, :], more[:, :], -1.0, 1.0, ALU.mult, ALU.add)
            ts(in_first[:, :], dst_x[:, 1:T + 1], dst_x[:, 1:2], None, ALU.is_equal)
            ts(in_last[:, :], dst_x[:, 1:T + 1], dst_x[:, T:T + 1], None, ALU.is_equal)
            link(tt(apart[:, :], dst_x[:, 1:2], dst_x[:, T:T + 1], ALU.not_equal))
            ts(pen_first[:, :], in_first[:, :], -1.0, FAR, ALU.add, ALU.mult)
            link(ts(pen_last[:, :], in_last[:, :], -1.0, FAR, ALU.add, ALU.mult))
            link(ts(in_last[:, :], in_last[:, :], apart[:, 0:1], None, ALU.mult))
            link(tt(t1[:, 0:T], in_first[:, :], in_last[:, :], ALU.add))
            link(ts(inside[:, :], t1[:, 0:T], -1.0, 1.0, ALU.mult, ALU.add))
            link(ts(t1[:, 0:T], in_first[:, :], equal[:, 0:1], None, ALU.mult))
            link(tt(head_end[:, :], t1[:, 0:T], stops[:, :], ALU.mult))
            link(ts(t0[:, 0:T], equal[:, 1:T + 1], -1.0, 1.0, ALU.mult, ALU.add))
            link(tt(pen_same[0][:, 0:T], t0[:, 0:T], head_end[:, :], ALU.mult))
            link(nc.vector.reduce_sum(valid[:, T:T + 1], pen_same[0][:, 0:T], AX.X))
            link(ts(t1[:, 0:T], t1[:, 0:T], -1.0, 1.0, ALU.mult, ALU.add))
            link(tt(valid[:, 0:T], t0[:, 0:T], t1[:, 0:T], ALU.mult))
            ts(t0[:, 0:T], dst_x[:, 1:T + 1], float(NODES), None, ALU.is_lt)
            link(ts(t0[:, T:T + 1], dst_x[:, 1:2], float(NODES), None, ALU.is_lt))
            link(tt(valid[:, :], valid[:, :], t0[:, :], ALU.mult))
            ts(t0[:, 0:T], dst_x[:, 1:T + 1], float(-NODES), None, ALU.add)
            link(ts(t0[:, T:T + 1], dst_x[:, 1:2], float(-NODES), None, ALU.add))
            link(tt(t0[:, :], t0[:, :], valid[:, :], ALU.mult))
            link(ts(t0[:, :], t0[:, :], float(NODES), None, ALU.add))
            link(cp(scatter_idx[:, 0:T + 1], t0[:, :]))
            dve.wait_ge(s_pool_done, 1)
            cp(m["iota_rel"][:, :], iota_i[:, :])
            dve.wait_ge(s_ends_in, 16)
            flat = ends_all[:, :, :].rearrange("p q c -> p (q c)")
            for q, mine in enumerate((dst_x[:, 1:2], dst_x[:, T:T + 1])):
                ts(same[q][:, :], flat, mine, None, ALU.is_equal)
            link(ts(base_tmp[:, 0:P], ends_all[:, :, 0], dst_x[:, T:T + 1], None, ALU.is_equal))
            link(tt(carried_by[:, :], carried_by[:, :], base_tmp[:, 0:P], ALU.mult))
            for q in range(2):
                ts(pen_same[q][:, :], same[q][:, :], -1.0, FAR, ALU.add, ALU.mult)
            dve.wait_ge(s_mm, 1)
            link(tt(base_tmp[:, :].rearrange("i (b o) -> i b o", b=BASES),
                    m["bases_sb"][:, :].rearrange("i (b o) -> i b o", b=BASES),
                    ps[:, 0, 0:D].unsqueeze(1).to_broadcast([D, BASES, D]), ALU.mult))
            nc.vector.tensor_reduce(base_att[:, :], base_tmp[:, :].rearrange("i (b o) -> i b o", b=BASES),
                                    AX.X, ALU.add).then_inc(s_base, 1)
            cp(m["wkv_sb"][:, D:2 * D], ps[:, 1, 0:D])
            link(cp(bias3[:, 1, :], ps[0:3, 2, 0:D]))
            t = (m["split_f"], m["split_b"])
            split3(nc, m, link, m["bkv_parts"][:, :], bias3[:, 0:2, :].rearrange("p a d -> p (a d)"), t)
            split3(nc, m, link, m["bq_parts"][:, :], bias3[:, 2, :], t)
            dve.wait_ge(s_bt, 1)
            cp(base_att_t[:, :], ps[0:BASES, 3, 0:D]).then_inc(s_base_t, 1)
            dve.wait_ge(s_fold, 1)
            cp(m["a_sb"][:, :], ps[:, 3, 256:256 + RELS])

        @block.tensor
        def _(pe):
            pe.wait_ge(s_weights, 16 * 14)
            pe.wait_ge(s_blocks, 16 * N_BLOCKS)
            pe.wait_ge(s_pool_done, 1)
            mm = nc.tensor.matmul
            mm(ps[:, 0, 0:D], m["ones_row"][:, :], att_row[:, :], start=True, stop=True)
            mm(ps[:, 1, 0:D], wv_nat[:, :], msg_blocks[:, :], start=True, stop=True)
            mm(ps[0:3, 2, 0:D], bv_col[:, :].to_broadcast([D, 3]), msg_blocks[:, :], start=True, stop=True)\
                .then_inc(s_mm, 1)
            pe.wait_ge(s_base, 1)
            nc.tensor.transpose(ps[0:BASES, 3, 0:D], base_att[:, :], ident[:, :]).then_inc(s_bt, 1)
            pe.wait_ge(s_base_t, 1)
            mm(ps[:, 3, 256:256 + RELS], base_att_t[:, :], coef_t[:, :], start=True, stop=True).then_inc(s_fold, 1)


def project(nc, m):
    rows, ident, att, gather_idx = m["rows"], m["ident"], m["att"], m["gather_idx"]
    with ExitStack() as c:
        new_sem = c.enter_context(phase_sems(nc))

        def sb(name, shape, dt=F32):
            return c.enter_context(nc.sbuf_tensor(name, shape, dt))

        def sems(name, n=2):
            return [new_sem(f"{name}{k}") for k in range(n)]

        def ps(name, shape):
            return c.enter_context(nc.psum_tensor(name, shape, F32))

        idx = sb("idx", [P, 2, 2 * G], I32)
        ends = sb("gathered", [P, 2, 2, G, D])
        ends_t = sb("gathered_t", [P, 2, 2, G * P])
        q_sb = sb("q_sb", [P, 2, G, D])
        prod = sb("prod", [P, 2, G, D])
        xin = sb("xin", [P, 4, CH, D])
        xout = sb("xout", [P, 2, CH, D])
        st = sb("st", [P, 2, CH, 6])
        mv = sb("mv", [P, 2, 3, CH])
        sd = sb("sd", [P, 2, CH])
        rstd = sb("rstd", [P, 2, CH])
        shift = sb("shift", [P, 2, CH])
        ps_t = ps("ps_t", [P, 2, G * P])
        ps_q = ps("ps_q", [P, 2, G, D])
        ps_kv = ps("ps_kv", [P, 2, G, 2 * D])
        idx_ready, s_chain = sems("idx_ready", 1)[0], sems("project_chain", 1)[0]
        fetched, saved, turned, turned_sb, projected, v_done, att_done = (
            sems(n) for n in ("fetched", "saved", "turned", "turned_sb", "projected", "v_done", "att_done"))
        x_stats, sd_ready, scale_ready, x_normed, x_out = (
            sems(n) for n in ("x_stats", "sd_ready", "scale_ready", "x_normed", "x_out"))
        x_in = sems("x_in", 4)
        block = c.enter_context(nc.Block())

        @block.gpsimd
        def _(pool):
            def gather(t):
                s, u = t.slot(), t.uses()
                pool.wait_ge(fetched[s], 128 * u)
                pool.wait_ge(turned[s], u)
                pool.wait_ge(saved[s], 16 * u)
                nc.gpsimd.tensor_copy(idx[:, s, :], gather_idx[:, ds(t.g, 1), :].rearrange("p a j -> p (a j)"))\
                    .then_inc(idx_ready, 1)
                pool.wait_ge(idx_ready, t.g + 1)
                carry_wait(nc, m)
                for e in range(2):
                    for j in range(G):
                        nc.gpsimd.indirect_dma_start(
                            out=ends[:, s, e, j, :], out_offset=None, in_=m["x"][:, :],
                            in_offset=bass.IndirectOffsetOnAxis(ap=idx[:, s, e * G + j:e * G + j + 1], axis=0),
                        ).then_inc(fetched[s], 16)
            in_turns(pool, gather)

        @block.sync
        def _(sp):
            def move(t):
                s, u, s4, u4 = t.slot(), t.uses(), t.slot(4), t.uses(4)
                if not t.starts:
                    sp.wait_ge(x_normed[s], u - 1)
                sp.dma_start(xin[0:t.np, s4, :, :], m["x"][ds(t.g * CHUNK, t.np * CH), :]
                             .rearrange("(p j) d -> p j d", j=CH)).then_inc(x_in[s4], 16)
                sp.wait_ge(fetched[s], 128 * (u + 1))
                sp.dma_start(m["xd_kept"][0][:, ds(G * t.g, G), :], ends[:, s, 1, :, :]).then_inc(saved[s], 16)
            in_turns(sp, move)
            for s in range(2):
                sp.wait_ge(saved[s], 16 * FIX_TURN_USES[s])

        @block.tensor
        def _(pe):
            mm = nc.tensor.matmul

            def turn_rows(t):
                s, u = t.slot(), t.uses()
                pe.wait_ge(fetched[s], 128 * (u + 1))
                pe.wait_ge(turned_sb[1 - s], t.uses() + s)
                for e in range(2):
                    for j in range(G):
                        last = nc.tensor.transpose(ps_t[:, e, j * P:(j + 1) * P], ends[:, s, e, j, :], ident[:, :])
                last.then_inc(turned[s], 1)

            def body(t):
                s, u = t.slot(), t.uses()
                if t.next():
                    turn_rows(t.next())
                pe.wait_ge(turned_sb[s], u + 1)
                pe.wait_ge(att_done[s], u)
                pe.wait_ge(v_done[s], u)
                mm(ps_q[:, s, :, :], m["ones3"][:, :], m["bq_parts"][:, :].unsqueeze(1).to_broadcast([3, G, D]),
                   start=True, stop=False, skip_group_check=True)
                for j in range(G):
                    mm(ps_q[:, s, j, :], ends_t[:, s, 1, j * P:(j + 1) * P], m["wq_sb"][:, :], start=False,
                       stop=True, skip_group_check=True)
                for j in range(G):
                    if j % 2 == 0:
                        mm(ps_kv[:, s, j:j + 2, :], m["ones3"][:, :],
                           m["bkv_parts"][:, :].unsqueeze(1).to_broadcast([3, 2, 2 * D]), start=True, stop=False,
                           skip_group_check=True)
                    last = mm(ps_kv[:, s, j, :], ends_t[:, s, 0, j * P:(j + 1) * P], m["wkv_sb"][:, :],
                              start=False, stop=True, skip_group_check=True)
                last.then_inc(projected[s], 1)
            turn_rows(Turn(0, 0))
            in_turns(pe, body)

        @block.scalar
        def _(act):
            def turned_out(t):
                s, u = t.slot(), t.uses()
                act.wait_ge(turned[s], u + 1)
                act.wait_ge(projected[s], u)
                nc.scalar.activation(ends_t[:, s, 0, :], ps_t[:, 0, :], ACT.Copy)
                nc.scalar.activation(ends_t[:, s, 1, :], ps_t[:, 1, :], ACT.Copy).then_inc(turned_sb[s], 1)

            def body(t):
                s, u, s4, np = t.slot(), t.uses(), t.slot(4), t.np
                if t.next():
                    turned_out(t.next())
                act.wait_ge(x_stats[s], u + 1)
                nc.scalar.activation(sd[0:np, s, :], mv[0:np, s, 1, :], ACT.Sqrt, bias=m["eps_col"][0:np, :],
                                     scale=1.0 / D).then_inc(sd_ready[s], 1)
                act.wait_ge(projected[s], u + 1)
                nc.scalar.activation(m["scrap"][:, 1:2], m["eps_col"][:, :], ACT.Copy)
                nc.scalar.activation(rows[:, ds(1 + G * t.g, G), :], ps_kv[:, s, :, D:2 * D], ACT.Copy)\
                    .then_inc(v_done[s], 1)
                act.wait_ge(scale_ready[s], u + 1)
                act.wait_ge(x_out[s], 16 * u)
                for j in range(CH):
                    last = nc.scalar.activation(xout[0:np, s, j, :], xin[0:np, s4, j, :], ACT.Identity,
                                                bias=shift[0:np, s, j:j + 1], scale=rstd[0:np, s, j:j + 1])
                last.then_inc(x_normed[s], 1)
                act.wait_ge(x_normed[s], u + 1)
                act.dma_start(m["x1_table"][ds(t.g * CHUNK, np * CH), :].rearrange("(p j) d -> p j d", j=CH),
                              xout[0:np, s, :, :]).then_inc(x_out[s], 16)
            turned_out(Turn(0, 0))
            in_turns(act, body)
            for s in range(2):
                act.wait_ge(x_out[s], 16 * FIX_TURN_USES[s])

        @block.vector
        def _(dve):
            PER = 9

            def body(t):
                s, u, s4, u4, np = t.slot(), t.uses(), t.slot(4), t.uses(4), t.np
                link = LoopChain(dve, s_chain, PER, t.g)
                dve.wait_ge(x_in[s4], 16 * (u4 + 1))
                dve.wait_ge(x_normed[s], u)
                row_stats(nc, link, st[:, s, :, :], mv[:, s, :, :], np, xin[:, s4, :, :], CH).then_inc(x_stats[s], 1)
                dve.wait_ge(projected[s], u + 1)
                for j in range(G):
                    link(nc.vector.scalar_tensor_tensor(q_sb[:, s, j, :], m["rel_att_all"][:, :],
                                                        m["ew_sb"][:, ds(G * t.g + j, 1)], ps_q[:, s, j, :],
                                                        ALU.mult, ALU.add), wait=j == G - 1)
                dve.wait_ge(v_done[s], u + 1)
                link(nc.vector.tensor_tensor(prod[:, s, :, :], q_sb[:, s, :, :], ps_kv[:, s, :, 0:D], ALU.mult))
                nc.vector.tensor_reduce(att[:, :, ds(G * t.g, G)].rearrange("p h j -> p j h"),
                                        prod[:, s, :, :].rearrange("p j (h d) -> p j h d", h=HEADS),
                                        AX.X, ALU.add).then_inc(att_done[s], 1)
                dve.wait_ge(sd_ready[s], u + 1)
                link(nc.vector.reciprocal(rstd[0:np, s, :], sd[0:np, s, :]))
                nc.vector.scalar_tensor_tensor(shift[0:np, s, :], mv[0:np, s, 2, :], -0.5, rstd[0:np, s, :],
                                               ALU.mult, ALU.mult).then_inc(scale_ready[s], 1)
                link.end()
            in_turns(dve, body)


def segment_softmax(nc, m, layer):
    att, weight = m["att"], m["weight"]
    H = HEADS if layer == 0 else 1
    HS = H + 1 if layer == 0 else 1
    scale = float(DK) ** -0.5 if layer == 0 else 1.0
    with ExitStack() as c:
        new_sem = c.enter_context(phase_sems(nc))

        def sb(name, shape, dt=F32):
            return c.enter_context(nc.sbuf_tensor(f"{name}_l{layer}", shape, dt))

        def sem(name):
            return new_sem(f"{name}_l{layer}")

        a = sb("scan_a", [P, HS, T])
        b = sb("scan_b", [P, HS, T])
        mine = sb("mine", [P, 2, 2, HS])
        tmp = sb("tmp", [P, HS, 2 * P])
        ps_all = c.enter_context(nc.psum_tensor(f"ps_all_l{layer}", [P, HS + HS % 2, 2, P], F32))
        whole = sb("whole", [P, 2, 2, HS])
        s_dve, s_mine, s_all, s_diff, s_exp, s_deg = (sem(n) for n in (
            "s_dve", "s_mine", "s_all", "s_diff", "s_exp", "s_deg"))
        block = c.enter_context(nc.Block())

        @block.tensor
        def _(pe):
            for n, h in enumerate((H, HS)):
                pe.wait_ge(s_mine, n + 1)
                for k in range(h):
                    for q in range(2):
                        last = nc.tensor.transpose(ps_all[:, k, q, :], mine[:, n, q, k:k + 1].to_broadcast([P, P]),
                                                   m["ident"][:, :])
                last.then_inc(s_all, 1)

        @block.scalar
        def _(act):
            act.wait_ge(s_diff, 1)
            nc.scalar.activation(a[:, 0:H, :], a[:, 0:H, :], ACT.Exp, scale=scale).then_inc(s_exp, 1)
            if layer == 0:
                act.wait_ge(s_deg, 1)
                nc.scalar.activation(m["norm"][:, :], b[:, H, :], ACT.Sqrt)

        @block.vector
        def _(dve):
            link = Chain(dve, s_dve)
            tt, stt, cp = nc.vector.tensor_tensor, nc.vector.scalar_tensor_tensor, nc.vector.tensor_copy
            scan = nc.vector.tensor_tensor_scan

            def over_heads(v, h):
                return v.unsqueeze(1).to_broadcast([P, h, v.shape[-1]])

            def boundary(n, h, masks, op, combine):
                dve.wait_ge(s_all, n + 1)
                for q in range(2):
                    link(tt(tmp[:, 0:h, :].rearrange("p h (c k) -> p h c k", c=2), ps_all[:, 0:h, :, :],
                            masks[q][:, :].rearrange("p (k c) -> p c k", c=2).unsqueeze(1).to_broadcast([P, h, 2, P]),
                            combine))
                    link(nc.vector.tensor_reduce(whole[:, n, q, 0:h], tmp[:, 0:h, :], AX.X, op))

            if layer == 1:
                link(nc.vector.tensor_scalar(a[:, 0, :], att[:, 0, :], SLOPE, None, ALU.mult))
                link(tt(att[:, 0, :], att[:, 0, :], a[:, 0, :], ALU.max))
            for h in range(H):
                last = scan(a[:, h, :], m["pen_cont"][:, :], att[:, h, :], 0.0, ALU.add, ALU.max)
            link(last)
            for h in range(H):
                last = scan(b[:, h, ::-1], m["pen_more"][:, ::-1], a[:, h, ::-1], 0.0, ALU.add, ALU.max)
            link(last)
            cp(mine[:, 0, 0, 0:H], b[:, 0:H, 0])
            cp(mine[:, 0, 1, 0:H], b[:, 0:H, T - 1]).then_inc(s_mine, 1)
            boundary(0, H, m["pen_same"], ALU.max, ALU.add)
            for q, pen in enumerate((m["pen_first"], m["pen_last"])):
                for h in range(H):
                    last = stt(b[:, h, :], pen[:, :], whole[:, 0, q, h:h + 1], b[:, h, :], ALU.add, ALU.max)
                link(last)
            tt(a[:, 0:H, :], att[:, 0:H, :], b[:, 0:H, :], ALU.subtract).then_inc(s_diff, 1)
            if layer == 0:
                link(nc.vector.memset(a[:, H, :], 1.0))
            dve.wait_ge(s_exp, 1)
            for h in range(HS):
                last = scan(b[:, h, :], m["cont"][:, :], a[:, h, :], 0.0, ALU.mult, ALU.add)
            link(last)
            link(tt(b[:, 0:HS, :], b[:, 0:HS, :], over_heads(m["stops"][:, :], HS), ALU.mult))
            for h in range(HS):
                last = scan(weight[:, h, ::-1], m["more"][:, ::-1], b[:, h, ::-1], 0.0, ALU.mult, ALU.add)
            link(last)
            nc.vector.tensor_scalar(mine[:, 1, 0, 0:HS], weight[:, 0:HS, 0], m["apart"][:, 0:1], None, ALU.mult)
            cp(mine[:, 1, 1, 0:HS], weight[:, 0:HS, T - 1]).then_inc(s_mine, 1)
            boundary(1, HS, m["same"], ALU.add, ALU.mult)
            link(tt(weight[:, 0:HS, :], weight[:, 0:HS, :], over_heads(m["inside"][:, :], HS), ALU.mult))
            for q, mask in enumerate((m["in_first"], m["in_last"])):
                for h in range(HS):
                    last = stt(weight[:, h, :], mask[:, :], whole[:, 1, q, h:h + 1], weight[:, h, :], ALU.mult, ALU.add)
                link(last)
            if layer == 0:
                link(nc.vector.tensor_scalar(weight[:, H, :], weight[:, H, :], 1.0, None, ALU.max))
            link(nc.vector.reciprocal(b[:, :, :], weight[:, 0:HS, :]))
            if layer == 0:
                tt(weight[:, 0:H, :], a[:, 0:H, :], b[:, 0:H, :], ALU.mult).then_inc(s_deg, 1)
            else:
                link(tt(weight[:, 0, :], a[:, 0, :], b[:, 0, :], ALU.mult))
                tt(weight[:, 0, :], weight[:, 0, :], m["norm"][:, :], ALU.mult)


def row_of(rows, t):
    return rows[:, ds(1 + t, 1), :].rearrange("p a d -> p (a d)")


def pick_heads(nc, m, t, head):
    nc.scalar.activation(m["scrap"][:, 2 + t.slot():3 + t.slot()], m["eps_col"][:, :], ACT.Copy)
    for j in range(G):
        last = nc.scalar.activation(head[:, j, :], row_of(m["rows"], G * t.g + j), ACT.Copy,
                                    scale=m["head_end"][:, ds(G * t.g + j, 1)])
    return last


def add_heads(nc, m, out, head):
    for j in range(G):
        last = nc.tensor.matmul(out[:, 0:D], m["ident"][:, :], head[:, j, :], start=False, stop=False,
                                skip_group_check=True)
    return last


def sum_layer0(nc, m):
    rows, ident, weight, coef = m["rows"], m["ident"], m["weight"], m["coef"]
    with ExitStack() as c:
        new_sem = c.enter_context(phase_sems(nc))

        def sb(name, shape, dt=F32):
            return c.enter_context(nc.sbuf_tensor(f"{name}_s0", shape, dt))

        def sems(name, n=2):
            return [new_sem(f"{name}_s0{k}") for k in range(n)]

        xd = sb("xd", [P, 4, G, D])
        z = sb("z", [P, 2, G, D])
        x1 = sb("x1", [P, 4, G, D])
        head = sb("head", [P, 2, G, D])
        st = sb("st", [P, 2, G, 6])
        mv = sb("mv", [P, 2, 3, G])
        sd = sb("sd", [P, 2, G])
        rstd = sb("rstd", [P, 2, G])
        shift = sb("shift", [P, 2, G])
        idx = sb("idx", [P, 4, G], I32)
        hot = sb("hot", [P, 2, G, RELS])
        hot_t = sb("hot_t", [P, 2, P])
        ps_h = c.enter_context(nc.psum_tensor("ps_h_s0", [P, 2, 512], F32))
        ps_c = c.enter_context(nc.psum_tensor("ps_c_s0", [P, 2, 512], F32))
        ps_t = c.enter_context(nc.psum_tensor("ps_t_s0", [P, G * P], F32))
        ps_l = c.enter_context(nc.psum_tensor("ps_l_s0", [P, 512], F32))
        x1_t = sb("x1_t", [P, G * P])
        ps_f = c.enter_context(nc.psum_tensor("ps_f_s0", [P, 512], F32))
        stats_ready, sd_ready, scale_ready, normed, hot_ready, hot_turned, hot_sb, coef_ps, coef_done = (
            sems(n) for n in ("stats_ready", "sd_ready", "scale_ready", "normed", "hot_ready", "hot_turned",
                              "hot_sb", "coef_ps", "coef_done"))
        head_ready, head_used = sems("head_ready"), sems("head_used")
        xd_in, xd_used, sent = sems("xd_in", 4), sems("xd_used", 4), sems("sent", 4)
        saved = sems("saved", 4)
        s_sum, s_stat, s_idx, s_tail, s_carried, s_turned, s_turned_sb, s_logits, s_masked = (
            sems(n, 1)[0] for n in ("sum", "stat", "idx_ready", "tail", "carried", "turned", "turned_sb", "logits",
                                    "masked"))
        block = c.enter_context(nc.Block())
        SUMS = 1 + G
        STATS = 4

        @block.sync
        def _(sp):
            def load(t):
                s4, u4 = t.slot(4), t.uses(4)
                sp.wait_ge(xd_used[s4], u4)
                sp.dma_start(xd[:, s4, :, :], m["xd_kept"][0][:, ds(G * t.g, G), :]).then_inc(xd_in[s4], 16)

            def save(t, col, n):
                s4 = t.slot(4)
                sp.wait_ge(normed[t.slot()], t.uses() + 1)
                sp.dma_start(m["xd_kept"][1][:, ds(col, n), :], x1[:, s4, 0:n, :]).then_inc(saved[s4], 16)

            def step(t, _, __, ppp):
                if t:
                    load(t)
                if ppp:
                    save(ppp, G * ppp.g, G)
            in_turns(sp, lambda t: step(*t.back(3)), peeled=2)
            f4, n4 = FIX_TURN.slot(4), FIX_TURN.uses(4)
            sp.wait_ge(xd_used[f4], n4)
            sp.dma_start(xd[:, f4, 0, :], m["xd_kept"][0][:, 0, :]).then_inc(xd_in[f4], 16)
            for turns in behind_last(3):
                step(*turns)
            save(FIX_TURN, T, 1)
            for s in range(4):
                sp.wait_ge(saved[s], 16 * (len(range(s, NG, 4)) + (s == f4)))

        @block.vector
        def _(dve):
            def residual(t, row, n):
                s, u, s4, u4 = t.slot(), t.uses(), t.slot(4), t.uses(4)
                dve.wait_ge(xd_in[s4], 16 * (u4 + 1))
                dve.wait_ge(normed[s], u)
                nc.vector.scalar_tensor_tensor(z[:, s, 0:n, :], row, 0.0, xd[:, s4, 0:n, :], ALU.max, ALU.add)\
                    .then_inc(xd_used[s4], 1)

            def scale_of(t, link, n):
                dve.wait_ge(sd_ready[t.slot()], t.uses() + 1)
                link(nc.vector.reciprocal(rstd[:, t.slot(), 0:n], sd[:, t.slot(), 0:n]), wait=False)

            def shift_of(t, n):
                s = t.slot()
                nc.vector.scalar_tensor_tensor(shift[:, s, 0:n], mv[:, s, 2, 0:n], -0.5, rstd[:, s, 0:n],
                                               ALU.mult, ALU.mult).then_inc(scale_ready[s], 1)

            def mask_logits(t):
                dve.wait_ge(s_logits, t.g + 1)
                nc.vector.tensor_tensor(m["dst_logits"][:, ds(G * t.g, G), :],
                                        ps_l[:, 0:G * RELS].rearrange("p (j r) -> p j r", j=G),
                                        m["valid"][:, ds(G * t.g, G)].unsqueeze(2).to_broadcast([P, G, RELS]),
                                        ALU.mult).then_inc(s_masked, 1)

            def step(t, p, pp, _, pppp):
                if t:
                    sums = LoopChain(dve, s_sum, SUMS, t.g)
                    wv = rows[:, ds(1 + G * t.g, G), :].rearrange("p j (h d) -> p j h d", h=HEADS)
                    sums(nc.vector.tensor_tensor(
                        wv, wv, weight[:, 0:HEADS, ds(G * t.g, G)].rearrange("p h j -> p j h").unsqueeze(3)
                        .to_broadcast([P, G, HEADS, DK]), ALU.mult), wait=False)
                if pp:
                    link = LoopChain(dve, s_stat, STATS, pp.g)
                    link.n = STATS - 1
                    scale_of(pp, link, G)
                if p:
                    dve.wait_ge(s_sum, SUMS * (p.g + 1))
                    residual(p, rows[:, ds(1 + G * p.g, G), :], G)
                if pp:
                    link.wait(STATS)
                    shift_of(pp, G)
                if p:
                    s = p.slot()
                    link = LoopChain(dve, s_stat, STATS, p.g)
                    dve.wait_ge(xd_used[p.slot(4)], p.uses(4) + 1)
                parts, last = row_stats_steps(nc, st[:, p.slot(), :, :], mv[:, p.slot(), :, :], P,
                                              z[:, p.slot(), :, :], G) if p else ((), None)
                for j in range(G):
                    if t:
                        sums.wait(sums.n)
                        sums(nc.vector.scalar_tensor_tensor(
                            row_of(rows, G * t.g + j), row_of(rows, G * t.g + j - 1), m["cont"][:, ds(G * t.g + j, 1)],
                            row_of(rows, G * t.g + j), ALU.mult, ALU.add), wait=False)
                    if p and j < 2:
                        ins = parts[0](2 * j, 2 * j + 2)
                        if j == 1:
                            link(ins, wait=False)
                    elif p:
                        link.wait(link.n)
                        link(parts[j - 1](), wait=False)
                if pppp:
                    mask_logits(pppp)
                if t:
                    sums.end()
                    s = t.slot()
                    dve.wait_ge(hot_turned[s], t.uses())
                    nc.vector.tensor_tensor(hot[:, s, :, :],
                                            m["iota_rel"][:, :].unsqueeze(1).to_broadcast([P, G, RELS]),
                                            m["rel_f"][:, ds(G * t.g, G)].unsqueeze(2).to_broadcast([P, G, RELS]),
                                            ALU.is_equal).then_inc(hot_ready[s], 1)
                if p:
                    s = p.slot()
                    link.wait(link.n)
                    last().then_inc(stats_ready[s], 1)
                    dve.wait_ge(coef_ps[s], p.uses() + 1)
                    nc.vector.tensor_scalar(coef[:, ds(G * p.g, G), :], ps_c[:, s, 0:G * BASES]
                                            .rearrange("p (j b) -> p j b", j=G), 1.0, None, ALU.mult)\
                        .then_inc(coef_done[s], 1)

            in_turns(dve, lambda t: step(*t.back(4)), peeled=2)
            for turns in behind_last(4):
                step(*turns)
            link = Chain(dve, s_tail)
            dve.wait_ge(s_carried, 1)
            link(nc.vector.tensor_copy(rows[:, FIX, :], ps_f[:, 0:D]))
            residual(FIX_TURN, rows[:, FIX:FIX + 1, :], 1)
            s, s4 = FIX_TURN.slot(), FIX_TURN.slot(4)
            dve.wait_ge(xd_used[s4], FIX_TURN.uses(4) + 1)
            row_stats(nc, link, st[:, s, :, :], mv[:, s, :, :], P, z[:, s, :, :], 1).then_inc(stats_ready[s], 1)
            scale_of(FIX_TURN, lambda ins, wait: link(ins), 1)
            shift_of(FIX_TURN, 1)
            dve.wait_ge(s_logits, NG + 1)
            nc.vector.tensor_scalar(m["logits_fix"][:, :], ps_l[:, 0:RELS], m["valid"][:, T:T + 1], None, ALU.mult)

        @block.tensor
        def _(pe):
            def turn_rows(t, n=G):
                pe.wait_ge(normed[t.slot()], t.uses() + 1)
                pe.wait_ge(s_turned_sb, t.g)
                for j in range(n):
                    last = nc.tensor.transpose(ps_t[:, j * P:(j + 1) * P], x1[:, t.slot(4), j, :], ident[:, :])
                last.then_inc(s_turned, 1)

            def products(t, n=G):
                pe.wait_ge(s_turned_sb, t.g + 1)
                pe.wait_ge(s_masked, t.g)
                for j in range(n):
                    last = nc.tensor.matmul(ps_l[:, j * RELS:(j + 1) * RELS], x1_t[:, j * P:(j + 1) * P],
                                            m["a_sb"][:, :], start=True, stop=True)
                last.then_inc(s_logits, 1)

            def step(t, p, pp, ppp):
                if t:
                    s, u = t.slot(), t.uses()
                    pe.wait_ge(hot_ready[s], u + 1)
                    pe.wait_ge(hot_sb[s], u)
                    nc.tensor.transpose(ps_h[:, s, 0:P], hot[:, s, :, :].rearrange("p j r -> p (j r)"), ident[:, :])\
                        .then_inc(hot_turned[s], 1)
                if p:
                    pe.wait_ge(head_ready[p.slot()], p.uses() + 1)
                    add_heads(nc, m, ps_f, head[:, p.slot(), :, :]).then_inc(head_used[p.slot()], 1)
                if ppp:
                    products(ppp)
                if t:
                    pe.wait_ge(hot_sb[s], u + 1)
                    pe.wait_ge(coef_done[s], u)
                    nc.tensor.matmul(ps_c[:, s, 0:G * BASES], hot_t[:, s, :], m["coef_blocks"][:, :], start=True,
                                     stop=True).then_inc(coef_ps[s], 1)
                if pp:
                    turn_rows(pp)
            nc.tensor.matmul(ps_f[:, 0:D], ident[:, :], rows[:, 0, :], start=True, stop=False, skip_group_check=True)
            in_turns(pe, lambda t: step(*t.back(3)), peeled=2)
            turns = behind_last(3)
            step(*turns[0])
            pe.wait_ge(s_sum, SUMS * NG)
            nc.tensor.matmul(ps_f[:, 0:D], m["carried_by"][:, :], rows[:, T, :], start=False, stop=True,
                             skip_group_check=True).then_inc(s_carried, 1)
            step(*turns[1])
            step(*turns[2])
            turn_rows(FIX_TURN, 1)
            products(FIX_TURN, 1)

        @block.scalar
        def _(act):
            def normalise(t, n):
                s, u, s4, u4 = t.slot(), t.uses(), t.slot(4), t.uses(4)
                act.wait_ge(scale_ready[s], u + 1)
                act.wait_ge(sent[s4], 16 * G * u4)
                act.wait_ge(saved[s4], 16 * u4)
                if not t.starts:
                    act.wait_ge(s_turned, t.g - 3)
                for j in range(n):
                    last = nc.scalar.activation(x1[:, s4, j, :], z[:, s, j, :], ACT.Identity,
                                                bias=shift[:, s, j:j + 1], scale=rstd[:, s, j:j + 1])
                last.then_inc(normed[s], 1)

            def deviation(t, n):
                s, u = t.slot(), t.uses()
                act.wait_ge(stats_ready[s], u + 1)
                nc.scalar.activation(sd[:, s, 0:n], mv[:, s, 1, 0:n], ACT.Sqrt, bias=m["eps_col"][:, :],
                                     scale=1.0 / D).then_inc(sd_ready[s], 1)

            def turned_out(t, n=G):
                act.wait_ge(s_turned, t.g + 1)
                act.wait_ge(s_logits, t.g)
                nc.scalar.activation(x1_t[:, 0:n * P], ps_t[:, 0:n * P], ACT.Copy).then_inc(s_turned_sb, 1)

            def step(t, p, pp, ppp):
                if pp:
                    normalise(pp, G)
                if p:
                    act.wait_ge(head_used[p.slot()], p.uses())
                    act.wait_ge(s_sum, SUMS * (p.g + 1))
                    pick_heads(nc, m, p, head[:, p.slot(), :, :]).then_inc(head_ready[p.slot()], 1)
                if ppp:
                    turned_out(ppp)
                if t:
                    s, u = t.slot(), t.uses()
                    act.wait_ge(hot_turned[s], u + 1)
                    act.wait_ge(coef_ps[s], u)
                    nc.scalar.activation(hot_t[:, s, :], ps_h[:, s, 0:P], ACT.Copy).then_inc(hot_sb[s], 1)
                if p:
                    deviation(p, G)
            in_turns(act, lambda t: step(*t.back(3)), peeled=2)
            for turns in behind_last(3):
                step(*turns)
            deviation(FIX_TURN, 1)
            normalise(FIX_TURN, 1)
            turned_out(FIX_TURN, 1)

        @block.gpsimd
        def _(pool):
            def scatter(t, col, n):
                s, u, s4, u4 = t.slot(), t.uses(), t.slot(4), t.uses(4)
                pool.wait_ge(sent[s4], 16 * G * u4)
                carry_wait(nc, m)
                nc.gpsimd.tensor_copy(idx[:, s4, 0:n], m["scatter_idx"][:, ds(col, n)]).then_inc(s_idx, 1)
                pool.wait_ge(s_idx, t.g + 1)
                pool.wait_ge(normed[s], u + 1)
                carry_wait(nc, m, 1)
                for j in range(n):
                    nc.gpsimd.indirect_dma_start(
                        out=m["x1_table"][:, :],
                        out_offset=bass.IndirectOffsetOnAxis(ap=idx[:, s4, j:j + 1], axis=0),
                        in_=x1[:, s4, j, :], in_offset=None, bounds_check=NODES - 1, oob_is_err=False,
                    ).then_inc(sent[s4], 16)
            in_turns(pool, lambda t: scatter(t, G * t.g, G))
            scatter(FIX_TURN, T, 1)
            for s in range(4):
                groups, fix = len(range(s, NG, 4)), s == FIX_TURN.slot(4)
                pool.wait_ge(sent[s], 16 * (G * groups + fix))


def messages(nc, m):
    rows, ident, att, gather_idx, coef = m["rows"], m["ident"], m["att"], m["gather_idx"], m["coef"]
    with ExitStack() as c:
        new_sem = c.enter_context(phase_sems(nc))

        def sb(name, shape, dt=F32):
            return c.enter_context(nc.sbuf_tensor(f"{name}_m", shape, dt))

        def sems(name, n=2):
            return [new_sem(f"{name}_m{k}") for k in range(n)]

        def ps(name, shape):
            return c.enter_context(nc.psum_tensor(f"{name}_m", shape, F32))

        idx = sb("idx", [P, 4, G], I32)
        ends = sb("gathered", [P, 4, G, D])
        ends_t = sb("gathered_t", [P, 2, G * P])
        hot = sb("hot", [P, 2, G, RELS])
        sel = sb("sel", [P, 2, G, RELS])
        even = sb("even", [P, 2, D])
        odd = sb("odd", [P, 2, D])
        coef_g = sb("coef_g", [P, 2, G, BASES])
        dst_logits = m["dst_logits"]
        by_t = sb("carried_by_t", [P, P])
        zeros = sb("zeros", [P, CH, D])
        ps_t = ps("ps_t", [P, G * P])
        ps_p = ps("ps_p", [P, 2, 2, BASES // 2, D])
        ps_s = ps("ps_s", [P, 512])
        fetched = sems("fetched", 4)
        turned, turned_sb, scored, score_done, coef_ready, begun, row_done = (
            sems(n) for n in ("turned", "turned_sb", "scored", "score_done", "coef_ready", "begun", "row_done"))
        based = [sems(f"based{h}_") for h in range(2)]
        p_free = [sems(f"p_free{h}_") for h in range(2)]
        idx_ready, s_chain, s_set, s_zeroed, by_turned, by_sb, l_carried, s_first = (
            sems(n, 1)[0] for n in ("idx_ready", "chain", "set", "zeroed", "by_turned", "by_sb", "l_carried",
                                    "first"))
        block = c.enter_context(nc.Block())
        PER = 3 + G * 4

        @block.gpsimd
        def _(pool):
            def gather(t):
                s4, u4 = t.slot(4), t.uses(4)
                pool.wait_ge(fetched[s4], 64 * u4)
                if not t.starts:
                    pool.wait_ge(turned[t.slot()], t.uses() - 1)
                nc.gpsimd.tensor_copy(idx[:, s4, :], gather_idx[:, ds(t.g, 1), 0:G].rearrange("p a j -> p (a j)"))\
                    .then_inc(idx_ready, 1)
                pool.wait_ge(idx_ready, t.g + 1)
                carry_wait(nc, m)
                for j in range(G):
                    nc.gpsimd.indirect_dma_start(
                        out=ends[:, s4, j, :], out_offset=None, in_=m["x1_table"][:, :],
                        in_offset=bass.IndirectOffsetOnAxis(ap=idx[:, s4, j:j + 1], axis=0),
                    ).then_inc(fetched[s4], 16)
            in_turns(pool, gather)

        @block.sync
        def _(sp):
            def move(t):
                sp.wait_ge(turned[t.slot()], t.uses() + 1)
                sp.dma_start(m["delta_table"][ds(t.g * CHUNK, t.np * CH), :].rearrange("(p j) d -> p j d", j=CH),
                             zeros[0:t.np, :, :]).then_inc(s_zeroed, 16)
            sp.wait_ge(s_set, 1)
            in_turns(sp, move)
            sp.wait_ge(s_zeroed, 16 * NG)

        @block.tensor
        def _(pe):
            mm = nc.tensor.matmul

            def turn_rows(t):
                s, s4 = t.slot(), t.slot(4)
                pe.wait_ge(fetched[s4], 64 * (t.uses(4) + 1))
                pe.wait_ge(turned_sb[1 - s], t.uses() + s)
                for j in range(G):
                    last = nc.tensor.transpose(ps_t[:, j * P:(j + 1) * P], ends[:, s4, j, :], ident[:, :])
                last.then_inc(turned[s], 1)

            def body(t):
                s, u, np = t.slot(), t.uses(), t.np
                pe.wait_ge(turned_sb[s], u + 1)
                pe.wait_ge(score_done[1 - s], t.uses() + s)
                for j in range(G):
                    last = mm(ps_s[:, j * RELS:(j + 1) * RELS], ends_t[:, s, j * P:(j + 1) * P], m["a_sb"][:, :],
                              start=True, stop=True)
                last.then_inc(scored[s], 1)
                for j in range(G):
                    if j == G // 2:
                        if t.next():
                            turn_rows(t.next())
                    s_t = ends_t[:, s, j * P:(j + 1) * P]
                    for half in range(2):
                        pe.wait_ge(p_free[half][j % 2], t.g * (G // 2) + j // 2)
                        last = mm(ps_p[:, j % 2, half, :, :], s_t, m["bases_sb"][:, half * 512:(half + 1) * 512],
                                  start=True, stop=True)
                        last.then_inc(based[half][j % 2], 1)

            nc.tensor.transpose(ps_s[:, 2 * P:3 * P], m["carried_by"][:, :], ident[:, :]).then_inc(by_turned, 1)
            pe.wait_ge(by_sb, 1)
            mm(ps_s[:, 3 * P:3 * P + RELS], by_t[:, :], m["logits_fix"][:, :], start=True, stop=True)\
                .then_inc(l_carried, 1)
            turn_rows(Turn(0, 0))
            pe.wait_ge(s_first, 2)
            in_turns(pe, body)

        def coefs(t, j, b):
            return coef_g[:, t.slot(), j, b:b + 1]

        def row_of(g, j):
            return rows[:, ds(1 + G * g + j, 1), :].rearrange("p a d -> p (a d)")

        @block.scalar
        def _(act):
            def turned_out(t):
                s, u = t.slot(), t.uses()
                act.wait_ge(turned[s], u + 1)
                nc.scalar.activation(ends_t[:, s, :], ps_t[:, :], ACT.Copy).then_inc(turned_sb[s], 1)

            def body(t):
                act.wait_ge(coef_ready[t.slot()], t.uses() + 1)
                for j in range(G):
                    if j == G // 2 and t.next():
                        turned_out(t.next())
                    n = t.g * (G // 2) + j // 2
                    act.wait_ge(based[0][j % 2], n + 1)
                    act.wait_ge(row_done[j % 2], n)
                    nc.scalar.activation(even[:, j % 2, :], ps_p[:, j % 2, 0, 0, :], ACT.Copy, scale=coefs(t, j, 0))
                    nc.scalar.activation(odd[:, j % 2, :], ps_p[:, j % 2, 0, 1, :], ACT.Copy,
                                         scale=coefs(t, j, 1)).then_inc(begun[j % 2], 1)
            turned_out(Turn(0, 0))
            in_turns(act, body)

        @block.vector
        def _(dve):
            dve.wait_ge(by_turned, 1)
            nc.vector.tensor_copy(by_t[:, :], ps_s[:, 2 * P:3 * P]).then_inc(by_sb, 1)
            first = Chain(dve, s_first)
            fix = m["logits_fix"]
            for r in range(RELS):
                last = nc.vector.scalar_tensor_tensor(dst_logits[:, :, r], m["head_end"][:, :], fix[:, r:r + 1],
                                                      dst_logits[:, :, r], ALU.mult, ALU.add)
            first(last)
            dve.wait_ge(l_carried, 1)
            first(nc.vector.tensor_tensor(dst_logits[:, T - 1, :], dst_logits[:, T - 1, :],
                                          ps_s[:, 3 * P:3 * P + RELS], ALU.add))
            for r in range(RELS):
                backwards = dst_logits[:, ::-1, r]
                last = nc.vector.tensor_tensor_scan(backwards, m["more"][:, ::-1], backwards, 0.0, ALU.mult, ALU.add)
            first(last)

            def copy_coefs(t):
                nc.vector.tensor_scalar(coef_g[:, t.slot(), :, :], coef[:, ds(G * t.g, G), :], 1.0, None, ALU.mult)\
                    .then_inc(coef_ready[t.slot()], 1)

            def add(t, j, b):
                out = (even, odd)[b % 2][:, j % 2, :]
                return nc.vector.scalar_tensor_tensor(out, ps_p[:, j % 2, b // 4, b % 4, :], coefs(t, j, b), out,
                                                      ALU.mult, ALU.add)

            def join(t, j):
                dve.wait_ge(p_free[1][j % 2], t.g * (G // 2) + j // 2 + 1)
                nc.vector.tensor_tensor(row_of(t.g, j), even[:, j % 2, :], odd[:, j % 2, :], ALU.add)\
                    .then_inc(row_done[j % 2], 1)

            def body(t):
                s, u, g = t.slot(), t.uses(), t.g
                link = LoopChain(dve, s_chain, PER, g)
                dve.wait_ge(coef_ready[s], u + 1)
                for j in range(G):
                    n = g * (G // 2) + j // 2
                    dve.wait_ge(begun[j % 2], n + 1)
                    link(add(t, j, 2), wait=False)
                    two = link.n
                    add(t, j, 3).then_inc(p_free[0][j % 2], 1)
                    if j > 0:
                        join(t, j - 1)
                    elif t.prev():
                        join(t.prev(), G - 1)
                    if j == 0:
                        link(nc.vector.tensor_tensor(hot[:, s, :, :],
                                                     m["iota_rel"][:, :].unsqueeze(1).to_broadcast([P, G, RELS]),
                                                     m["rel_f"][:, ds(G * g, G)].unsqueeze(2).to_broadcast([P, G, RELS]),
                                                     ALU.is_equal), wait=False)
                    if j == 2 and t.next():
                        copy_coefs(t.next())
                    dve.wait_ge(based[1][j % 2], n + 1)
                    link.wait(two)
                    link(add(t, j, 4), wait=False)
                    four = link.n
                    dve.wait_ge(p_free[0][j % 2], n + 1)
                    link(add(t, j, 5), wait=False)
                    five = link.n
                    if j == 0:
                        dve.wait_ge(scored[s], u + 1)
                        link(nc.vector.tensor_tensor(sel[:, s, :, :],
                                                     ps_s[:, 0:G * RELS].rearrange("p (j r) -> p j r", j=G),
                                                     dst_logits[:, ds(G * g, G), :], ALU.add), wait=False)
                        both = link.n
                    if j == 1:
                        link.wait(both)
                        link(nc.vector.tensor_tensor(sel[:, s, :, :], sel[:, s, :, :], hot[:, s, :, :], ALU.mult),
                             wait=False)
                        picked = link.n
                    link.wait(four)
                    link(add(t, j, 6), wait=False)
                    link.wait(five)
                    add(t, j, 7).then_inc(p_free[1][j % 2], 1)
                    if j == 1:
                        link.wait(picked)
                        nc.vector.tensor_reduce(att[:, 0, ds(G * g, G)], sel[:, s, :, :], AX.X, ALU.add)\
                            .then_inc(score_done[s], 1)
                link.end()
            nc.vector.memset(zeros[:, :, :], 0.0).then_inc(s_set, 1)
            copy_coefs(Turn(0, 0))
            in_turns(dve, body)
            join(Turn(NG // UNROLL, 0), G - 1)


def sum_layer1(nc, m):
    rows, ident, weight, valid = m["rows"], m["ident"], m["weight"], m["valid"]
    with ExitStack() as c:
        new_sem = c.enter_context(phase_sems(nc))

        def sb(name, shape, dt=F32):
            return c.enter_context(nc.sbuf_tensor(f"{name}_s1", shape, dt))

        def sems(name, n=2):
            return [new_sem(f"{name}_s1{k}") for k in range(n)]

        def ps(name):
            return c.enter_context(nc.psum_tensor(f"{name}_s1", [P, 512], F32))

        xd = sb("xd", [P, 4, G, D])
        delta = sb("delta", [P, 4, G, D + 1])
        head = sb("head", [P, 2, G, D])
        xg = sb("xg", [P, 2, CH, D + 1])
        idx = sb("idx", [P, 4, G], I32)
        ps_g, ps_xd, ps_dd, ps_f = ps("ps_g"), ps("ps_xd"), ps("ps_dd"), ps("ps_f")
        head_ready, head_used, x_in, grammed = (sems(n) for n in ("head_ready", "head_used", "x_in", "grammed"))
        xd_in, summed, masked, sent = sems("xd_in", 4), sems("summed", 4), sems("masked", 4), sems("sent", 4)
        s_sum, s_weighed, s_set, s_idx, s_carried, s_all = (sems(n, 1)[0] for n in (
            "sum", "weighed", "set", "idx_ready", "carried", "all"))
        block = c.enter_context(nc.Block())
        f4, n4 = FIX_TURN.slot(4), FIX_TURN.uses(4)

        @block.sync
        def _(sp):
            def load(t):
                s, u, s4, u4 = t.slot(), t.uses(), t.slot(4), t.uses(4)
                sp.wait_ge(grammed[s], u)
                sp.dma_start(xg[0:t.np, s, :, 0:D], m["x1_table"][ds(t.g * CHUNK, t.np * CH), :]
                             .rearrange("(p j) d -> p j d", j=CH)).then_inc(x_in[s], 16)
                sp.wait_ge(summed[s4], u4)
                sp.dma_start(xd[:, s4, :, :], m["xd_kept"][1][:, ds(G * t.g, G), :]).then_inc(xd_in[s4], 16)
            in_turns(sp, load)
            sp.wait_ge(summed[f4], n4)
            sp.dma_start(xd[:, f4, 0, :], m["xd_kept"][1][:, T, :]).then_inc(xd_in[f4], 16)

        @block.tensor
        def _(pe):
            def add(out, lhs_t, rhs):
                return nc.tensor.matmul(out, lhs_t, rhs, start=False, stop=False, skip_group_check=True)

            def products(t, n=G):
                s4, u4 = t.slot(4), t.uses(4)
                pe.wait_ge(xd_in[s4], 16 * (u4 + 1))
                pe.wait_ge(masked[s4], u4 + 1)
                for j in range(n):
                    add(ps_xd[:, 0:D], xd[:, s4, j, :], delta[:, s4, j, 0:D])
                    last = add(ps_dd[:, 0:D + 1], delta[:, s4, j, 0:D], delta[:, s4, j, :])
                last.then_inc(summed[s4], 1)

            def body(t):
                s, u = t.slot(), t.uses()
                pe.wait_ge(x_in[s], 16 * (u + 1))
                for j in range(CH):
                    last = add(ps_g[:, 0:D + 1], xg[0:t.np, s, j, 0:D], xg[0:t.np, s, j, :])
                last.then_inc(grammed[s], 1)
                pe.wait_ge(head_ready[s], u + 1)
                add_heads(nc, m, ps_f, head[:, s, :, :]).then_inc(head_used[s], 1)
                products(t)

            def zeros(start):
                for out in (ps_g, ps_xd, ps_dd):
                    last = nc.tensor.matmul(out[:, 0:D + 1], ident[:, :], rows[:, 0, 0:1].to_broadcast([P, D + 1]),
                                            start=start, stop=not start, skip_group_check=True)
                return last
            zeros(True)
            nc.tensor.matmul(ps_f[:, 0:D], ident[:, :], rows[:, 0, :], start=True, stop=False, skip_group_check=True)
            pe.wait_ge(s_set, 1)
            in_turns(pe, body)
            pe.wait_ge(s_sum, G * NG)
            nc.tensor.matmul(ps_f[:, 0:D], m["carried_by"][:, :], rows[:, T, :], start=False, stop=True,
                             skip_group_check=True).then_inc(s_carried, 1)
            products(FIX_TURN, 1)
            zeros(False).then_inc(s_all, 1)

        @block.scalar
        def _(act):
            def body(t):
                s, u, s4, u4 = t.slot(), t.uses(), t.slot(4), t.uses(4)
                act.wait_ge(head_used[s], u)
                act.wait_ge(sent[s4], 16 * G * u4)
                act.wait_ge(summed[s4], u4)
                act.wait_ge(s_sum, G * (t.g + 1))
                pick_heads(nc, m, t, head[:, s, :, :]).then_inc(head_ready[s], 1)
                for j in range(G):
                    nc.scalar.activation(delta[:, s4, j, 0:D], row_of(rows, G * t.g + j), ACT.Copy,
                                         scale=valid[:, ds(G * t.g + j, 1)])
                nc.scalar.activation(delta[:, s4, :, D], valid[:, ds(G * t.g, G)], ACT.Copy).then_inc(masked[s4], 1)
            in_turns(act, body)

        @block.vector
        def _(dve):
            def weigh(t):
                mine = rows[:, ds(1 + G * t.g, G), :]
                nc.vector.tensor_tensor(mine, mine, weight[:, 0, ds(G * t.g, G)].unsqueeze(2).to_broadcast([P, G, D]),
                                        ALU.mult).then_inc(s_weighed, 1)

            def body(t):
                sums = LoopChain(dve, s_sum, G, t.g)
                dve.wait_ge(s_weighed, t.g + 1)
                for j in range(G):
                    sums.wait(sums.n)
                    sums(nc.vector.scalar_tensor_tensor(
                        row_of(rows, G * t.g + j), row_of(rows, G * t.g + j - 1), m["cont"][:, ds(G * t.g + j, 1)],
                        row_of(rows, G * t.g + j), ALU.mult, ALU.add), wait=False)
                    if j == 0 and t.next():
                        weigh(t.next())
                sums.end()
            nc.vector.memset(xg[:, 0, :, D:D + 1], 1.0)
            nc.vector.memset(xg[:, 1, :, D:D + 1], 1.0).then_inc(s_set, 1)
            weigh(Turn(0, 0))
            in_turns(dve, body)
            dve.wait_ge(s_carried, 1)
            dve.wait_ge(sent[f4], 16 * G * n4)
            dve.wait_ge(summed[f4], n4)
            nc.vector.tensor_copy(delta[:, f4, 0, D:D + 1], valid[:, T:T + 1])
            nc.vector.tensor_scalar(delta[:, f4, 0, 0:D], ps_f[:, 0:D], valid[:, T:T + 1], None, ALU.mult)\
                .then_inc(masked[f4], 1)
            dve.wait_ge(s_all, 1)
            nc.vector.tensor_copy(m["gram_sb"][:, :], ps_g[:, 0:D + 1])
            nc.vector.tensor_copy(m["xd_sb"][:, :], ps_xd[:, 0:D])
            nc.vector.tensor_copy(m["dd_sb"][:, :], ps_dd[:, 0:D + 1])

        @block.gpsimd
        def _(pool):
            def scatter(t, col, n):
                s4, u4 = t.slot(4), t.uses(4)
                pool.wait_ge(sent[s4], 16 * G * u4)
                carry_wait(nc, m)
                nc.gpsimd.tensor_copy(idx[:, s4, 0:n], m["scatter_idx"][:, ds(col, n)]).then_inc(s_idx, 1)
                pool.wait_ge(s_idx, t.g + 1)
                pool.wait_ge(masked[s4], u4 + 1)
                carry_wait(nc, m, 1)
                for j in range(n):
                    nc.gpsimd.indirect_dma_start(
                        out=m["delta_table"][:, :],
                        out_offset=bass.IndirectOffsetOnAxis(ap=idx[:, s4, j:j + 1], axis=0),
                        in_=delta[:, s4, j, 0:D], in_offset=None, bounds_check=NODES - 1, oob_is_err=False,
                    ).then_inc(sent[s4], 16)
            in_turns(pool, lambda t: scatter(t, G * t.g, G))
            scatter(FIX_TURN, T, 1)
            for s in range(4):
                groups, fix = len(range(s, NG, 4)), s == f4
                pool.wait_ge(sent[s], 16 * (G * groups + fix))


def centre(nc, m):
    with ExitStack() as c:
        new_sem = c.enter_context(phase_sems(nc))

        def sb(name, shape, dt=F32):
            return c.enter_context(nc.sbuf_tensor(f"{name}_c", shape, dt))

        def sem(name):
            return new_sem(f"{name}_c")

        mean_x = sb("mean_x", [D, 1])
        mean_d = sb("mean_d", [D, 1])
        x_row = sb("x_row", [1, D])
        d_row = sb("d_row", [3, D])
        gram_n = sb("gram_n", [D, D])
        cross = sb("cross", [D, D])
        own = sb("own", [D, D])
        cov = sb("cov", [D, D])
        cw = sb("cw", [D, D])
        mu = sb("mu", [3, D])
        ps_rows = c.enter_context(nc.psum_tensor("ps_rows_c", [P, 512], F32))
        ps_outer = c.enter_context(nc.psum_tensor("ps_outer_c", [P, 2, 512], F32))
        ps_cw = c.enter_context(nc.psum_tensor("ps_cw_c", [P, 512], F32))
        ps_var = c.enter_context(nc.psum_tensor("ps_var_c", [P, 512], F32))
        s_dve, s_mean, s_row, s_row_sb, s_outer, s_cov, s_cw, s_cw_sb, s_var = (sem(n) for n in (
            "s_dve", "s_mean", "s_row", "s_row_sb", "s_outer", "s_cov", "s_cw", "s_cw_sb", "s_var"))
        block = c.enter_context(nc.Block())

        @block.vector
        def _(dve):
            link = Chain(dve, s_dve)
            ts, tt, stt = nc.vector.tensor_scalar, nc.vector.tensor_tensor, nc.vector.scalar_tensor_tensor
            ts(mean_d[:, :], m["dd_sb"][:, D:D + 1], 1.0 / NODES, None, ALU.mult)
            ts(mean_x[:, :], m["gram_sb"][:, D:D + 1], 1.0 / NODES, None, ALU.mult).then_inc(s_mean, 1)
            ts(gram_n[:, :], m["gram_sb"][:, 0:D], 1.0 / NODES, None, ALU.mult)
            ts(cross[:, :], m["xd_sb"][:, :], 1.0 / NODES, None, ALU.mult)
            link(stt(own[:, :], m["dd_sb"][:, 0:D], 1.0 / NODES, m["ident"][:, :], ALU.mult, ALU.mult))
            dve.wait_ge(s_row, 1)
            nc.vector.tensor_copy(d_row[:, :], ps_rows[0:3, 2 * D:3 * D])
            nc.vector.tensor_copy(x_row[:, :], ps_rows[0:1, 0:D]).then_inc(s_row_sb, 1)
            dve.wait_ge(s_row_sb, 1)
            link(tt(mu[:, :], ps_rows[0:3, D:2 * D], m["vec_rows"][:, 0, :], ALU.add))
            link(tt(mu[:, :], mu[:, :], d_row[:, :], ALU.add))
            link(tt(m["centre_row"][:, :], m["vec_rows"][:, 0, :], mu[:, :], ALU.subtract))
            dve.wait_ge(s_outer, 1)
            tt(cov[:, :], gram_n[:, :], ps_outer[:, 0, 0:D], ALU.subtract).then_inc(s_cov, 1)
            link(tt(cross[:, :], cross[:, :], ps_outer[:, 1, 0:D], ALU.subtract))
            dve.wait_ge(s_cw, 1)
            link(stt(cw[:, :], cross[:, :], 2.0, ps_cw[:, 0:D], ALU.mult, ALU.add))
            link(tt(cw[:, :], cw[:, :], m["wloop_sb"][:, :], ALU.mult))
            tt(cw[:, :], cw[:, :], own[:, :], ALU.add).then_inc(s_cw_sb, 1)
            link(tt(mu[:, :], d_row[:, :], d_row[:, :], ALU.mult))
            dve.wait_ge(s_var, 1)
            tt(m["var_row"][:, :], ps_var[0:3, 0:D], mu[:, :], ALU.subtract)

        @block.tensor
        def _(pe):
            mm = nc.tensor.matmul
            pe.wait_ge(s_mean, 1)
            nc.tensor.transpose(ps_rows[0:1, 0:D], mean_x[:, :], m["ident"][:, :])
            mm(ps_rows[0:3, D:2 * D], mean_x[:, :].to_broadcast([D, 3]), m["wloop_sb"][:, :], start=True, stop=True)
            mm(ps_rows[0:3, 2 * D:3 * D], mean_d[:, :].to_broadcast([D, 3]), m["ident"][:, :], start=True, stop=True)\
                .then_inc(s_row, 1)
            pe.wait_ge(s_row_sb, 1)
            mm(ps_outer[:, 0, 0:D], x_row[:, :], x_row[:, :], start=True, stop=True)
            mm(ps_outer[:, 1, 0:D], x_row[:, :], d_row[0:1, :], start=True, stop=True).then_inc(s_outer, 1)
            pe.wait_ge(s_cov, 1)
            mm(ps_cw[:, 0:D], cov[:, :], m["wloop_sb"][:, :], start=True, stop=True).then_inc(s_cw, 1)
            pe.wait_ge(s_cw_sb, 1)
            mm(ps_var[0:3, 0:D], m["ones_col"][:, :].to_broadcast([P, 3]), cw[:, :], start=True, stop=True)\
                .then_inc(s_var, 1)


def output(nc, m):
    rows, ident = m["rows"], m["ident"]
    with ExitStack() as c:
        new_sem = c.enter_context(phase_sems(nc))

        def sb(name, shape, dt=F32):
            return c.enter_context(nc.sbuf_tensor(f"{name}_o", shape, dt))

        def sems(name, n=2):
            return [new_sem(f"{name}_o{k}") for k in range(n)]

        def ps(name, shape):
            return c.enter_context(nc.psum_tensor(f"{name}_o", shape, F32))

        def space(n, slots):
            return rows[:, 4 * CH * n:(4 * n + slots) * CH, :].rearrange("p (s j) d -> p s j d", s=slots)

        x1, delta, z, y = space(0, 4), space(1, 4), space(2, 4), space(3, 4)
        a_row = sb("a_row", [3, D])
        base_row = sb("base_row", [3, D])
        base_parts = sb("base_parts", [3, D], BF16)
        r = sb("r", [3, 4, D])
        a_all = sb("a_all", [P, D])
        w_scaled = sb("w_scaled", [D, D])
        x1_t = sb("x1_t", [P, 2, CH * P])
        st = sb("st", [P, 4, CH, 6])
        mv = sb("mv", [P, 4, 3, CH])
        sd = sb("sd", [P, 4, CH])
        rstd = sb("rstd", [P, 4, CH])
        shift = sb("shift", [P, 4, CH])
        ps_t = ps("ps_t", [P, 2, G * P])
        ps_u = ps("ps_u", [P, 2, CH, D])
        ps_a = ps("ps_a", [P, 512])
        turned, turned_sb, lin = (sems(n) for n in ("turned", "turned_sb", "lin"))
        x_in, x_used, d_in, d_scaled, zed, sd_ready, scale_ready, normed, x_out = (
            sems(n, 4) for n in ("x_in", "x_used", "d_in", "d_scaled", "zed", "sd_ready", "scale_ready",
                                 "normed", "x_out"))
        s_add, s_relu, s_stat, s_rows, s_sqrt, s_sqrt_done, s_a, s_bc, s_ready, s_tail = (
            sems(n, 1)[0] for n in ("add", "relu", "stat", "rows", "sqrt", "sqrt_done", "a", "bc", "ready", "tail"))
        block = c.enter_context(nc.Block())
        STATS = 4

        @block.sync
        def _(sp):
            def load(t):
                s4, u4 = t.slot(4), t.uses(4)
                sp.wait_ge(x_used[s4], u4)
                sp.dma_start(x1[0:t.np, s4, :, :], m["x1_table"][ds(t.g * CHUNK, t.np * CH), :]
                             .rearrange("(p j) d -> p j d", j=CH)).then_inc(x_in[s4], 16)
                if not t.starts:
                    sp.wait_ge(s_add, 2 * (t.g - 3))
                sp.dma_start(delta[0:t.np, s4, :, :], m["delta_table"][ds(t.g * CHUNK, t.np * CH), :]
                             .rearrange("(p j) d -> p j d", j=CH)).then_inc(d_in[s4], 16)
            in_turns(sp, load)

        @block.tensor
        def _(pe):
            mm = nc.tensor.matmul

            def turn_rows(t):
                s, u, s4, u4 = t.slot(), t.uses(), t.slot(4), t.uses(4)
                pe.wait_ge(x_in[s4], 16 * (u4 + 1))
                for h in range(2):
                    pe.wait_ge(turned_sb[h], t.g)
                    for j in range(G):
                        last = nc.tensor.transpose(ps_t[:, h, j * P:(j + 1) * P], x1[:, s4, h * G + j, :], ident[:, :])
                    last.then_inc(turned[h], 1)

            def body(t):
                s, u = t.slot(), t.uses()
                if t.next():
                    turn_rows(t.next())
                if not (t.starts and t.k < 2):
                    pe.wait_ge(s_add, 2 * (t.g - 1))
                for h in range(2):
                    pe.wait_ge(turned_sb[h], t.g + 1)
                    mm(ps_u[:, s, h * G:(h + 1) * G, :], m["ones3"][:, :],
                       base_parts[:, :].unsqueeze(1).to_broadcast([3, G, D]), start=True, stop=False,
                       skip_group_check=True)
                    for j in range(h * G, (h + 1) * G):
                        last = mm(ps_u[:, s, j, :], x1_t[:, s, j * P:(j + 1) * P], w_scaled[:, :], start=False,
                                  stop=True, skip_group_check=True)
                last.then_inc(lin[s], 1)

            pe.wait_ge(s_a, 1)
            mm(ps_a[:, 0:D], m["ones_row"][:, :], a_row[0:1, :], start=True, stop=True).then_inc(s_bc, 1)
            turn_rows(Turn(0, 0))
            pe.wait_ge(s_ready, 1)
            in_turns(pe, body)

        @block.scalar
        def _(act):
            def turned_out(t):
                s, u = t.slot(), t.uses()
                act.wait_ge(lin[s], u)
                for h in range(2):
                    act.wait_ge(turned[h], t.g + 1)
                    nc.scalar.activation(x1_t[:, s, h * G * P:(h + 1) * G * P], ps_t[:, h, :], ACT.Copy)\
                        .then_inc(turned_sb[h], 1)

            def deviation(t):
                s4, u4 = t.slot(4), t.uses(4)
                act.wait_ge(zed[s4], u4 + 1)
                nc.scalar.activation(sd[:, s4, :], mv[:, s4, 1, :], ACT.Sqrt, bias=m["eps_col"][:, :],
                                     scale=1.0 / D).then_inc(sd_ready[s4], 1)

            def normalise(t, j0, j1):
                s4, u4 = t.slot(4), t.uses(4)
                if j0 == 0:
                    act.wait_ge(scale_ready[s4], u4 + 1)
                    act.wait_ge(x_out[s4], 16 * u4)
                for j in range(j0, j1):
                    last = nc.scalar.activation(y[:, s4, j, :], z[:, s4, j, :], ACT.Identity,
                                                bias=shift[:, s4, j:j + 1], scale=rstd[:, s4, j:j + 1])
                if j1 == CH:
                    last.then_inc(normed[s4], 1)
                    act.wait_ge(normed[s4], u4 + 1)
                    act.dma_start(m["out"][ds(t.g * CHUNK, t.np * CH), :].rearrange("(p j) d -> p j d", j=CH),
                                  y[0:t.np, s4, :, :]).then_inc(x_out[s4], 16)

            def step(t, p, pp):
                if t and t.next():
                    turned_out(t.next())
                if pp:
                    normalise(pp, 0, CH // 2)
                if p:
                    deviation(p)
                if pp:
                    normalise(pp, CH // 2, CH)

            act.wait_ge(s_sqrt, 1)
            nc.scalar.activation(r[:, 1, :], r[:, 0, :], ACT.Sqrt).then_inc(s_sqrt_done, 1)
            turned_out(Turn(0, 0))
            in_turns(act, lambda t: step(t, t.prev(), t.prev() and t.prev().prev()), peeled=2)
            step(None, LAST, LAST.prev())
            normalise(LAST, 0, CH)
            for s in range(4):
                act.wait_ge(x_out[s], 16 * len(range(s, NG, 4)))

        @block.vector
        def _(dve):
            link = Chain(dve, s_rows)
            ts, tt, stt = nc.vector.tensor_scalar, nc.vector.tensor_tensor, nc.vector.scalar_tensor_tensor
            ts(r[:, 0, :], m["var_row"][:, :], EPS, None, ALU.add).then_inc(s_sqrt, 1)
            dve.wait_ge(s_sqrt_done, 1)
            link(nc.vector.reciprocal(r[:, 2, :], r[:, 1, :]))
            tt(a_row[:, :], m["vec_rows"][:, 1, :], r[:, 2, :], ALU.mult).then_inc(s_a, 1)
            dve.wait_ge(s_a, 1)
            link(tt(r[:, 3, :], m["centre_row"][:, :], a_row[:, :], ALU.mult))
            link(tt(base_row[:, :], r[:, 3, :], m["vec_rows"][:, 2, :], ALU.add))
            split3(nc, m, link, base_parts[:, :], base_row[:, :], (m["split_f"], m["split_b"]))
            dve.wait_ge(s_bc, 1)
            link(nc.vector.tensor_copy(a_all[:, :], ps_a[:, 0:D]))
            tt(w_scaled[:, :], m["wloop_sb"][:, :], a_all[:, :], ALU.mult).then_inc(s_ready, 1)

            def step(t, p):
                halves = [slice(h * G, (h + 1) * G) for h in range(2)]
                if p:
                    q4 = p.slot(4)
                    stat = LoopChain(dve, s_stat, STATS, p.g)
                    stat.n = 1
                    stat.wait(1)
                    parts, finish = row_stats_steps(nc, st[:, q4, :, :], mv[:, q4, :, :], P, z[:, q4, :, :], CH)
                if t:
                    s, u, s4, u4 = t.slot(), t.uses(), t.slot(4), t.uses(4)
                    add = LoopChain(dve, s_add, 2, t.g)
                    dve.wait_ge(lin[s], u + 1)
                    dve.wait_ge(normed[s4], u4)
                    dve.wait_ge(d_scaled[s4], u4 + 1)
                    add(tt(z[:, s4, halves[0], :], ps_u[:, s, halves[0], :], delta[:, s4, halves[0], :], ALU.add),
                        wait=False)
                if p:
                    stat(parts[1](), wait=not t)
                if t:
                    add(tt(z[:, s4, halves[1], :], ps_u[:, s, halves[1], :], delta[:, s4, halves[1], :], ALU.add),
                        wait=False)
                if p:
                    stat.wait(2)
                    stat(parts[2](), wait=not t)
                if t:
                    add.wait(1)
                    stt(z[:, s4, halves[0], :], z[:, s4, halves[0], :], 0.0, x1[:, s4, halves[0], :], ALU.max, ALU.add)\
                        .then_inc(s_relu, 1)
                if p:
                    stat.wait(3)
                    finish().then_inc(zed[q4], 1)
                if t:
                    add.wait(2)
                    stt(z[:, s4, halves[1], :], z[:, s4, halves[1], :], 0.0, x1[:, s4, halves[1], :], ALU.max, ALU.add)\
                        .then_inc(x_used[s4], 1)
                    first, _ = row_stats_steps(nc, st[:, s4, :, :], mv[:, s4, :, :], P, z[:, s4, :, :], CH)
                    dve.wait_ge(s_relu, t.g + 1)
                    first[0](0, G)
                if p:
                    dve.wait_ge(sd_ready[q4], p.uses(4) + 1)
                    stat(nc.vector.reciprocal(rstd[:, q4, :], sd[:, q4, :]), wait=not t)
                if t:
                    dve.wait_ge(x_used[s4], u4 + 1)
                    own = LoopChain(dve, s_stat, STATS, t.g)
                    own(first[0](G, CH), wait=False)
                if p:
                    stat.wait(4)
                    stt(shift[:, q4, :], mv[:, q4, 2, :], -0.5, rstd[:, q4, :], ALU.mult, ALU.mult)\
                        .then_inc(scale_ready[q4], 1)
            in_turns(dve, lambda t: step(t, t.prev()), peeled=2)
            step(None, LAST)

        @block.gpsimd
        def _(pool):
            def scale(t):
                s4, u4 = t.slot(4), t.uses(4)
                pool.wait_ge(d_in[s4], 16 * (u4 + 1))
                nc.gpsimd.tensor_tensor(delta[:, s4, :, :], delta[:, s4, :, :],
                                        a_all[:, :].unsqueeze(1).to_broadcast([P, CH, D]), ALU.mult)\
                    .then_inc(d_scaled[s4], 1)
            pool.wait_ge(s_ready, 1)
            in_turns(pool, scale)


def kernel(**inputs):
    import numpy as np
    import concourse.bacc as bacc
    from concourse.bass_utils import run_bass_kernel_spmd as run

    fill = P * T - EDGES
    a = {n: np.asarray(v) for n, v in inputs.items()}
    pad = lambda v: np.concatenate([v, np.zeros(fill, v.dtype)])
    dst = a["dst"]
    dst = np.concatenate([np.full(1, -1, dst.dtype), dst, np.full(fill, NODES, dst.dtype),
                          np.full(1, NODES + 1, dst.dtype)])
    arrays = {
        "x": a["x"], "src": pad(a["src"]), "dst": dst[1:-1], "near": np.stack([dst[0:P * T:T], dst[T + 1::T]], 1),
        "rel": pad(a["edge_type_32"]), "ew": pad(a["edge_weight"]),
        "wk": a["L0_gnn_Wk"], "wk_t": a["L0_gnn_Wk"].T, "bk": a["L0_gnn_bk"], "wq_t": a["L0_gnn_Wq"].T,
        "bq": a["L0_gnn_bq"], "wv": a["L0_gnn_Wv"], "bv": a["L0_gnn_bv"], "rel_att": a["L0_gnn_rel_att"],
        "rel_msg": a["L0_gnn_rel_msg"], "w_loop": a["L1_gnn_w_loop"], "w_bases": a["L1_gnn_w_bases"],
        "w_coef": a["L1_gnn_w_rel_coef"], "w_coef_t": a["L1_gnn_w_rel_coef"].T, "att_l": a["L1_gnn_att_l_w"],
        "w_bias": a["L1_gnn_w_bias"], "gamma": a["L1_gnn_bn_gamma"], "beta": a["L1_gnn_bn_beta"],
    }
    arrays = {n: np.ascontiguousarray(v) for n, v in arrays.items()}
    nc = bacc.Bacc("TRN2", target_bir_lowering=False, num_devices=1)
    args = {n: nc.dram_tensor(f"in_{n}", v.shape, mybir.dt.from_np(v.dtype), kind="ExternalInput").ap()
            for n, v in arrays.items()}
    out = nc.dram_tensor("out_0", (NODES, D), F32, kind="ExternalOutput").ap()
    program(nc, out=out, **args)
    r = run(nc, [{f"in_{n}": v for n, v in arrays.items()}], core_ids=[0])
    return r.results[0]["out_0"]
```
